# Optimizing a Trainium2 kernel written in Bass

```python
import numpy as np
import jax
import jax.numpy as jnp

def _softmax(x, axis=-1):
    return jax.nn.softmax(x, axis=axis)

def _gelu(x):
    return jax.nn.gelu(x, approximate=True)

def _silu(x):
    return jax.nn.silu(x)

def _sigmoid(x):
    return jax.nn.sigmoid(x)

def _layernorm(x, axis=-1, eps=1e-05):
    m = jnp.mean(x, axis=axis, keepdims=True)
    v = jnp.var(x, axis=axis, keepdims=True)
    return (x - m) / jnp.sqrt(v + eps)

def _scatter_add(tgt, idx, src, axis=0):
    return tgt.at[idx].add(src)

def _segment_sum(src, seg, n):
    return jax.ops.segment_sum(src, seg, n)
kernel_name = 'mk_hybrid_d1_jaxref_r8_cf753c'

def setup_inputs(seed: int=0):
    np.random.seed(seed)
    _w = jnp.asarray

    def _L0_attn_a_setup():
        import jax, jax.numpy as jnp
        import numpy as np
        HEADS = 16
        DIM_HEAD = 64
        SCALE = DIM_HEAD ** (-0.5)
        key = jax.random.key(seed)
        k1, k2, k3 = jax.random.split(key, 3)
        B, N, D = (4, 1024, 128)
        inner = HEADS * DIM_HEAD
        x = jax.random.normal(k1, (B, N, D), dtype=jnp.float32)
        w_qkv = jax.random.normal(k2, (D, 3 * inner), dtype=jnp.float32) * D ** (-0.5)
        w_out = jax.random.normal(k3, (inner, D), dtype=jnp.float32) * inner ** (-0.5)
        b_out = jnp.zeros((D,), dtype=jnp.float32)
        return {'x': x, 'w_qkv': w_qkv, 'w_out': w_out, 'b_out': b_out}
    _L0_attn_a_in = _L0_attn_a_setup()

    def _L0_attn_b_setup():
        import jax, jax.numpy as jnp
        import numpy as np
        import math
        D_MODEL = 128
        NUM_HEADS = 16
        HEAD_DIM = D_MODEL // NUM_HEADS
        ROPE_THETA = 10000.0

        def _rope_tables(seq_len, dim, theta=ROPE_THETA):
            inv = 1.0 / theta ** (jnp.arange(0, dim, 2, dtype=jnp.float32) / dim)
            t = jnp.arange(seq_len, dtype=jnp.float32)
            f = jnp.outer(t, inv)
            cos = jnp.repeat(jnp.cos(f), 2, axis=-1)
            sin = jnp.repeat(jnp.sin(f), 2, axis=-1)
            return (cos, sin)

        def _rotate_half(x):
            x1 = x[..., ::2]
            x2 = x[..., 1::2]
            return jnp.stack((-x2, x1), axis=-1).reshape(x.shape)
        key = jax.random.key(seed)
        ks = jax.random.split(key, 5)
        scale = 1.0 / math.sqrt(D_MODEL)
        return {'x': jax.random.normal(ks[0], (2, 256, D_MODEL), dtype=jnp.float32), 'W_Q': jax.random.normal(ks[1], (D_MODEL, D_MODEL), dtype=jnp.float32) * scale, 'W_K': jax.random.normal(ks[2], (D_MODEL, D_MODEL), dtype=jnp.float32) * scale, 'W_V': jax.random.normal(ks[3], (D_MODEL, D_MODEL), dtype=jnp.float32) * scale, 'W_O': jax.random.normal(ks[4], (D_MODEL, D_MODEL), dtype=jnp.float32) * scale}
    _L0_attn_b_in = _L0_attn_b_setup()

    def _L0_ffn_setup():
        import jax, jax.numpy as jnp
        import numpy as np
        DIM = 128

        def _reference_tuple_inner(x, W_r, W_k, W_v, mu_r, mu_k):
            B, T, C = x.shape
            x_prev = jnp.concatenate([jnp.zeros((B, 1, C), x.dtype), x[:, :-1, :]], axis=1)
            xr = mu_r * x + (1.0 - mu_r) * x_prev
            xk = mu_k * x + (1.0 - mu_k) * x_prev
            r = jax.nn.sigmoid(jnp.einsum('btc,dc->btd', xr, W_r))
            k = jnp.einsum('btc,dc->btd', xk, W_k)
            k_act = jnp.square(jax.nn.relu(k))
            out = r * jnp.einsum('btc,dc->btd', k_act, W_v)
            new_state = x[:, -1, :]
            return (out, new_state)
        key = jax.random.key(seed)
        ks = jax.random.split(key, 6)
        B, T, C = (8, 256, DIM)
        x = jax.random.normal(ks[0], (B, T, C), dtype=jnp.float32)
        s = 1.0 / np.sqrt(C)
        W_r = jax.random.uniform(ks[1], (C, C), jnp.float32, -s, s)
        W_k = jax.random.uniform(ks[2], (C, C), jnp.float32, -s, s)
        W_v = jax.random.uniform(ks[3], (C, C), jnp.float32, -s, s)
        mu_r = jax.random.uniform(ks[4], (C,), jnp.float32)
        mu_k = jax.random.uniform(ks[5], (C,), jnp.float32)
        return {'x': x, 'W_r': W_r, 'W_k': W_k, 'W_v': W_v, 'mu_r': mu_r, 'mu_k': mu_k}
    _L0_ffn_in = _L0_ffn_setup()
    _d = {'L0_attn_a_x': _L0_attn_a_in['x'], 'L0_attn_a_w_qkv': _L0_attn_a_in['w_qkv'], 'L0_attn_a_w_out': _L0_attn_a_in['w_out'], 'L0_attn_a_b_out': _L0_attn_a_in['b_out'], 'L0_attn_b_W_Q': _L0_attn_b_in['W_Q'], 'L0_attn_b_W_K': _L0_attn_b_in['W_K'], 'L0_attn_b_W_V': _L0_attn_b_in['W_V'], 'L0_attn_b_W_O': _L0_attn_b_in['W_O'], 'L0_ffn_W_r': _L0_ffn_in['W_r'], 'L0_ffn_W_k': _L0_ffn_in['W_k'], 'L0_ffn_W_v': _L0_ffn_in['W_v'], 'L0_ffn_mu_r': _L0_ffn_in['mu_r'], 'L0_ffn_mu_k': _L0_ffn_in['mu_k']}
    _x0 = _d['L0_attn_a_x']
    _d['L0_attn_a_x'] = jax.random.normal(jax.random.fold_in(jax.random.key(seed), 1), (16, 512, 128), dtype=_x0.dtype)
    del _x0
    return _d

def reference(L0_attn_a_x, L0_attn_a_w_qkv, L0_attn_a_w_out, L0_attn_a_b_out, L0_attn_b_W_Q, L0_attn_b_W_K, L0_attn_b_W_V, L0_attn_b_W_O, L0_ffn_W_r, L0_ffn_W_k, L0_ffn_W_v, L0_ffn_mu_r, L0_ffn_mu_k):

    def _L0_attn_a_ref(x, w_qkv, w_out, b_out):
        import jax, jax.numpy as jnp
        import numpy as np
        HEADS = 16
        DIM_HEAD = 64
        SCALE = DIM_HEAD ** (-0.5)
        B, N, D = x.shape
        h, d = (HEADS, DIM_HEAD)
        qkv = x @ w_qkv
        q, k, v = jnp.split(qkv, 3, axis=-1)

        def to_heads(t):
            return t.reshape(B, N, h, d).transpose(0, 2, 1, 3).reshape(B * h, N, d)
        q, k, v = map(to_heads, (q, k, v))
        q = jax.nn.softmax(q * SCALE, axis=-1)
        k = jax.nn.softmax(k, axis=-2)
        context = jnp.einsum('bnd,bne->bde', q, k)
        out = jnp.einsum('bde,bnd->bne', context, v)
        out = out.reshape(B, h, N, d).transpose(0, 2, 1, 3).reshape(B, N, h * d)
        return out @ w_out + b_out

    def _L0_attn_b_ref(x, W_Q, W_K, W_V, W_O):
        import jax, jax.numpy as jnp
        import numpy as np
        import math
        D_MODEL = 128
        NUM_HEADS = 16
        HEAD_DIM = D_MODEL // NUM_HEADS
        ROPE_THETA = 10000.0

        def _rope_tables(seq_len, dim, theta=ROPE_THETA):
            inv = 1.0 / theta ** (jnp.arange(0, dim, 2, dtype=jnp.float32) / dim)
            t = jnp.arange(seq_len, dtype=jnp.float32)
            f = jnp.outer(t, inv)
            cos = jnp.repeat(jnp.cos(f), 2, axis=-1)
            sin = jnp.repeat(jnp.sin(f), 2, axis=-1)
            return (cos, sin)

        def _rotate_half(x):
            x1 = x[..., ::2]
            x2 = x[..., 1::2]
            return jnp.stack((-x2, x1), axis=-1).reshape(x.shape)
        B, L, _ = x.shape

        def proj(W):
            return jnp.einsum('bld,ed->ble', x, W).reshape(B, L, NUM_HEADS, HEAD_DIM).transpose(0, 2, 1, 3)
        q, k, v = (proj(W_Q), proj(W_K), proj(W_V))
        cos, sin = _rope_tables(L, HEAD_DIM)
        cos = cos[None, None].astype(x.dtype)
        sin = sin[None, None].astype(x.dtype)
        q = q * cos + _rotate_half(q) * sin
        k = k * cos + _rotate_half(k) * sin
        scores = jnp.einsum('bhqd,bhkd->bhqk', q, k) / math.sqrt(HEAD_DIM)
        attn = jax.nn.softmax(scores, axis=-1)
        ctx = jnp.einsum('bhqk,bhkd->bhqd', attn, v)
        ctx = ctx.transpose(0, 2, 1, 3).reshape(B, L, D_MODEL)
        return jnp.einsum('bld,ed->ble', ctx, W_O)

    def _L0_ffn_ref(x, W_r, W_k, W_v, mu_r, mu_k):
        import jax, jax.numpy as jnp
        import numpy as np
        DIM = 128

        def _reference_tuple_inner(x, W_r, W_k, W_v, mu_r, mu_k):
            B, T, C = x.shape
            x_prev = jnp.concatenate([jnp.zeros((B, 1, C), x.dtype), x[:, :-1, :]], axis=1)
            xr = mu_r * x + (1.0 - mu_r) * x_prev
            xk = mu_k * x + (1.0 - mu_k) * x_prev
            r = jax.nn.sigmoid(jnp.einsum('btc,dc->btd', xr, W_r))
            k = jnp.einsum('btc,dc->btd', xk, W_k)
            k_act = jnp.square(jax.nn.relu(k))
            out = r * jnp.einsum('btc,dc->btd', k_act, W_v)
            new_state = x[:, -1, :]
            return (out, new_state)
        return _reference_tuple_inner(x, W_r, W_k, W_v, mu_r, mu_k)[0]
    x = L0_attn_a_x
    x = x + _L0_attn_a_ref(_layernorm(x, axis=-1), L0_attn_a_w_qkv, L0_attn_a_w_out, L0_attn_a_b_out)
    x = x + _L0_ffn_ref(_layernorm(x, axis=-1), L0_ffn_W_r, L0_ffn_W_k, L0_ffn_W_v, L0_ffn_mu_r, L0_ffn_mu_k)
    x = x + _L0_attn_b_ref(_layernorm(x, axis=-1), L0_attn_b_W_Q, L0_attn_b_W_K, L0_attn_b_W_V, L0_attn_b_W_O)
    x = x + _L0_ffn_ref(_layernorm(x, axis=-1), L0_ffn_W_r, L0_ffn_W_k, L0_ffn_W_v, L0_ffn_mu_r, L0_ffn_mu_k)
    return x

_drawn_inputs = setup_inputs


def setup_inputs(seed=0):
    import zlib

    import numpy as np

    out = dict(_drawn_inputs(seed))
    spreads = {'L0_attn_a_b_out': (0.0, 0.1)}
    factors = {'L0_ffn_mu_r': 3.229}
    for name, (base, spread) in spreads.items():
        noise = np.random.default_rng([zlib.crc32(name.encode()), seed]).standard_normal(out[name].shape)
        drawn = base * np.exp(spread * noise) if base else spread * noise
        out[name] = jnp.asarray(drawn.astype(out[name].dtype))
    for name, factor in factors.items():
        out[name] = (out[name] * factor).astype(out[name].dtype)
    return out
```

```python
from contextlib import ExitStack

import numpy as np

import concourse.bass as bass
from concourse import mybir

F32 = mybir.dt.float32
F32R = mybir.dt.float32r
ALU = mybir.AluOpType
ACT = mybir.ActivationFunctionType
AX_X = mybir.AxisListType.X

P = 128
EPS = 1e-5


class Signal:

    def __init__(self, ctx, nc, name, per):
        self.sem = ctx.enter_context(nc.semaphore(name))
        self.per = per

    def at(self, batch, count=None):
        return batch * self.per + (self.per if count is None else count)


def exists(value):
    return not isinstance(value, int) or value > 0


def over_batches(eng, step, n):
    for b in range(3):
        step(b, b % 2, b == 0, False)
    with eng.Fori(3, n - 2, 2) as i:
        step(i, 1, False, False)
        step(i + 1, 0, False, False)
    step(n - 1, 1, False, True)


def hybrid_block(nc, x, w_qkv, w_out, b_out, W_Q, W_K, W_V, W_O, W_r, W_k, W_v, mu_r, mu_k,
                 rope_cos, rope_sin, out):
    NB, N, D = x.shape
    NC = N // P
    INNER = w_out.shape[0]
    DA = 64
    HA = INNER // DA
    PAIRS = INNER // P
    HB = 16
    DB = D // HB
    NG = HB // 4
    W3 = 3 * D
    assert D == P and NC == 4 and PAIRS == 8 and DB == 8 and NB % 2 == 0 and NB >= 6
    SCALE_A = DA ** -0.5

    x2_dram = nc.dram_tensor("x2_scratch", [NB, P, NC * D], F32, kind="Internal").ap()
    qkv_dram = nc.dram_tensor("qkv_scratch", [NB, P, NC * W3], F32, kind="Internal").ap()

    x_view = x.rearrange("b (c p) d -> b p c d", p=P)
    out_view = out.rearrange("b (c p) d -> b p c d", p=P)

    with ExitStack() as ctx:
        def sb(name, shape, dt=F32):
            return ctx.enter_context(nc.sbuf_tensor(name, shape, dt))

        def sig(name, per=1):
            return Signal(ctx, nc, name, per)

        work = sb("work", [P, 16384])
        work_r = sb("work_r", [P, 4096], F32R)
        taken = [0]

        def carve(cols):
            at = taken[0]
            taken[0] += cols
            assert taken[0] <= 16384
            return work[:, at:at + cols]

        E_all = carve(NC * 2 * INNER)
        E_v = E_all.rearrange("p (c n) -> p c n", c=NC)
        EQ = [E_v[:, c, 0:INNER] for c in range(NC)]
        EK = [E_v[:, c, INNER:2 * INNER] for c in range(NC)]
        wqkv_raw = E_all[:, 0:3 * INNER]
        ctx_bd = carve(INNER).rearrange("p (a n) -> p a n", a=PAIRS)
        T_sb = carve(INNER).rearrange("p (a n) -> p a n", a=PAIRS)
        q_sh = carve(INNER)
        WvT = carve(INNER).rearrange("p (a n) -> p a n", a=PAIRS)
        wout_sb = carve(INNER).rearrange("p (a n) -> p a n", a=PAIRS)
        h1T = [carve(N) for _ in range(2)]
        xa = carve(N).rearrange("p (c d) -> p c d", c=NC)
        h1 = carve(N).rearrange("p (c d) -> p c d", c=NC)
        xr = carve(N).rearrange("p (c d) -> p c d", c=NC)
        wqk_hi, wqk_lo = work_r[:, 0:2 * INNER], work_r[:, 2 * INNER:4 * INNER]
        probs = [work[:, g * 8192:(g + 1) * 8192].rearrange("p (j k n) -> p j k n", j=4, k=NC)
                 for g in range(2)]
        k_pad = [work_r[:, g * 2048:(g + 1) * 2048].rearrange("p (j n) -> p j n", j=4)
                 for g in range(2)]

        ident = sb("ident", [P, P])
        raw7 = sb("raw7", [P, 7, D])
        W7T = sb("W7T", [P, 7, D])
        WrT, WkT, WvfT, WOT = (W7T[:, n, :] for n in (0, 1, 2, 6))
        mu = sb("mu", [P, 4])
        b_row = sb("b_row", [1, D])
        ones_row = sb("ones_row", [1, P])
        b_all = sb("b_all", [P, D])
        one = sb("one", [P, 1])
        half_neg = sb("half_neg", [P, NC])
        cos_t = sb("cos_t", [P, NC, 2 * D])
        sin_t = sb("sin_t", [P, NC, 2 * D])

        h1h, h1l = sb("h1h", [P, N], F32R), sb("h1l", [P, N], F32R)
        h3h, h3l = sb("h3h", [P, N], F32R), sb("h3l", [P, N], F32R)
        w3h, w3l = sb("w3h", [P, W3], F32R), sb("w3l", [P, W3], F32R)
        ones8f = sb("ones8f", [8, P])
        ones8 = sb("ones8", [8, P], F32R)
        negmask = sb("negmask", [8, PAIRS, P])
        k_neg = sb("k_neg", [8, PAIRS, P], F32R)
        k_max = sb("k_max", [P, PAIRS])
        M_sb = sb("M_sb", [P, D])
        q_max = sb("q_max", [P, HA])
        q_sum, q_rcp = sb("q_sum", [P, HA]), sb("q_rcp", [P, HA])
        z_sum, z_rcp = sb("z_sum", [P, PAIRS]), sb("z_rcp", [P, PAIRS])
        stats = [(sb(f"st{n}", [P, NC, 6]), sb(f"mom{n}", [P, 6, NC]), sb(f"ve{n}", [P, NC]),
                  sb(f"rs{n}", [P, NC])) for n in range(4)]
        x1 = sb("x1", [P, NC, D])
        x2 = sb("x2", [P, NC, D])
        hn = sb("hn", [P, NC, D])
        h3 = sb("h3", [P, NC, D])
        mixed = [sb("mixed_r", [P, N]), sb("mixed_k", [P, N])]
        k_relu, k_act = sb("k_relu", [P, N]), sb("k_act", [P, N])
        gate = sb("gate", [P, NC, D])
        gated = sb("gated", [P, NC, D])
        qkv_sb = sb("qkv_sb", [P, NC, W3])

        qk_rot = sb("qk_rot", [P, NC, 2 * D])
        rot = sb("rot", [P, NC, 2 * D])
        v32 = [sb(f"v32_{p}", [P, NC, HB, 32]) for p in range(2)]
        parts = [sb(f"parts{g}", [P, 2, NC, P], F32R) for g in range(2)]
        q_st = [sb(f"q_st{g}", [P, N], F32R) for g in range(2)]
        k_st = [sb(f"k_st{g}", [P, N], F32R) for g in range(2)]
        row_max = sb("row_max", [P, NC, 4])
        neg_c = sb("neg_c", [4, N], F32R)
        sel4f = sb("sel4f", [4, 4, P])
        sel4 = sb("sel4", [4, 4, P], F32R)
        U = [sb(f"U{g}", [P, N]) for g in range(2)]
        den_rcp = sb("den_rcp", [P, NC, 4])
        c_tok = sb("c_tok", [P, NC, D])
        cT = sb("cT", [P, N])
        PS = ctx.enter_context(nc.psum_tensor("PS", [P, 8, 512], F32))

        def as_chunks(ap):
            return ap.rearrange("p (c d) -> p c d", c=NC)

        w_in, c_in = sig("w_in", 16 * 10), sig("c_in", 16 * 6)
        id0, id_ok, const_ok = sig("id0"), sig("id_ok"), sig("const_ok")
        sel_ok = sig("sel_ok")
        wsplit, wT, wT_sb, w3s, b_ps, b_ok = (sig(s, n) for s, n in (
            ("wsplit", 3), ("wT", 5), ("wT_sb", 5), ("w3s", 2), ("b_ps", 1), ("b_ok", 3)))

        xa_in, xr_in, x2_st, qkv_st = (sig(s, 16) for s in ("xa_in", "xr_in", "x2_st", "qkv_st"))
        ln = [sig(f"ln{n}", 2 * NC + 7) for n in range(4)]
        rstd = [sig(f"rstd{n}") for n in range(4)]
        h1_T, h1_sb, h1_sp = sig("h1_T"), sig("h1_sb"), sig("h1_sp", 2)
        kx_mm, kx_max, kx_T, kx_ok = (sig("kx_mm", PAIRS), sig("kx_max", PAIRS), sig("kx_T"),
                                      sig("kx_ok"))
        q_mm, k_mm, q_mx, q_exp, k_exp = (sig("q_mm", NC), sig("k_mm", NC), sig("q_mx", 2 * NC),
                                          sig("q_exp", NC), sig("k_exp", NC))
        q_rc, q_hat, c_mm, c_ev = sig("q_rc", 2 * NC), sig("q_hat", NC), sig("c_mm", NC), sig("c_ev", 5)
        t_mm, t_ev, m_mm, m_ev, y_mm, xb_ok, x1_ok = (sig(s) for s in (
            "t_mm", "t_ev", "m_mm", "m_ev", "y_mm", "xb_ok", "x1_ok"))
        ffn = []
        for n in range(2):
            ffn.append({s: sig(f"f{n}_{s}", c) for s, c in (
                ("hT", 1), ("mu", 2), ("mix", 4), ("k", 1), ("r", 1), ("relu", 1), ("act", 1),
                ("gate", 1), ("v", 1), ("x", 2))})
        h3_T, h3_sp, p_mm, p_ev = sig("h3_T"), sig("h3_sp", 2), sig("p_mm", NC), sig("p_ev", NC)
        qkv_in, x2_in, out_st = sig("qkv_in", 16), sig("x2_in", 16), sig("out_st", 16)
        k_padded = [sig(f"k_padded{g}", 16 * 4 * NG // 2) for g in range(2)]
        zeroed = sig("zeroed", 3)
        roped, v_ok, part = sig("roped", 4), sig("v_ok"), sig("part", 8 * NG)
        kT_ps, qT_ps, kT_sb, qT_sb = (sig(s, NG) for s in ("kT_ps", "qT_ps", "kT_sb", "qT_sb"))
        mx_mm, mx_ok, mx_T, mx_neg = (sig("mx_mm", 8 * NG), sig("mx_ok", 8 * NG), sig("mx_T", NG),
                                      sig("mx_neg", NG))
        s_mm, s_exp, pv, pv_sb = sig("s_mm", 32), sig("s_exp", 32), sig("pv", 16), sig("pv_sb", NG)
        u_T, u_norm = sig("u_T", NG), sig("u_norm", 2 * NG)
        ct_ps, ct_sb, o_mm, x3_ok = sig("ct_ps"), sig("ct_sb"), sig("o_mm"), sig("x3_ok")

        block = ctx.enter_context(nc.Block())

        @block.sync
        def _(sp):
            sp.dma_start(wqkv_raw, w_qkv).then_inc(w_in.sem, 16)
            for n, w in enumerate((W_r, W_k, W_v, W_Q, W_K, W_V, W_O)):
                sp.dma_start(raw7[:, n, :], w).then_inc(w_in.sem, 16)
            sp.dma_start(wout_sb, w_out.rearrange("(a p) d -> p a d", p=P)).then_inc(w_in.sem, 16)
            sp.dma_start(b_row[:, :], b_out.rearrange("(a d) -> a d", a=1)).then_inc(w_in.sem, 16)
            sp.dma_start(xa, x_view[0]).then_inc(xa_in.sem, 16)
            sp.dma_start(mu[:, 0:1], mu_r.rearrange("(d a) -> d a", a=1)).then_inc(c_in.sem, 16)
            sp.dma_start(mu[:, 1:2], mu_k.rearrange("(d a) -> d a", a=1)).then_inc(c_in.sem, 16)
            sp.dma_start(cos_t[:, :, :], rope_cos).then_inc(c_in.sem, 16)
            sp.dma_start(sin_t[:, :, :], rope_sin).then_inc(c_in.sem, 16)

            def side(j):
                if exists(x1_ok.at(j - 1)):
                    sp.wait_ge(x1_ok.sem, x1_ok.at(j - 1))
                sp.dma_start(xr, x_view[j]).then_inc(xr_in.sem, 16)

            def stores(j):
                sp.wait_ge(ffn[0]["x"].sem, ffn[0]["x"].at(j))
                sp.dma_start(x2_dram[j], x2[:, :, :].rearrange("p c d -> p (c d)")).then_inc(x2_st.sem, 16)
                sp.wait_ge(p_ev.sem, p_ev.at(j))
                sp.dma_start(qkv_dram[j], qkv_sb[:, :, :].rearrange("p c d -> p (c d)")).then_inc(qkv_st.sem, 16)

            def first_half(i, p, first, last):
                if not first:
                    side(i - 1)
                if not last:
                    sp.wait_ge(ln[0].sem, ln[0].at(i))
                    sp.dma_start(xa, x_view[i + 1]).then_inc(xa_in.sem, 16)
                if not first:
                    stores(i - 1)

            over_batches(sp, first_half, NB)
            side(NB - 1)
            stores(NB - 1)

            sp.wait_ge(qkv_st.sem, qkv_st.at(NB - 1))
            sp.wait_ge(x2_st.sem, x2_st.at(NB - 1))
            sp.dma_start(qkv_sb[:, :, :].rearrange("p c d -> p (c d)"), qkv_dram[0]).then_inc(qkv_in.sem, 16)

            def pad(i, g):
                sp.wait_ge(kT_sb.sem, kT_sb.at(i, g + 1))
                for j in range(4):
                    sp.dma_start(k_pad[g % 2][32 * j:32 * j + 32, j, :].bitcast(F32),
                                 k_st[g % 2][32 * j:32 * j + 32, :].bitcast(F32))\
                      .then_inc(k_padded[g % 2].sem, 16)

            sp.wait_ge(zeroed.sem, zeroed.at(0))
            pad(0, 0)

            def second_half(i, p, first, last):
                if not first:
                    if exists(x3_ok.at(i - 2)):
                        sp.wait_ge(x3_ok.sem, x3_ok.at(i - 2))
                    sp.dma_start(x2[:, :, :].rearrange("p c d -> p (c d)"), x2_dram[i - 1]).then_inc(x2_in.sem, 16)
                if not last:
                    sp.wait_ge(roped.sem, roped.at(i))
                    sp.dma_start(qkv_sb[:, :, :].rearrange("p c d -> p (c d)"), qkv_dram[i + 1])\
                      .then_inc(qkv_in.sem, 16)
                for g in range(1, NG):
                    pad(i, g)
                if not last:
                    pad(i + 1, 0)
                if not first:
                    sp.wait_ge(ffn[1]["x"].sem, ffn[1]["x"].at(i - 1))
                    sp.dma_start(out_view[i - 1], gated[:, :, :]).then_inc(out_st.sem, 16)

            over_batches(sp, second_half, NB)
            sp.wait_ge(x3_ok.sem, x3_ok.at(NB - 2))
            sp.dma_start(x2[:, :, :].rearrange("p c d -> p (c d)"), x2_dram[NB - 1]).then_inc(x2_in.sem, 16)
            sp.wait_ge(ffn[1]["x"].sem, ffn[1]["x"].at(NB - 1))
            sp.dma_start(out_view[NB - 1], gated[:, :, :]).then_inc(out_st.sem, 16)
            sp.wait_ge(out_st.sem, out_st.at(NB - 1))

        @block.gpsimd
        def _(pool):
            pool.memset(ident[:, :], 0.0).then_inc(id0.sem, 1)
            pool.memset(negmask[:, :, :], 0.0).then_inc(const_ok.sem, 1)
            pool.memset(ones8f[:, :], 1.0).then_inc(const_ok.sem, 1)
            pool.memset(sel4f[:, :, :], 0.0).then_inc(const_ok.sem, 1)
            pool.memset(ones_row[:, :], 1.0).then_inc(const_ok.sem, 1)
            pool.memset(half_neg[:, :], -0.5).then_inc(const_ok.sem, 1)
            pool.memset(ctx_bd, 0.0).then_inc(const_ok.sem, 1)
            for t in range(2):
                pool.memset(v32[t][:, :, :, :], 0.0).then_inc(const_ok.sem, 1)
            pool.memset(one[:, :], 1.0).then_inc(const_ok.sem, 1)
            pool.wait_ge(id0.sem, 1)
            pool.affine_select(out=ident[:, :], in_=ident[:, :], compare_op=ALU.not_equal, fill=1.0, base=0,
                               pattern=[[-1, P]], channel_multiplier=1).then_inc(id_ok.sem, 1)
            pool.wait_ge(const_ok.sem, 9)
            pool.affine_select(out=negmask[:, :, :], in_=negmask[:, :, :], compare_op=ALU.not_equal, fill=-1.0,
                               base=0, pattern=[[-1, PAIRS], [0, P]], channel_multiplier=1).then_inc(const_ok.sem, 1)
            pool.affine_select(out=sel4f[:, :, :], in_=sel4f[:, :, :], compare_op=ALU.not_equal, fill=1.0,
                               base=0, pattern=[[-1, 4], [0, P]], channel_multiplier=1).then_inc(const_ok.sem, 1)
            for t in range(2):
                pool.memset(v32[t][:, :, :, DB:DB + 1], 1.0).then_inc(const_ok.sem, 1)

            def rsqrt_var(n, j):
                _, _, ve, rs = stats[n]
                pool.wait_ge(ln[n].sem, ln[n].at(j, NC + 7))
                pool.tensor_tensor(rs[:, :], ve[:, :], half_neg[:, :], ALU.pow).then_inc(rstd[n].sem, 1)

            def split_h1(j, p):
                pool.wait_ge(h1_sb.sem, h1_sb.at(j))
                pool.tensor_tensor(h1h[:, :], h1T[p], one[:, 0:1].to_broadcast([P, N]), ALU.mult).then_inc(h1_sp.sem, 1)
                pool.wait_ge(h1_sp.sem, h1_sp.at(j, 1))
                pool.tensor_tensor(h1l[:, :], h1T[p], h1h[:, :].bitcast(F32), ALU.subtract).then_inc(h1_sp.sem, 1)

            def q_hats(i, c):
                pool.wait_ge(q_rc.sem, q_rc.at(i, 2 * c + 2))
                q3 = EQ[c].rearrange("p (h d) -> p h d", h=HA)
                pool.tensor_tensor(q3, q3, q_rcp[:, :].unsqueeze(2).to_broadcast([P, HA, DA]), ALU.mult)\
                    .then_inc(q_hat.sem, 1)

            def add_bias(j):
                pool.wait_ge(xr_in.sem, xr_in.at(j))
                pool.tensor_tensor(xr, xr, b_all[:, :].unsqueeze(1).to_broadcast([P, NC, D]), ALU.add)\
                    .then_inc(xb_ok.sem, 1)

            pool.wait_ge(b_ok.sem, 3)
            rsqrt_var(0, 0)
            split_h1(0, 0)

            def first_half(i, p, first, last):
                if not first:
                    add_bias(i - 1)
                q_hats(i, 0)
                if not first:
                    rsqrt_var(1, i - 1)
                q_hats(i, 1)
                q_hats(i, 2)
                if not last:
                    rsqrt_var(0, i + 1)
                q_hats(i, 3)
                if not first:
                    rsqrt_var(2, i - 1)
                if not last:
                    split_h1(i + 1, 1 - p)

            over_batches(pool, first_half, NB)
            add_bias(NB - 1)
            rsqrt_var(1, NB - 1)
            rsqrt_var(2, NB - 1)

            pool.wait_ge(qkv_st.sem, qkv_st.at(NB - 1))
            pool.wait_ge(x2_st.sem, x2_st.at(NB - 1))
            for g in range(2):
                pool.memset(k_pad[g].bitcast(F32), 0.0).then_inc(zeroed.sem, 1)
            pool.tensor_copy(sel4[:, :, :], sel4f[:, :, :]).then_inc(zeroed.sem, 1)

            qk = qkv_sb[:, :, 0:2 * D]

            def rope(i, p):
                if exists(pv.at(i - 2)):
                    pool.wait_ge(pv.sem, pv.at(i - 2))
                if exists(part.at(i - 1)):
                    pool.wait_ge(part.sem, part.at(i - 1))
                pool.wait_ge(qkv_in.sem, qkv_in.at(i))
                pool.tensor_tensor(qk_rot[:, :, :], qk, cos_t[:, :, :], ALU.mult).then_inc(roped.sem, 1)
                pool.tensor_tensor(rot[:, :, 0::2], qk[:, :, 1::2], sin_t[:, :, 0::2], ALU.mult).then_inc(roped.sem, 1)
                pool.tensor_tensor(rot[:, :, 1::2], qk[:, :, 0::2], sin_t[:, :, 1::2], ALU.mult).then_inc(roped.sem, 1)
                pool.tensor_copy(v32[p][:, :, :, 0:DB],
                                 qkv_sb[:, :, 2 * D:W3].rearrange("p c (h d) -> p c h d", h=HB)).then_inc(v_ok.sem, 1)
                pool.wait_ge(v_ok.sem, v_ok.at(i))
                pool.wait_ge(roped.sem, roped.at(i, 3))
                pool.tensor_tensor(qk_rot[:, :, :], qk_rot[:, :, :], rot[:, :, :], ALU.add).then_inc(roped.sem, 1)

            def split_parts(i, g):
                pool.wait_ge(roped.sem, roped.at(i))
                if exists(qT_ps.at(i, g - 1)):
                    pool.wait_ge(qT_ps.sem, qT_ps.at(i, g - 1))
                if exists(kT_ps.at(i, g - 1)):
                    pool.wait_ge(kT_ps.sem, kT_ps.at(i, g - 1))
                src = [qk_rot[:, :, t * D + 32 * g:t * D + 32 * g + 32].rearrange("p c (j d) -> p c j d", j=4)
                       for t in range(2)]
                dst = [parts[g % 2][:, t, :, :].rearrange("p c (j r d) -> p c j r d", j=4, r=4) for t in range(2)]
                for t, his in ((0, (0, 1)), (1, (0, 2))):
                    for r in his:
                        pool.tensor_tensor(dst[t][:, :, :, r, :], src[t],
                                           one[:, 0:1].unsqueeze(2).unsqueeze(3).to_broadcast([P, NC, 4, DB]),
                                           ALU.mult).then_inc(part.sem, 1)
                pool.wait_ge(part.sem, part.at(i, 8 * g + 4))
                for t, los in ((0, (2, 3)), (1, (1, 3))):
                    for r in los:
                        pool.tensor_tensor(dst[t][:, :, :, r, :], src[t], dst[t][:, :, :, 0, :].bitcast(F32),
                                           ALU.subtract).then_inc(part.sem, 1)

            rope(0, 0)
            split_parts(0, 0)

            def second_half(i, p, first, last):
                for g in range(1, NG):
                    split_parts(i, g)
                    if g == 2 and not first:
                        rsqrt_var(3, i - 1)
                if not last:
                    rope(i + 1, 1 - p)
                    split_parts(i + 1, 0)

            over_batches(pool, second_half, NB)
            rsqrt_var(3, NB - 1)

        @block.scalar
        def _(act):
            def h1_copy(j, p):
                act.wait_ge(h1_T.sem, h1_T.at(j))
                act.activation(h1T[p], PS[:, 7, :], ACT.Copy).then_inc(h1_sb.sem, 1)

            def exps(i, c):
                if exists(c_mm.at(i - 1, c + 1)):
                    act.wait_ge(c_mm.sem, c_mm.at(i - 1, c + 1))
                act.wait_ge(q_mx.sem, q_mx.at(i, 2 * c + 2))
                act.activation(EQ[c], q_sh, ACT.Exp).then_inc(q_exp.sem, 1)
                act.wait_ge(k_mm.sem, k_mm.at(i, c + 1))
                act.activation(EK[c], PS[:, 2:4, :].rearrange("p a n -> p (a n)"), ACT.Exp).then_inc(k_exp.sem, 1)

            def relu(f, j, bank):
                act.wait_ge(f["k"].sem, f["k"].at(j))
                act.activation(k_relu[:, :], PS[:, bank, :], ACT.Relu).then_inc(f["relu"].sem, 1)

            def gates(f, j, bank):
                act.wait_ge(f["r"].sem, f["r"].at(j))
                act.activation(gate[:, :, :].rearrange("p c d -> p (c d)"), PS[:, bank, :], ACT.Tanh, scale=0.5)\
                   .then_inc(f["gate"].sem, 1)

            def scale_mu(f, j, bank):
                act.wait_ge(f["hT"].sem, f["hT"].at(j))
                if exists(f["r"].at(j - 1)):
                    act.wait_ge(f["r"].sem, f["r"].at(j - 1))
                for n in range(2):
                    act.activation(mixed[n][:, :], PS[:, bank, :], ACT.Copy, scale=mu[:, n:n + 1])\
                       .then_inc(f["mu"].sem, 1)

            def t_copy(j):
                act.wait_ge(t_mm.sem, t_mm.at(j))
                act.activation(T_sb.rearrange("p a n -> p (a n)"), PS[:, 5:7, :].rearrange("p a n -> p (a n)"),
                               ACT.Copy).then_inc(t_ev.sem, 1)

            def p_copy(j):
                if exists(qkv_st.at(j - 1)):
                    act.wait_ge(qkv_st.sem, qkv_st.at(j - 1))
                for c in range(NC):
                    act.wait_ge(p_mm.sem, p_mm.at(j, c + 1))
                    act.activation(qkv_sb[:, c, :], PS[:, (4, 7)[c % 2], 0:W3], ACT.Copy).then_inc(p_ev.sem, 1)

            act.wait_ge(b_ok.sem, 3)
            h1_copy(0, 0)

            def first_half(i, p, first, last):
                exps(i, 0)
                if not first:
                    t_copy(i - 1)
                exps(i, 1)
                exps(i, 2)
                if not first:
                    scale_mu(ffn[0], i - 1, 7)
                exps(i, 3)
                if not first:
                    relu(ffn[0], i - 1, 4)
                    gates(ffn[0], i - 1, 7)
                if not last:
                    h1_copy(i + 1, 1 - p)
                if not first:
                    p_copy(i - 1)

            over_batches(act, first_half, NB)
            t_copy(NB - 1)
            scale_mu(ffn[0], NB - 1, 7)
            relu(ffn[0], NB - 1, 4)
            gates(ffn[0], NB - 1, 7)
            p_copy(NB - 1)

            act.wait_ge(qkv_st.sem, qkv_st.at(NB - 1))
            act.wait_ge(x2_st.sem, x2_st.at(NB - 1))

            def second_half(i, p, first, last, main=True):
                for s in range(HB):
                    if main:
                        g, j = s // 4, s % 4
                        for hf in range(2):
                            if j == 0 and hf == 0:
                                if exists(pv.at(i, 4 * (g - 1))):
                                    act.wait_ge(pv.sem, pv.at(i, 4 * (g - 1)))
                            act.wait_ge(s_mm.sem, s_mm.at(i, 2 * s + hf + 1))
                            act.activation(probs[g % 2][:, j, 2 * hf:2 * hf + 2, :], PS[:, 2 * hf:2 * hf + 2, :],
                                           ACT.Exp).then_inc(s_exp.sem, 1)
                    if s == 12 and not first:
                        relu(ffn[1], i - 1, 6)
                        gates(ffn[1], i - 1, 7)

            over_batches(act, second_half, NB)
            second_half(NB, 0, False, True, main=False)

        @block.vector
        def _(dve):
            raw_q, raw_k = wqkv_raw[:, 0:INNER], wqkv_raw[:, INNER:2 * INNER]
            dve.wait_ge(w_in.sem, 160)
            dve.tensor_scalar(raw_q, raw_q, SCALE_A, None, ALU.mult).then_inc(wsplit.sem, 1)
            dve.wait_ge(wsplit.sem, 1)
            dve.tensor_copy(wqk_hi, wqkv_raw[:, 0:2 * INNER]).then_inc(wsplit.sem, 1)
            dve.wait_ge(wsplit.sem, 2)
            dve.tensor_tensor(wqk_lo, wqkv_raw[:, 0:2 * INNER], wqk_hi.bitcast(F32), ALU.subtract).then_inc(wsplit.sem, 1)
            dve.wait_ge(const_ok.sem, 13)
            dve.tensor_copy(ones8[:, :], ones8f[:, :]).then_inc(b_ok.sem, 1)
            dve.wait_ge(wT.sem, 4)
            for n in range(2):
                dve.tensor_copy(WvT[:, 4 * n:4 * n + 4, :], PS[:, n, :].rearrange("p (a n) -> p a n", a=4))\
                   .then_inc(wT_sb.sem, 1)
            dve.tensor_copy(W7T[:, 0:4, :], PS[:, 2, :].rearrange("p (a n) -> p a n", a=4)).then_inc(wT_sb.sem, 1)
            dve.tensor_copy(W7T[:, 4:7, :], PS[:, 3, 0:3 * D].rearrange("p (a n) -> p a n", a=3)).then_inc(wT_sb.sem, 1)
            dve.wait_ge(wT.sem, 5)
            dve.tensor_copy(b_all[:, :], PS[:, 4, 0:D]).then_inc(b_ok.sem, 1)
            dve.wait_ge(wT_sb.sem, 4)
            w3 = W7T[:, 3:6, :].rearrange("p a n -> p (a n)")
            dve.tensor_copy(w3h[:, :], w3).then_inc(w3s.sem, 1)
            dve.wait_ge(w3s.sem, 1)
            dve.tensor_tensor(w3l[:, :], w3, w3h[:, :].bitcast(F32), ALU.subtract).then_inc(w3s.sem, 1)
            dve.wait_ge(c_in.sem, 64)
            dve.tensor_scalar(mu[:, 2:4], mu[:, 0:2], -1.0, 1.0, ALU.mult, ALU.add).then_inc(b_ok.sem, 1)

            def ln_stats(n, j, src):
                st, mom, ve, _ = stats[n]
                mean, d, both, m2, d2, m2e = (mom[:, t, :] for t in range(6))
                for c in range(NC):
                    dve.bn_stats(st[:, c, :], src[:, c, :]).then_inc(ln[n].sem, 1)
                dve.wait_ge(ln[n].sem, ln[n].at(j, NC))
                dve.tensor_tensor(both, st[:, :, 1], st[:, :, 4], ALU.add).then_inc(ln[n].sem, 1)
                dve.tensor_tensor(d, st[:, :, 1], st[:, :, 4], ALU.subtract).then_inc(ln[n].sem, 1)
                dve.tensor_tensor(m2, st[:, :, 2], st[:, :, 5], ALU.add).then_inc(ln[n].sem, 1)
                dve.wait_ge(ln[n].sem, ln[n].at(j, NC + 3))
                dve.tensor_scalar(mean, both, 0.5, None, ALU.mult).then_inc(ln[n].sem, 1)
                dve.scalar_tensor_tensor(d2, d, 0.25, d, ALU.mult, ALU.mult).then_inc(ln[n].sem, 1)
                dve.tensor_scalar(m2e, m2, 1.0 / D, EPS, ALU.mult, ALU.add).then_inc(ln[n].sem, 1)
                dve.wait_ge(ln[n].sem, ln[n].at(j, NC + 6))
                dve.tensor_tensor(ve[:, :], d2, m2e, ALU.add).then_inc(ln[n].sem, 1)

            def ln_norm(n, j, src, dst):
                _, mom, _, rs = stats[n]
                dve.wait_ge(ln[n].sem, ln[n].at(j, NC + 4))
                dve.wait_ge(rstd[n].sem, rstd[n].at(j))
                for c in range(NC):
                    dve.tensor_scalar(dst[:, c, :], src[:, c, :], mom[:, 0, c:c + 1], rs[:, c:c + 1],
                                      ALU.subtract, ALU.mult).then_inc(ln[n].sem, 1)

            def ln1(j):
                dve.wait_ge(xa_in.sem, xa_in.at(j))
                ln_stats(0, j, xa)
                if exists(h1_T.at(j - 1)):
                    dve.wait_ge(h1_T.sem, h1_T.at(j - 1))
                ln_norm(0, j, xa, h1)

            def k_maxima(j):
                for a in range(PAIRS):
                    dve.wait_ge(kx_mm.sem, kx_mm.at(j, a + 1))
                    dve.reduce_max(k_max[:, a:a + 1], PS[:, (4, 7)[a % 2], :], AX_X).then_inc(kx_max.sem, 1)

            def k_shift(j):
                dve.wait_ge(kx_T.sem, kx_T.at(j))
                dve.tensor_tensor(k_neg[:, :, :], PS[0:8, 4, 0:P].unsqueeze(1).to_broadcast([8, PAIRS, P]),
                                  negmask[:, :, :], ALU.mult).then_inc(kx_ok.sem, 1)

            def q_shift(i, c):
                src = PS[:, 0:2, :].rearrange("p a (h d) -> p (a h) d", d=DA)
                dve.wait_ge(q_mm.sem, q_mm.at(i, c + 1))
                dve.reduce_max(q_max[:, :], src, AX_X).then_inc(q_mx.sem, 1)
                dve.wait_ge(q_mx.sem, q_mx.at(i, 2 * c + 1))
                if exists(q_exp.at(i, c)):
                    dve.wait_ge(q_exp.sem, q_exp.at(i, c))
                dve.tensor_tensor(q_sh.rearrange("p (h d) -> p h d", h=HA), src,
                                  q_max[:, :].unsqueeze(2).to_broadcast([P, HA, DA]), ALU.subtract)\
                   .then_inc(q_mx.sem, 1)

            def q_sums(i, c):
                if exists(q_rc.at(i, 2 * c)):
                    dve.wait_ge(q_rc.sem, q_rc.at(i, 2 * c))
                dve.wait_ge(q_exp.sem, q_exp.at(i, c + 1))
                dve.reduce_sum(q_sum[:, :], EQ[c].rearrange("p (h d) -> p h d", h=HA), AX_X).then_inc(q_rc.sem, 1)
                dve.wait_ge(q_rc.sem, q_rc.at(i, 2 * c + 1))
                if exists(q_hat.at(i, c)):
                    dve.wait_ge(q_hat.sem, q_hat.at(i, c))
                dve.reciprocal(q_rcp[:, :], q_sum[:, :]).then_inc(q_rc.sem, 1)

            def c_norm(i):
                src = PS[:, 5:7, :].rearrange("p a (b n) -> p (a b) n", n=P)
                dve.wait_ge(c_mm.sem, c_mm.at(i))
                for s in range(2):
                    lo, hi = DA * s, DA * s + DA
                    dve.reduce_sum(z_sum[lo:hi, :], src[lo:hi, :, lo:hi], AX_X).then_inc(c_ev.sem, 1)
                dve.wait_ge(c_ev.sem, c_ev.at(i, 2))
                dve.reciprocal(z_rcp[:, :], z_sum[:, :]).then_inc(c_ev.sem, 1)
                dve.wait_ge(c_ev.sem, c_ev.at(i, 3))
                for s in range(2):
                    lo, hi = DA * s, DA * s + DA
                    dve.tensor_tensor(ctx_bd[lo:hi, :, lo:hi], src[lo:hi, :, lo:hi],
                                      z_rcp[lo:hi, :].unsqueeze(2).to_broadcast([DA, PAIRS, DA]), ALU.mult)\
                       .then_inc(c_ev.sem, 1)

            def m_copy(j):
                dve.wait_ge(m_mm.sem, m_mm.at(j))
                dve.tensor_copy(M_sb[:, :], PS[:, 7, 0:D]).then_inc(m_ev.sem, 1)

            def add_x1(j):
                dve.wait_ge(xb_ok.sem, xb_ok.at(j))
                dve.wait_ge(y_mm.sem, y_mm.at(j))
                dve.tensor_tensor(x1[:, :, :], as_chunks(PS[:, 4, :]), xr, ALU.add).then_inc(x1_ok.sem, 1)
                dve.wait_ge(x1_ok.sem, x1_ok.at(j))
                ln_stats(1, j, x1)

            def mix(f, j, bank, scaled):
                if scaled:
                    dve.wait_ge(f["hT"].sem, f["hT"].at(j))
                    if exists(f["r"].at(j - 1)):
                        dve.wait_ge(f["r"].sem, f["r"].at(j - 1))
                    for n in range(2):
                        dve.tensor_scalar(mixed[n][:, :], PS[:, bank, :], mu[:, n:n + 1], None, ALU.mult)\
                           .then_inc(f["mix"].sem, 1)
                    dve.wait_ge(f["mix"].sem, f["mix"].at(j, 2))
                else:
                    dve.wait_ge(f["mu"].sem, f["mu"].at(j))
                for n in range(2):
                    dve.scalar_tensor_tensor(mixed[n][:, 1:N], PS[:, bank, 0:N - 1], mu[:, 2 + n:3 + n],
                                             mixed[n][:, 1:N], ALU.mult, ALU.add)\
                       .then_inc(f["mix"].sem, 1 if scaled else 2)

            def square(f, j, bank):
                dve.wait_ge(f["relu"].sem, f["relu"].at(j))
                if exists(f["v"].at(j - 1)):
                    dve.wait_ge(f["v"].sem, f["v"].at(j - 1))
                dve.tensor_tensor(k_act[:, :], PS[:, bank, :], k_relu[:, :], ALU.mult).then_inc(f["act"].sem, 1)

            def gate_v(f, j, bank, res, dst):
                dve.wait_ge(f["gate"].sem, f["gate"].at(j))
                dve.wait_ge(f["v"].sem, f["v"].at(j))
                dve.scalar_tensor_tensor(gated[:, :, :], gate[:, :, :], 1.0, as_chunks(PS[:, bank, :]),
                                         ALU.add, ALU.mult).then_inc(f["x"].sem, 1)
                dve.wait_ge(f["x"].sem, f["x"].at(j, 1))
                dve.scalar_tensor_tensor(dst[:, :, :], gated[:, :, :], 0.5, res[:, :, :], ALU.mult, ALU.add)\
                   .then_inc(f["x"].sem, 1)

            def split_h3(j):
                dve.wait_ge(h3_T.sem, h3_T.at(j))
                dve.tensor_copy(h3h[:, :], PS[:, 7, :]).then_inc(h3_sp.sem, 1)
                dve.wait_ge(h3_sp.sem, h3_sp.at(j, 1))
                dve.tensor_tensor(h3l[:, :], PS[:, 7, :], h3h[:, :].bitcast(F32), ALU.subtract).then_inc(h3_sp.sem, 1)

            def end_ffn1(j):
                if exists(x2_st.at(j - 1)):
                    dve.wait_ge(x2_st.sem, x2_st.at(j - 1))
                gate_v(ffn[0], j, 4, x1, x2)
                dve.wait_ge(ffn[0]["x"].sem, ffn[0]["x"].at(j))
                ln_stats(2, j, x2)

            ln1(0)
            k_maxima(0)
            k_shift(0)

            def first_half(i, p, first, last):
                j = i - 1
                q_shift(i, 0)
                q_shift(i, 1)
                q_sums(i, 0)
                if not first:
                    m_copy(j)
                q_shift(i, 2)
                if not first:
                    add_x1(j)
                q_sums(i, 1)
                if not first:
                    ln_norm(1, j, x1, hn)
                q_shift(i, 3)
                if not first:
                    mix(ffn[0], j, 7, False)
                q_sums(i, 2)
                if not last:
                    ln1(i + 1)
                if not first:
                    square(ffn[0], j, 4)
                q_sums(i, 3)
                if not first:
                    end_ffn1(j)
                c_norm(i)
                if not first:
                    ln_norm(2, j, x2, h3)
                if not last:
                    k_maxima(i + 1)
                if not first:
                    split_h3(j)
                if not last:
                    k_shift(i + 1)

            over_batches(dve, first_half, NB)
            m_copy(NB - 1)
            add_x1(NB - 1)
            ln_norm(1, NB - 1, x1, hn)
            mix(ffn[0], NB - 1, 7, False)
            square(ffn[0], NB - 1, 4)
            end_ffn1(NB - 1)
            ln_norm(2, NB - 1, x2, h3)
            split_h3(NB - 1)

            dve.wait_ge(qkv_st.sem, qkv_st.at(NB - 1))
            dve.wait_ge(x2_st.sem, x2_st.at(NB - 1))

            def k_copy(i, g):
                dve.wait_ge(kT_ps.sem, kT_ps.at(i, g + 1))
                if exists(k_padded[g % 2].at(i, 64 * (g // 2))):
                    dve.wait_ge(k_padded[g % 2].sem, k_padded[g % 2].at(i, 64 * (g // 2)))
                if exists(mx_mm.at(i, 8 * (g - 1))):
                    dve.wait_ge(mx_mm.sem, mx_mm.at(i, 8 * (g - 1)))
                if exists(s_mm.at(i, 8 * (g - 1))):
                    dve.wait_ge(s_mm.sem, s_mm.at(i, 8 * (g - 1)))
                dve.tensor_copy(k_st[g % 2][:, :], PS[:, 7, :]).then_inc(kT_sb.sem, 1)

            def q_copy(i, g, bank):
                dve.wait_ge(qT_ps.sem, qT_ps.at(i, g + 1))
                if exists(s_mm.at(i, 8 * (g - 1))):
                    dve.wait_ge(s_mm.sem, s_mm.at(i, 8 * (g - 1)))
                dve.tensor_copy(q_st[g % 2][:, :], PS[:, bank, :]).then_inc(qT_sb.sem, 1)

            def maxima(i, g):
                for m in range(8):
                    h, half = m // 2, m % 2
                    dve.wait_ge(mx_mm.sem, mx_mm.at(i, 8 * g + m + 1))
                    dve.reduce_max(row_max[:, 2 * half:2 * half + 2, h], PS[:, 2 * half:2 * half + 2, :], AX_X)\
                       .then_inc(mx_ok.sem, 1)
                dve.wait_ge(mx_T.sem, mx_T.at(i, g + 1))
                dve.tensor_scalar(neg_c[:, :], PS[0:4, 0, :], -1.0, None, ALU.mult).then_inc(mx_neg.sem, 1)

            def pv_copy(i, g):
                dve.wait_ge(pv.sem, pv.at(i, 4 * g + 4))
                if exists(u_T.at(i, g - 1)):
                    dve.wait_ge(u_T.sem, u_T.at(i, g - 1))
                dve.tensor_copy(U[g % 2][:, :], PS[:, 4 + g % 2, :]).then_inc(pv_sb.sem, 1)

            def normalise(i, g, bank):
                src = PS[:, bank, :].rearrange("p (c j r) -> p c j r", c=NC, j=4)
                dve.wait_ge(u_T.sem, u_T.at(i, g + 1))
                dve.reciprocal(den_rcp[:, :, :], src[:, :, :, DB]).then_inc(u_norm.sem, 1)
                dve.wait_ge(u_norm.sem, u_norm.at(i, 2 * g + 1))
                dve.tensor_tensor(c_tok[:, :, 32 * g:32 * g + 32].rearrange("p c (j d) -> p c j d", j=4),
                                  src[:, :, :, 0:DB], den_rcp[:, :, :].unsqueeze(3).to_broadcast([P, NC, 4, DB]),
                                  ALU.mult).then_inc(u_norm.sem, 1)

            def add_x3(j):
                dve.wait_ge(x2_in.sem, x2_in.at(j))
                dve.wait_ge(o_mm.sem, o_mm.at(j))
                dve.tensor_tensor(x1[:, :, :], as_chunks(PS[:, 6, :]), x2[:, :, :], ALU.add).then_inc(x3_ok.sem, 1)
                dve.wait_ge(x3_ok.sem, x3_ok.at(j))
                ln_stats(3, j, x1)

            k_copy(0, 0)
            q_copy(0, 0, 6)

            def second_half(i, p, first, last, main=True):
                j = i - 1
                if main:
                    maxima(i, 0)
                    k_copy(i, 1)
                if not first:
                    normalise(j, 2, 6)
                if main:
                    q_copy(i, 1, 6)
                if not first:
                    pv_copy(j, 3)
                if main:
                    maxima(i, 1)
                    k_copy(i, 2)
                if not first:
                    normalise(j, 3, 6)
                if main:
                    q_copy(i, 2, 6)
                if not first:
                    dve.wait_ge(ct_ps.sem, ct_ps.at(j))
                    dve.tensor_copy(cT[:, :], PS[:, 7, :]).then_inc(ct_sb.sem, 1)
                if main:
                    pv_copy(i, 0)
                if not first:
                    add_x3(j)
                if main:
                    maxima(i, 2)
                    k_copy(i, 3)
                    normalise(i, 0, 6)
                if not first:
                    ln_norm(3, j, x1, hn)
                if main:
                    q_copy(i, 3, 6)
                if not first:
                    mix(ffn[1], j, 7, True)
                if main:
                    pv_copy(i, 1)
                    maxima(i, 3)
                if not first:
                    square(ffn[1], j, 6)
                if main and not last:
                    k_copy(i + 1, 0)
                if not first:
                    if exists(out_st.at(j - 1)):
                        dve.wait_ge(out_st.sem, out_st.at(j - 1))
                    gate_v(ffn[1], j, 6, x1, gated)
                if main and not last:
                    q_copy(i + 1, 0, 7)
                if main:
                    normalise(i, 1, 6)
                    pv_copy(i, 2)

            over_batches(dve, second_half, NB)
            second_half(NB, 0, False, True, main=False)

        @block.tensor
        def _(pe):
            pe.wait_ge(w_in.sem, 160)
            pe.wait_ge(id_ok.sem, 1)
            pe.wait_ge(const_ok.sem, 13)
            for n in range(2):
                for a in range(4):
                    last_mm = pe.transpose(PS[:, n, a * P:(a + 1) * P],
                                           wqkv_raw[:, 2 * INNER + (4 * n + a) * P:2 * INNER + (4 * n + a + 1) * P],
                                           ident[:, :])
                last_mm.then_inc(wT.sem, 1)
            for n, some in ((2, range(0, 4)), (3, range(4, 7))):
                for a, w in enumerate(some):
                    last_mm = pe.transpose(PS[:, n, a * P:(a + 1) * P], raw7[:, w, :], ident[:, :])
                last_mm.then_inc(wT.sem, 1)
            pe.matmul(PS[:, 4, 0:D], ones_row[:, :], b_row[:, :], start=True, stop=True).then_inc(wT.sem, 1)
            pe.wait_ge(wsplit.sem, 3)
            pe.wait_ge(wT_sb.sem, 4)
            pe.wait_ge(w3s.sem, 2)
            pe.wait_ge(b_ok.sem, 3)

            def four_transposes(src, bank):
                for c in range(NC):
                    mm = pe.transpose(PS[:, bank, c * P:(c + 1) * P], src(c), ident[:, :])
                return mm

            def halves(dst, w, h, stop=True):
                pe.matmul(dst, w[0], h[0], start=True, stop=False)
                pe.matmul(dst, w[0], h[1], start=False, stop=False)
                return pe.matmul(dst, w[1], h[0], start=False, stop=stop)

            def head_T(n):
                if exists(ffn[0]["gate"].at(n - 2)):
                    pe.wait_ge(ffn[0]["gate"].sem, ffn[0]["gate"].at(n - 2))
                if exists(h1_sb.at(n - 1)):
                    pe.wait_ge(h1_sb.sem, h1_sb.at(n - 1))
                if exists(kx_max.at(n - 1)):
                    pe.wait_ge(kx_max.sem, kx_max.at(n - 1))
                pe.wait_ge(ln[0].sem, ln[0].at(n))
                four_transposes(lambda c: h1[:, c, :], 7).then_inc(h1_T.sem, 1)

            def head_kmax(n):
                pe.wait_ge(h1_sp.sem, h1_sp.at(n))
                if exists(ffn[0]["x"].at(n - 2)):
                    pe.wait_ge(ffn[0]["x"].sem, ffn[0]["x"].at(n - 2))
                if exists(kx_ok.at(n - 1)):
                    pe.wait_ge(kx_ok.sem, kx_ok.at(n - 1))
                pe.wait_ge(h1_sb.sem, h1_sb.at(n))
                for a in range(PAIRS):
                    if a >= 2:
                        pe.wait_ge(kx_max.sem, kx_max.at(n, a - 1))
                    pe.matmul(PS[:, (4, 7)[a % 2], :], wqk_hi[:, INNER + a * P:INNER + (a + 1) * P], h1h[:, :],
                              start=True, stop=True).then_inc(kx_mm.sem, 1)

            def head_kT(n):
                pe.wait_ge(kx_max.sem, kx_max.at(n))
                pe.transpose(PS[0:8, 4, 0:P], k_max[:, :], ident[:, :]).then_inc(kx_T.sem, 1)

            def proj_q(i, c):
                if exists(q_mx.at(i, 2 * c)):
                    pe.wait_ge(q_mx.sem, q_mx.at(i, 2 * c))
                for b in range(2):
                    cols = slice(b * 512, b * 512 + 512)
                    tok = slice(c * P, c * P + P)
                    mm = halves(PS[:, b, :], (h1h[:, tok], h1l[:, tok]), (wqk_hi[:, cols], wqk_lo[:, cols]))
                mm.then_inc(q_mm.sem, 1)

            def proj_k(i, c):
                if exists(k_exp.at(i, c)):
                    pe.wait_ge(k_exp.sem, k_exp.at(i, c))
                if c == 0:
                    pe.wait_ge(kx_ok.sem, kx_ok.at(i))
                for b in range(2):
                    cols = slice(INNER + b * 512, INNER + b * 512 + 512)
                    tok = slice(c * P, c * P + P)
                    halves(PS[:, 2 + b, :], (h1h[:, tok], h1l[:, tok]), (wqk_hi[:, cols], wqk_lo[:, cols]), stop=False)
                    mm = pe.matmul(PS[:, 2 + b, :], ones8[:, :],
                                   k_neg[:, 4 * b:4 * b + 4, :].rearrange("p a n -> p (a n)"), start=False, stop=True)
                mm.then_inc(k_mm.sem, 1)

            def context(i, c):
                if c == 0:
                    if exists(t_ev.at(i - 1)):
                        pe.wait_ge(t_ev.sem, t_ev.at(i - 1))
                    if exists(c_ev.at(i - 1)):
                        pe.wait_ge(c_ev.sem, c_ev.at(i - 1))
                pe.wait_ge(q_hat.sem, q_hat.at(i, c + 1))
                pe.wait_ge(k_exp.sem, k_exp.at(i, c + 1))
                for a in range(PAIRS):
                    cols = slice(a * P, a * P + P)
                    mm = pe.matmul(PS[:, 5 + a // 4, (a % 4) * P:(a % 4) * P + P], EK[c][:, cols], EQ[c][:, cols],
                                   start=(c == 0 and a % 4 == 0), stop=(c == NC - 1), skip_group_check=True)
                mm.then_inc(c_mm.sem, 1)

            def ctx_wout(j):
                pe.wait_ge(c_ev.sem, c_ev.at(j))
                for a in range(PAIRS):
                    mm = pe.matmul(PS[:, 5 + a // 4, (a % 4) * P:(a % 4) * P + P], ctx_bd[:, a, :], wout_sb[:, a, :],
                                   start=True, stop=True)
                mm.then_inc(t_mm.sem, 1)

            def wv_ctx_wout(j):
                pe.wait_ge(t_ev.sem, t_ev.at(j))
                if exists(p_ev.at(j - 1)):
                    pe.wait_ge(p_ev.sem, p_ev.at(j - 1))
                for a in range(PAIRS):
                    mm = pe.matmul(PS[:, 7, 0:D], WvT[:, a, :], T_sb[:, a, :], start=(a == 0), stop=(a == PAIRS - 1))
                mm.then_inc(m_mm.sem, 1)

            def attn_out(j, p):
                pe.wait_ge(m_ev.sem, m_ev.at(j))
                for c in range(NC):
                    mm = pe.matmul(PS[:, 4, c * D:(c + 1) * D], h1T[p][:, c * P:(c + 1) * P], M_sb[:, :],
                                   start=True, stop=True)
                mm.then_inc(y_mm.sem, 1)

            def ffn_T(f, n, j, bank):
                pe.wait_ge(ln[n].sem, ln[n].at(j))
                four_transposes(lambda c: hn[:, c, :], bank).then_inc(f["hT"].sem, 1)

            def ffn_kr(f, j, bank_k, bank_r):
                pe.wait_ge(f["mix"].sem, f["mix"].at(j))
                pe.matmul(PS[:, bank_k, :], WkT, mixed[1][:, :], start=True, stop=True).then_inc(f["k"].sem, 1)
                for c in range(NC):
                    mm = pe.matmul(PS[:, bank_r, c * D:(c + 1) * D], mixed[0][:, c * P:(c + 1) * P], WrT,
                                   start=True, stop=True)
                mm.then_inc(f["r"].sem, 1)

            def ffn_v(f, j, bank):
                pe.wait_ge(f["act"].sem, f["act"].at(j))
                for c in range(NC):
                    mm = pe.matmul(PS[:, bank, c * D:(c + 1) * D], k_act[:, c * P:(c + 1) * P], WvfT,
                                   start=True, stop=True)
                mm.then_inc(f["v"].sem, 1)

            def h3_transposes(j, final):
                pe.wait_ge(ln[2].sem, ln[2].at(j))
                if not final:
                    pe.wait_ge(kx_max.sem, kx_max.at(j + 2))
                pe.wait_ge(ffn[0]["gate"].sem, ffn[0]["gate"].at(j))
                four_transposes(lambda c: h3[:, c, :], 7).then_inc(h3_T.sem, 1)

            def proj_b(j, final):
                pe.wait_ge(h3_sp.sem, h3_sp.at(j))
                pe.wait_ge(ffn[0]["x"].sem, ffn[0]["x"].at(j))
                if not final:
                    pe.wait_ge(kx_ok.sem, kx_ok.at(j + 2))
                for c in range(NC):
                    if c >= 2:
                        pe.wait_ge(p_ev.sem, p_ev.at(j, c - 1))
                    tok = slice(c * P, c * P + P)
                    halves(PS[:, (4, 7)[c % 2], 0:W3], (h3h[:, tok], h3l[:, tok]), (w3h[:, :], w3l[:, :]))\
                        .then_inc(p_mm.sem, 1)

            head_T(0)
            head_kmax(0)
            head_kT(0)

            def first_half(i, p, first, last):
                j = i - 1
                side = not first
                proj_q(i, 0)
                proj_k(i, 0)
                proj_q(i, 1)
                if side:
                    ctx_wout(j)
                proj_k(i, 1)
                if side:
                    wv_ctx_wout(j)
                proj_q(i, 2)
                if side:
                    attn_out(j, 1 - p)
                proj_k(i, 2)
                context(i, 0)
                proj_q(i, 3)
                if side:
                    ffn_T(ffn[0], 1, j, 7)
                proj_k(i, 3)
                if side:
                    pe.wait_ge(x1_ok.sem, x1_ok.at(j))
                    ffn_kr(ffn[0], j, 4, 7)
                context(i, 1)
                if side:
                    ffn_v(ffn[0], j, 4)
                context(i, 2)
                if not last:
                    head_T(i + 1)
                context(i, 3)
                if not last:
                    head_kmax(i + 1)
                if side:
                    h3_transposes(j, last)
                if not last:
                    head_kT(i + 1)
                if side:
                    proj_b(j, last)

            over_batches(pe, first_half, NB)
            j = NB - 1
            ctx_wout(j)
            wv_ctx_wout(j)
            attn_out(j, 1)
            ffn_T(ffn[0], 1, j, 7)
            pe.wait_ge(x1_ok.sem, x1_ok.at(j))
            ffn_kr(ffn[0], j, 4, 7)
            ffn_v(ffn[0], j, 4)
            h3_transposes(j, True)
            proj_b(j, True)

            pe.wait_ge(qkv_st.sem, qkv_st.at(NB - 1))
            pe.wait_ge(x2_st.sem, x2_st.at(NB - 1))
            pe.wait_ge(zeroed.sem, zeroed.at(0))

            def parts_T(i, g, t, bank):
                pe.wait_ge(part.sem, part.at(i, 8 * g + 8))
                mm = four_transposes(lambda c: parts[g % 2][:, t, c, :].bitcast(F32), bank)
                mm.then_inc((qT_ps, kT_ps)[t].sem, 1)

            def maxima(i, g):
                if exists(s_exp.at(i, 8 * g)):
                    pe.wait_ge(s_exp.sem, s_exp.at(i, 8 * g))
                pe.wait_ge(qT_sb.sem, qT_sb.at(i, g + 1))
                pe.wait_ge(kT_sb.sem, kT_sb.at(i, g + 1))
                for m in range(8):
                    h, half = m // 2, m % 2
                    if m >= 2:
                        pe.wait_ge(mx_ok.sem, mx_ok.at(i, 8 * g + m - 1))
                    rows = slice(32 * h, 32 * h + 32)
                    for t in range(2):
                        c = 2 * half + t
                        mm = pe.matmul(PS[:, c, :], q_st[g % 2][rows, c * P:(c + 1) * P], k_st[g % 2][rows, :],
                                       start=True, stop=True)
                    mm.then_inc(mx_mm.sem, 1)
                pe.wait_ge(mx_ok.sem, mx_ok.at(i, 8 * g + 8))
                for c in range(NC):
                    mm = pe.transpose(PS[0:4, 0, c * P:(c + 1) * P], row_max[:, c, :], ident[:, :])
                mm.then_inc(mx_T.sem, 1)

            def scores(i, s):
                g, h = s // 4, s % 4
                if h == 0:
                    pe.wait_ge(k_padded[g % 2].sem, k_padded[g % 2].at(i, 64 * (g // 2) + 64))
                    pe.wait_ge(mx_neg.sem, mx_neg.at(i, g + 1))
                for half in range(2):
                    if exists(s_exp.at(i, 2 * s + half - 1)):
                        pe.wait_ge(s_exp.sem, s_exp.at(i, 2 * s + half - 1))
                    for t in range(2):
                        kc = 2 * half + t
                        pe.matmul(PS[:, kc, :], k_pad[g % 2][:, h, kc * P:(kc + 1) * P], q_st[g % 2][:, :],
                                  start=True, stop=False)
                        mm = pe.matmul(PS[:, kc, :], sel4[:, h, :], neg_c[:, :], start=False, stop=True)
                    mm.then_inc(s_mm.sem, 1)

            def weigh_values(i, g, kc, p):
                if kc == 0:
                    if exists(pv_sb.at(i, g - 1)):
                        pe.wait_ge(pv_sb.sem, pv_sb.at(i, g - 1))
                    pe.wait_ge(v_ok.sem, v_ok.at(i))
                pe.wait_ge(s_exp.sem, s_exp.at(i, 8 * g + 7 + kc // 2))
                for h in range(4):
                    mm = pe.matmul(PS[32 * h:32 * h + 32, 4 + g % 2, :], v32[p][:, kc, 4 * g + h, :],
                                   probs[g % 2][:, h, kc, :], start=(kc == 0), stop=(kc == NC - 1),
                                   tile_position=(0, 32 * h), skip_group_check=True)
                mm.then_inc(pv.sem, 1)

            def u_transposes(i, g, bank):
                pe.wait_ge(pv_sb.sem, pv_sb.at(i, g + 1))
                four_transposes(lambda c: U[g % 2][:, c * P:(c + 1) * P], bank).then_inc(u_T.sem, 1)

            parts_T(0, 0, 1, 7)
            parts_T(0, 0, 0, 6)

            def second_half(i, p, first, last, main=True):
                j = i - 1
                f = ffn[1]
                side = not first
                for s in range(HB):
                    g = s // 4
                    if main:
                        if s % 4 == 0:
                            maxima(i, g)
                        scores(i, s)
                    if main and g >= 1:
                        weigh_values(i, g - 1, s % 4, p)
                    if side and g == 0:
                        weigh_values(j, NG - 1, s % 4, 1 - p)
                    if s == 0:
                        if main:
                            pe.wait_ge(qT_sb.sem, qT_sb.at(i, 1))
                            parts_T(i, 1, 1, 7)
                        if side:
                            pe.wait_ge(u_norm.sem, u_norm.at(j, 4))
                            u_transposes(j, 2, 6)
                    if s == 1 and main:
                        if exists(u_norm.at(j, 6)):
                            pe.wait_ge(u_norm.sem, u_norm.at(j, 6))
                        pe.wait_ge(qT_sb.sem, qT_sb.at(i, 1))
                        parts_T(i, 1, 0, 6)
                    if s == 4:
                        if main:
                            pe.wait_ge(kT_sb.sem, kT_sb.at(i, 2))
                            parts_T(i, 2, 1, 7)
                            pe.wait_ge(qT_sb.sem, qT_sb.at(i, 2))
                        if side:
                            u_transposes(j, 3, 6)
                    if s == 5 and main:
                        if exists(u_norm.at(j)):
                            pe.wait_ge(u_norm.sem, u_norm.at(j))
                        pe.wait_ge(qT_sb.sem, qT_sb.at(i, 2))
                        parts_T(i, 2, 0, 6)
                    if s == 6 and side:
                        if main:
                            pe.wait_ge(kT_sb.sem, kT_sb.at(i, 3))
                        pe.wait_ge(u_norm.sem, u_norm.at(j))
                        four_transposes(lambda c: c_tok[:, c, :], 7).then_inc(ct_ps.sem, 1)
                    if s == 7 and side:
                        if main:
                            pe.wait_ge(qT_sb.sem, qT_sb.at(i, 3))
                        pe.wait_ge(ct_sb.sem, ct_sb.at(j))
                        for c in range(NC):
                            mm = pe.matmul(PS[:, 6, c * D:(c + 1) * D], cT[:, c * P:(c + 1) * P], WOT,
                                           start=True, stop=True)
                        mm.then_inc(o_mm.sem, 1)
                    if s == 8 and main:
                        if exists(ct_sb.at(j)):
                            pe.wait_ge(ct_sb.sem, ct_sb.at(j))
                        pe.wait_ge(kT_sb.sem, kT_sb.at(i, 3))
                        parts_T(i, 3, 1, 7)
                        if exists(x3_ok.at(j)):
                            pe.wait_ge(x3_ok.sem, x3_ok.at(j))
                        pe.wait_ge(qT_sb.sem, qT_sb.at(i, 3))
                        u_transposes(i, 0, 6)
                    if s == 9 and main:
                        pe.wait_ge(u_norm.sem, u_norm.at(i, 2))
                        parts_T(i, 3, 0, 6)
                    if s == 10 and side:
                        if main:
                            pe.wait_ge(kT_sb.sem, kT_sb.at(i, 4))
                        ffn_T(f, 3, j, 7)
                    if s == 11 and side:
                        if main:
                            pe.wait_ge(qT_sb.sem, qT_sb.at(i, 4))
                        ffn_kr(f, j, 6, 7)
                    if s == 13:
                        if main and not last:
                            if exists(f["gate"].at(j)):
                                pe.wait_ge(f["gate"].sem, f["gate"].at(j))
                            pe.wait_ge(kT_sb.sem, kT_sb.at(i, 4))
                            parts_T(i + 1, 0, 1, 7)
                        if side:
                            ffn_v(f, j, 6)
                    if s == 14 and main and not last:
                        pe.wait_ge(kT_sb.sem, kT_sb.at(i + 1, 1))
                        parts_T(i + 1, 0, 0, 7)
                    if s == 15 and main:
                        if exists(f["x"].at(j)):
                            pe.wait_ge(f["x"].sem, f["x"].at(j))
                        pe.wait_ge(qT_sb.sem, qT_sb.at(i, 4))
                        u_transposes(i, 1, 6)

            over_batches(pe, second_half, NB)
            second_half(NB, 0, False, True, main=False)


_PRE = "L0_"
_INS = ["attn_a_x", "attn_a_w_qkv", "attn_a_w_out", "attn_a_b_out", "attn_b_W_Q", "attn_b_W_K", "attn_b_W_V",
        "attn_b_W_O", "ffn_W_r", "ffn_W_k", "ffn_W_v", "ffn_mu_r", "ffn_mu_k"]


def rope_tables(n, d, heads, theta=10000.0):
    inv = 1.0 / theta ** (np.arange(0, d, 2, dtype=np.float32) / np.float32(d))
    angle = np.outer(np.arange(n, dtype=np.float32), inv.astype(np.float32)).astype(np.float32)
    cos, sin = np.repeat(np.cos(angle), 2, axis=-1), np.repeat(np.sin(angle), 2, axis=-1)
    sin[:, 0::2] *= -1.0

    def lay(t):
        both = np.concatenate([np.tile(t / np.sqrt(d), (1, heads)), np.tile(t, (1, heads))], axis=1)
        return np.ascontiguousarray(both.reshape(n // P, P, -1).transpose(1, 0, 2)).astype(np.float32)

    return lay(cos), lay(sin)


def kernel(**inputs):
    import numpy as _np
    import concourse.bacc as _bacc
    from concourse.bass_utils import run_bass_kernel_spmd as _run

    nc = _bacc.Bacc("TRN2", target_bir_lowering=False, num_devices=1)
    arrays, args = {}, []
    for name in _INS:
        a = _np.ascontiguousarray(inputs[_PRE + name])
        arrays[f"in_{name}"] = a
        args.append(nc.dram_tensor(f"in_{name}", a.shape, mybir.dt.from_np(a.dtype), kind="ExternalInput").ap())
    shape = tuple(inputs["L0_attn_a_x"].shape)
    for name, a in zip(("cos", "sin"), rope_tables(shape[1], 8, 16)):
        arrays[f"rope_{name}"] = a
        args.append(nc.dram_tensor(f"rope_{name}", a.shape, F32, kind="ExternalInput").ap())
    out = nc.dram_tensor("out_0", shape, F32, kind="ExternalOutput").ap()
    hybrid_block(nc, *args, out)
    r = _run(nc, [arrays], core_ids=[0])
    return r.results[0]["out_0"]
```

```python
from contextlib import ExitStack

import numpy as np

import concourse.bass as bass
from concourse import mybir

F32 = mybir.dt.float32
F32R = mybir.dt.float32r
I32 = mybir.dt.int32
ALU = mybir.AluOpType
ACT = mybir.ActivationFunctionType
AX_X = mybir.AxisListType.X

P = 128
EPS = 1e-5


class Signal:

    def __init__(self, ctx, nc, name, per):
        self.sem = ctx.enter_context(nc.semaphore(name))
        self.per = per

    def at(self, batch, count=None):
        return batch * self.per + (self.per if count is None else count)


def exists(value):
    return not isinstance(value, int) or value > 0


def over_batches(eng, step, n, tail):
    for b in range(3):
        step(b, b % 2)
    with eng.Fori(3, n - 2, 2) as i:
        step(i, 1)
        step(i + 1, 0)
    for b in range(n - 1, n + tail):
        step(b, b % 2)


def hybrid_block(nc, x, w_qkv, w_out, b_out, W_Q, W_K, W_V, W_O, W_r, W_k, W_v, mu_r, mu_k,
                 rope_cos, rope_sin, out):
    NB, N, D = x.shape
    NC = N // P
    INNER = w_out.shape[0]
    DA = 64
    HA = INNER // DA
    PAIRS = INNER // P
    HB = 16
    DB = D // HB
    NG = HB // 4
    W3 = 3 * D
    assert D == P and NC == 4 and PAIRS == 8 and DB == 8 and NB % 2 == 0 and NB >= 6
    SCALE_A = DA ** -0.5
    REACH = 40.0

    x2_dram = nc.dram_tensor("x2_scratch", [NB, P, NC * D], F32, kind="Internal").ap()
    qkv_dram = nc.dram_tensor("qkv_scratch", [NB, P, NC * W3], F32, kind="Internal").ap()

    x_view = x.rearrange("b (c p) d -> b p c d", p=P)
    out_view = out.rearrange("b (c p) d -> b p c d", p=P)

    with ExitStack() as ctx:
        def sb(name, shape, dt=F32):
            return ctx.enter_context(nc.sbuf_tensor(name, shape, dt))

        def sig(name, per=1):
            return Signal(ctx, nc, name, per)

        work = sb("work", [P, 16384])
        work_r = sb("work_r", [P, 4096], F32R)
        taken = [0]

        def carve(cols):
            at = taken[0]
            taken[0] += cols
            assert taken[0] <= 16384
            return work[:, at:at + cols]

        E_all = carve(NC * 2 * INNER)
        E_v = E_all.rearrange("p (c n) -> p c n", c=NC)
        EQ = [E_v[:, c, 0:INNER] for c in range(NC)]
        EK = [E_v[:, c, INNER:2 * INNER] for c in range(NC)]
        wqkv_raw = E_all[:, 0:3 * INNER]
        ctx_bd = carve(INNER).rearrange("p (a n) -> p a n", a=PAIRS)
        T_sb = carve(INNER).rearrange("p (a n) -> p a n", a=PAIRS)
        q_sh = carve(INNER)
        WvT = carve(INNER).rearrange("p (a n) -> p a n", a=PAIRS)
        wout_sb = carve(INNER).rearrange("p (a n) -> p a n", a=PAIRS)
        h1T = [carve(N) for _ in range(2)]
        xa = carve(N).rearrange("p (c d) -> p c d", c=NC)
        h1 = carve(N).rearrange("p (c d) -> p c d", c=NC)
        xr = carve(N).rearrange("p (c d) -> p c d", c=NC)
        wqk_hi, wqk_lo = work_r[:, 0:2 * INNER], work_r[:, 2 * INNER:4 * INNER]
        probs = [work[:, g * 8192:(g + 1) * 8192].rearrange("p (j k n) -> p j k n", j=4, k=NC)
                 for g in range(2)]
        k_pad = [work_r[:, g * 2048:(g + 1) * 2048].rearrange("p (j n) -> p j n", j=4)
                 for g in range(2)]

        ident = sb("ident", [P, P])
        raw7 = sb("raw7", [P, 7, D])
        W7T = sb("W7T", [P, 7, D])
        WrT, WkT, WvfT, WOT = (W7T[:, n, :] for n in (0, 1, 2, 6))
        mu = sb("mu", [P, 4])
        b_row = sb("b_row", [1, D])
        ones_row = sb("ones_row", [1, P])
        b_all = sb("b_all", [P, D])
        one = sb("one", [P, 1])
        half_neg = sb("half_neg", [P, NC])
        cos_t = sb("cos_t", [P, NC, 2 * D])
        sin_t = sb("sin_t", [P, NC, 2 * D])

        h1h, h1l = sb("h1h", [P, N], F32R), sb("h1l", [P, N], F32R)
        h3h, h3l = sb("h3h", [P, N], F32R), sb("h3l", [P, N], F32R)
        w3h, w3l = sb("w3h", [P, W3], F32R), sb("w3l", [P, W3], F32R)
        ones8f = sb("ones8f", [8, P])
        ones8 = sb("ones8", [8, P], F32R)
        negmask = sb("negmask", [8, PAIRS, P])
        k_neg = sb("k_neg", [8, PAIRS, P], F32R)
        k_max = sb("k_max", [P, PAIRS])
        M_sb = sb("M_sb", [P, D])
        q_max = sb("q_max", [P, HA])
        q_sum, q_rcp = sb("q_sum", [P, HA]), sb("q_rcp", [P, HA])
        z_sum, z_rcp = sb("z_sum", [P, PAIRS]), sb("z_rcp", [P, PAIRS])
        stats = [(sb(f"st{n}", [P, NC, 6]), sb(f"mom{n}", [P, 6, NC]), sb(f"ve{n}", [P, NC]),
                  sb(f"rs{n}", [P, NC])) for n in range(4)]
        x1 = sb("x1", [P, NC, D])
        x2 = sb("x2", [P, NC, D])
        hn = sb("hn", [P, NC, D])
        h3 = sb("h3", [P, NC, D])
        mixed = [sb("mixed_r", [P, N]), sb("mixed_k", [P, N])]
        k_relu, k_act = sb("k_relu", [P, N]), sb("k_act", [P, N])
        gate = sb("gate", [P, NC, D])
        gated = sb("gated", [P, NC, D])
        qkv_sb = sb("qkv_sb", [P, NC, W3])

        qk_rot = sb("qk_rot", [P, NC, 2 * D])
        rot = sb("rot", [P, NC, 2 * D])
        v32 = [sb(f"v32_{p}", [P, NC, HB, 32]) for p in range(2)]
        parts = [sb(f"parts{g}", [P, 2, NC, P], F32R) for g in range(2)]
        q_st = [sb(f"q_st{g}", [P, N], F32R) for g in range(2)]
        k_st = [sb(f"k_st{g}", [P, N], F32R) for g in range(2)]
        row_max = sb("row_max", [P, NC, 4])
        neg_c = sb("neg_c", [4, N], F32R)
        sel4f = sb("sel4f", [4, 4, P])
        sel4 = sb("sel4", [4, 4, P], F32R)
        U = [sb(f"U{g}", [P, N]) for g in range(2)]
        den_rcp = sb("den_rcp", [P, NC, 4])
        c_tok = sb("c_tok", [P, NC, D])
        cT = sb("cT", [P, N])
        w_sq = E_all[:, 3 * INNER:5 * INNER]
        ones_col = sb("ones_col", [P, 1])
        w_norm = sb("w_norm", [1, 1])
        qk_sq = sb("qk_sq", [P, NC, 2 * D])
        qk_norm = sb("qk_norm", [P, NC, 2 * HB])
        norm_max = sb("norm_max", [P, NC, 2 * HB])
        norm_col = sb("norm_col", [P, 2])
        norm_two = sb("norm_two", [1, 3])
        bounded_a, bounded_b = sb("bounded_a", [1, 1], I32), sb("bounded_b", [1, 1], I32)
        PS = ctx.enter_context(nc.psum_tensor("PS", [P, 8, 512], F32))

        def there(batch):
            return not isinstance(batch, int) or 0 <= batch < NB

        def as_chunks(ap):
            return ap.rearrange("p (c d) -> p c d", c=NC)

        w_in, c_in = sig("w_in", 16 * 10), sig("c_in", 16 * 6)
        id0, id_ok, const_ok = sig("id0"), sig("id_ok"), sig("const_ok")
        w_sq_ok, w_norm_ps, a_known, b_known = sig("w_sq_ok"), sig("w_norm_ps"), sig("a_known", 2), sig("b_known", 4)
        n_sq, n_red, n_max, n_T = sig("n_sq"), sig("n_red"), sig("n_max"), sig("n_T")
        wsplit, wT, wT_sb, w3s, b_ps, b_ok = (sig(s, n) for s, n in (
            ("wsplit", 3), ("wT", 5), ("wT_sb", 5), ("w3s", 2), ("b_ps", 1), ("b_ok", 3)))

        xa_in, xr_in, x2_st, qkv_st = (sig(s, 16) for s in ("xa_in", "xr_in", "x2_st", "qkv_st"))
        ln = [sig(f"ln{n}", 2 * NC + 7) for n in range(4)]
        rstd = [sig(f"rstd{n}") for n in range(4)]
        h1_T, h1_sb, h1_sp = sig("h1_T"), sig("h1_sb"), sig("h1_sp", 2)
        kx_mm, kx_max, kx_T, kx_ok = (sig("kx_mm", PAIRS), sig("kx_max", PAIRS), sig("kx_T"),
                                      sig("kx_ok"))
        q_mm, k_mm, q_mx, q_exp, k_exp = (sig("q_mm", NC), sig("k_mm", NC), sig("q_mx", 2 * NC),
                                          sig("q_exp", NC), sig("k_exp", NC))
        q_rc, q_hat, c_mm, c_ev = sig("q_rc", 2 * NC), sig("q_hat", NC), sig("c_mm", NC), sig("c_ev", 5)
        t_mm, t_ev, m_mm, m_ev, y_mm, xb_ok, x1_ok = (sig(s) for s in (
            "t_mm", "t_ev", "m_mm", "m_ev", "y_mm", "xb_ok", "x1_ok"))
        ffn = []
        for n in range(2):
            ffn.append({s: sig(f"f{n}_{s}", c) for s, c in (
                ("hT", 1), ("mu", 2), ("mix", 4), ("k", 1), ("r", 1), ("relu", 1), ("act", 1),
                ("gate", 1), ("v", 1), ("x", 2))})
        h3_T, h3_sp, p_mm, p_ev = sig("h3_T"), sig("h3_sp", 2), sig("p_mm", NC), sig("p_ev", NC)
        qkv_in, x2_in, out_st = sig("qkv_in", 16), sig("x2_in", 16), sig("out_st", 16)
        k_padded = [sig(f"k_padded{g}", 16 * 4 * NG // 2) for g in range(2)]
        zeroed = sig("zeroed", 3)
        roped, v_ok, part = sig("roped", 4), sig("v_ok"), sig("part", 8 * NG)
        kT_ps, qT_ps, kT_sb, qT_sb = (sig(s, NG) for s in ("kT_ps", "qT_ps", "kT_sb", "qT_sb"))
        mx_mm, mx_ok, mx_T, mx_neg = (sig("mx_mm", 8 * NG), sig("mx_ok", 8 * NG), sig("mx_T", NG),
                                      sig("mx_neg", NG))
        s_mm, s_exp, pv, pv_sb = sig("s_mm", 32), sig("s_exp", 32), sig("pv", 16), sig("pv_sb", NG)
        u_T, u_norm = sig("u_T", NG), sig("u_norm", 2 * NG)
        ct_ps, ct_sb, o_mm, x3_ok = sig("ct_ps"), sig("ct_sb"), sig("o_mm"), sig("x3_ok")

        block = ctx.enter_context(nc.Block())

        @block.sync
        def _(sp):
            sp.dma_start(wqkv_raw, w_qkv).then_inc(w_in.sem, 16)
            for n, w in enumerate((W_r, W_k, W_v, W_Q, W_K, W_V, W_O)):
                sp.dma_start(raw7[:, n, :], w).then_inc(w_in.sem, 16)
            sp.dma_start(wout_sb, w_out.rearrange("(a p) d -> p a d", p=P)).then_inc(w_in.sem, 16)
            sp.dma_start(b_row[:, :], b_out.rearrange("(a d) -> a d", a=1)).then_inc(w_in.sem, 16)
            sp.dma_start(xa, x_view[0]).then_inc(xa_in.sem, 16)
            sp.dma_start(mu[:, 0:1], mu_r.rearrange("(d a) -> d a", a=1)).then_inc(c_in.sem, 16)
            sp.dma_start(mu[:, 1:2], mu_k.rearrange("(d a) -> d a", a=1)).then_inc(c_in.sem, 16)
            sp.dma_start(cos_t[:, :, :], rope_cos).then_inc(c_in.sem, 16)
            sp.dma_start(sin_t[:, :, :], rope_sin).then_inc(c_in.sem, 16)

            def side(j):
                if exists(x1_ok.at(j - 1)):
                    sp.wait_ge(x1_ok.sem, x1_ok.at(j - 1))
                sp.dma_start(xr, x_view[j]).then_inc(xr_in.sem, 16)

            def store_x2(j):
                sp.wait_ge(ffn[0]["x"].sem, ffn[0]["x"].at(j))
                sp.dma_start(x2_dram[j], x2[:, :, :].rearrange("p c d -> p (c d)")).then_inc(x2_st.sem, 16)

            def store_qkv(j):
                sp.wait_ge(p_ev.sem, p_ev.at(j))
                sp.dma_start(qkv_dram[j], qkv_sb[:, :, :].rearrange("p c d -> p (c d)")).then_inc(qkv_st.sem, 16)

            def first_half(i, p):
                if there(i - 1):
                    side(i - 1)
                if there(i + 1):
                    sp.wait_ge(ln[0].sem, ln[0].at(i))
                    sp.dma_start(xa, x_view[i + 1]).then_inc(xa_in.sem, 16)
                if there(i - 2):
                    store_qkv(i - 2)
                if there(i - 1):
                    store_x2(i - 1)

            over_batches(sp, first_half, NB, 2)

            sp.wait_ge(qkv_st.sem, qkv_st.at(NB - 1))
            sp.wait_ge(n_sq.sem, n_sq.at(NB - 1))
            sp.wait_ge(x2_st.sem, x2_st.at(NB - 1))
            sp.dma_start(qkv_sb[:, :, :].rearrange("p c d -> p (c d)"), qkv_dram[0]).then_inc(qkv_in.sem, 16)

            def pad(i, g):
                sp.wait_ge(kT_sb.sem, kT_sb.at(i, g + 1))
                for j in range(4):
                    sp.dma_start(k_pad[g % 2][32 * j:32 * j + 32, j, :].bitcast(F32),
                                 k_st[g % 2][32 * j:32 * j + 32, :].bitcast(F32))\
                      .then_inc(k_padded[g % 2].sem, 16)

            sp.wait_ge(zeroed.sem, zeroed.at(0))
            pad(0, 0)

            def second_half(i, p):
                if there(i - 1):
                    if exists(x3_ok.at(i - 2)):
                        sp.wait_ge(x3_ok.sem, x3_ok.at(i - 2))
                    sp.dma_start(x2[:, :, :].rearrange("p c d -> p (c d)"), x2_dram[i - 1]).then_inc(x2_in.sem, 16)
                if there(i + 1):
                    sp.wait_ge(roped.sem, roped.at(i))
                    sp.dma_start(qkv_sb[:, :, :].rearrange("p c d -> p (c d)"), qkv_dram[i + 1])\
                      .then_inc(qkv_in.sem, 16)
                for g in range(1, NG):
                    if there(i):
                        pad(i, g)
                if there(i + 1):
                    pad(i + 1, 0)
                if there(i - 1):
                    sp.wait_ge(ffn[1]["x"].sem, ffn[1]["x"].at(i - 1))
                    sp.dma_start(out_view[i - 1], gated[:, :, :]).then_inc(out_st.sem, 16)

            over_batches(sp, second_half, NB, 1)
            sp.wait_ge(out_st.sem, out_st.at(NB - 1))

        @block.gpsimd
        def _(pool):
            pool.memset(ident[:, :], 0.0).then_inc(id0.sem, 1)
            pool.memset(negmask[:, :, :], 0.0).then_inc(const_ok.sem, 1)
            pool.memset(ones8f[:, :], 1.0).then_inc(const_ok.sem, 1)
            pool.memset(sel4f[:, :, :], 0.0).then_inc(const_ok.sem, 1)
            pool.memset(ones_row[:, :], 1.0).then_inc(const_ok.sem, 1)
            pool.memset(ones_col[:, :], 1.0).then_inc(const_ok.sem, 1)
            pool.memset(half_neg[:, :], -0.5).then_inc(const_ok.sem, 1)
            pool.memset(ctx_bd, 0.0).then_inc(const_ok.sem, 1)
            for t in range(2):
                pool.memset(v32[t][:, :, :, :], 0.0).then_inc(const_ok.sem, 1)
            pool.memset(one[:, :], 1.0).then_inc(const_ok.sem, 1)
            pool.memset(norm_max[:, :, :], 0.0).then_inc(const_ok.sem, 1)
            pool.wait_ge(id0.sem, 1)
            pool.affine_select(out=ident[:, :], in_=ident[:, :], compare_op=ALU.not_equal, fill=1.0, base=0,
                               pattern=[[-1, P]], channel_multiplier=1).then_inc(id_ok.sem, 1)
            pool.wait_ge(const_ok.sem, 11)
            pool.affine_select(out=negmask[:, :, :], in_=negmask[:, :, :], compare_op=ALU.not_equal, fill=-1.0,
                               base=0, pattern=[[-1, PAIRS], [0, P]], channel_multiplier=1).then_inc(const_ok.sem, 1)
            pool.affine_select(out=sel4f[:, :, :], in_=sel4f[:, :, :], compare_op=ALU.not_equal, fill=1.0,
                               base=0, pattern=[[-1, 4], [0, P]], channel_multiplier=1).then_inc(const_ok.sem, 1)
            for t in range(2):
                pool.memset(v32[t][:, :, :, DB:DB + 1], 1.0).then_inc(const_ok.sem, 1)

            def rsqrt_var(n, j):
                _, _, ve, rs = stats[n]
                pool.wait_ge(ln[n].sem, ln[n].at(j, NC + 7))
                pool.tensor_tensor(rs[:, :], ve[:, :], half_neg[:, :], ALU.pow).then_inc(rstd[n].sem, 1)

            def split_h1(j, p):
                pool.wait_ge(h1_sb.sem, h1_sb.at(j))
                pool.tensor_tensor(h1h[:, :], h1T[p], one[:, 0:1].to_broadcast([P, N]), ALU.mult).then_inc(h1_sp.sem, 1)
                pool.wait_ge(h1_sp.sem, h1_sp.at(j, 1))
                pool.tensor_tensor(h1l[:, :], h1T[p], h1h[:, :].bitcast(F32), ALU.subtract).then_inc(h1_sp.sem, 1)

            def q_hats(i, c):
                pool.wait_ge(q_rc.sem, q_rc.at(i, 2 * c + 2))
                q3 = EQ[c].rearrange("p (h d) -> p h d", h=HA)
                pool.tensor_tensor(q3, q3, q_rcp[:, :].unsqueeze(2).to_broadcast([P, HA, DA]), ALU.mult)\
                    .then_inc(q_hat.sem, 1)

            def add_bias(j):
                pool.wait_ge(xr_in.sem, xr_in.at(j))
                pool.tensor_tensor(xr, xr, b_all[:, :].unsqueeze(1).to_broadcast([P, NC, D]), ALU.add)\
                    .then_inc(xb_ok.sem, 1)

            pool.wait_ge(b_ok.sem, 3)
            rsqrt_var(0, 0)
            split_h1(0, 0)

            qk = qkv_sb[:, :, 0:2 * D]

            def norms(j):
                pool.wait_ge(p_ev.sem, p_ev.at(j))
                if exists(n_red.at(j - 1)):
                    pool.wait_ge(n_red.sem, n_red.at(j - 1))
                pool.tensor_tensor(qk_sq[:, :, :], qk, qk, ALU.mult).then_inc(n_sq.sem, 1)

            def first_half(i, p):
                j = i - 1
                if there(j):
                    add_bias(j)
                if there(i):
                    q_hats(i, 0)
                    q_hats(i, 1)
                if there(i - 2):
                    norms(i - 2)
                if there(j):
                    rsqrt_var(1, j)
                if there(i):
                    q_hats(i, 2)
                if there(i + 1):
                    rsqrt_var(0, i + 1)
                if there(i):
                    q_hats(i, 3)
                if there(i + 1):
                    split_h1(i + 1, 1 - p)
                if there(j):
                    rsqrt_var(2, j)

            over_batches(pool, first_half, NB, 2)

            pool.wait_ge(qkv_st.sem, qkv_st.at(NB - 1))
            pool.wait_ge(x2_st.sem, x2_st.at(NB - 1))
            for g in range(2):
                pool.memset(k_pad[g].bitcast(F32), 0.0).then_inc(zeroed.sem, 1)
            pool.tensor_copy(sel4[:, :, :], sel4f[:, :, :]).then_inc(zeroed.sem, 1)

            def rope(i, p):
                if exists(pv.at(i - 2)):
                    pool.wait_ge(pv.sem, pv.at(i - 2))
                if exists(part.at(i - 1)):
                    pool.wait_ge(part.sem, part.at(i - 1))
                pool.wait_ge(qkv_in.sem, qkv_in.at(i))
                pool.tensor_tensor(qk_rot[:, :, :], qk, cos_t[:, :, :], ALU.mult).then_inc(roped.sem, 1)
                pool.tensor_tensor(rot[:, :, 0::2], qk[:, :, 1::2], sin_t[:, :, 0::2], ALU.mult).then_inc(roped.sem, 1)
                pool.tensor_tensor(rot[:, :, 1::2], qk[:, :, 0::2], sin_t[:, :, 1::2], ALU.mult).then_inc(roped.sem, 1)
                pool.tensor_copy(v32[p][:, :, :, 0:DB],
                                 qkv_sb[:, :, 2 * D:W3].rearrange("p c (h d) -> p c h d", h=HB)).then_inc(v_ok.sem, 1)
                pool.wait_ge(v_ok.sem, v_ok.at(i))
                pool.wait_ge(roped.sem, roped.at(i, 3))
                pool.tensor_tensor(qk_rot[:, :, :], qk_rot[:, :, :], rot[:, :, :], ALU.add).then_inc(roped.sem, 1)

            def split_parts(i, g):
                pool.wait_ge(roped.sem, roped.at(i))
                if exists(qT_ps.at(i, g - 1)):
                    pool.wait_ge(qT_ps.sem, qT_ps.at(i, g - 1))
                if exists(kT_ps.at(i, g - 1)):
                    pool.wait_ge(kT_ps.sem, kT_ps.at(i, g - 1))
                src = [qk_rot[:, :, t * D + 32 * g:t * D + 32 * g + 32].rearrange("p c (j d) -> p c j d", j=4)
                       for t in range(2)]
                dst = [parts[g % 2][:, t, :, :].rearrange("p c (j r d) -> p c j r d", j=4, r=4) for t in range(2)]
                for t, his in ((0, (0, 1)), (1, (0, 2))):
                    for r in his:
                        pool.tensor_tensor(dst[t][:, :, :, r, :], src[t],
                                           one[:, 0:1].unsqueeze(2).unsqueeze(3).to_broadcast([P, NC, 4, DB]),
                                           ALU.mult).then_inc(part.sem, 1)
                pool.wait_ge(part.sem, part.at(i, 8 * g + 4))
                for t, los in ((0, (2, 3)), (1, (1, 3))):
                    for r in los:
                        pool.tensor_tensor(dst[t][:, :, :, r, :], src[t], dst[t][:, :, :, 0, :].bitcast(F32),
                                           ALU.subtract).then_inc(part.sem, 1)

            rope(0, 0)
            split_parts(0, 0)

            def second_half(i, p):
                for g in range(1, NG):
                    if there(i):
                        split_parts(i, g)
                    if g == 2 and there(i - 1):
                        rsqrt_var(3, i - 1)
                if there(i + 1):
                    rope(i + 1, 1 - p)
                    split_parts(i + 1, 0)

            over_batches(pool, second_half, NB, 1)

        @block.scalar
        def _(act):
            def h1_copy(j, p):
                act.wait_ge(h1_T.sem, h1_T.at(j))
                act.activation(h1T[p], PS[:, 4, :], ACT.Copy).then_inc(h1_sb.sem, 1)

            def exp_q(i, c, guarded):
                if exists(c_mm.at(i - 1, c + 1)):
                    act.wait_ge(c_mm.sem, c_mm.at(i - 1, c + 1))
                if guarded:
                    act.wait_ge(q_mx.sem, q_mx.at(i, 2 * c + 2))
                    act.activation(EQ[c], q_sh, ACT.Exp).then_inc(q_exp.sem, 1)
                else:
                    act.wait_ge(q_mm.sem, q_mm.at(i, c + 1))
                    act.activation(EQ[c], PS[:, 0:2, :].rearrange("p a n -> p (a n)"), ACT.Exp).then_inc(q_exp.sem, 1)

            def exp_k(i, c):
                act.wait_ge(k_mm.sem, k_mm.at(i, c + 1))
                act.activation(EK[c], PS[:, 2:4, :].rearrange("p a n -> p (a n)"), ACT.Exp).then_inc(k_exp.sem, 1)

            def relu(f, j, bank):
                act.wait_ge(f["k"].sem, f["k"].at(j))
                act.activation(k_relu[:, :], PS[:, bank, :], ACT.Relu).then_inc(f["relu"].sem, 1)

            def gates(f, j, bank):
                act.wait_ge(f["r"].sem, f["r"].at(j))
                act.activation(gate[:, :, :].rearrange("p c d -> p (c d)"), PS[:, bank, :], ACT.Tanh, scale=0.5)\
                   .then_inc(f["gate"].sem, 1)

            def scale_mu(f, j, bank):
                act.wait_ge(f["hT"].sem, f["hT"].at(j))
                if exists(f["r"].at(j - 1)):
                    act.wait_ge(f["r"].sem, f["r"].at(j - 1))
                for n in range(2):
                    act.activation(mixed[n][:, :], PS[:, bank, :], ACT.Copy, scale=mu[:, n:n + 1])\
                       .then_inc(f["mu"].sem, 1)

            def t_copy(j):
                act.wait_ge(t_mm.sem, t_mm.at(j))
                act.activation(T_sb.rearrange("p a n -> p (a n)"), PS[:, 5:7, :].rearrange("p a n -> p (a n)"),
                               ACT.Copy).then_inc(t_ev.sem, 1)

            def p_copy(j, chunks):
                for c in chunks:
                    if c == 0:
                        if exists(qkv_st.at(j - 1)):
                            act.wait_ge(qkv_st.sem, qkv_st.at(j - 1))
                        if exists(n_sq.at(j - 1)):
                            act.wait_ge(n_sq.sem, n_sq.at(j - 1))
                    act.wait_ge(p_mm.sem, p_mm.at(j, c + 1))
                    act.activation(qkv_sb[:, c, :], PS[:, (4, 7)[c % 2], 0:W3], ACT.Copy).then_inc(p_ev.sem, 1)

            act.wait_ge(b_ok.sem, 3)
            h1_copy(0, 0)

            def first_half(guarded):
                def step(i, p):
                    j = i - 1
                    main = there(i)
                    if main:
                        exp_q(i, 0, guarded)
                        exp_k(i, 0)
                        exp_q(i, 1, guarded)
                    if there(j):
                        t_copy(j)
                    if there(i - 2):
                        p_copy(i - 2, (0, 1))
                    if main:
                        exp_k(i, 1)
                    if there(i - 2):
                        p_copy(i - 2, (2, 3))
                    if main:
                        exp_q(i, 2, guarded)
                        exp_k(i, 2)
                        exp_q(i, 3, guarded)
                        exp_k(i, 3)
                    if there(j):
                        scale_mu(ffn[0], j, 7)
                    if there(i + 1):
                        h1_copy(i + 1, 1 - p)
                    if there(j):
                        relu(ffn[0], j, 4)
                        gates(ffn[0], j, 7)
                over_batches(act, step, NB, 2)

            act.wait_ge(a_known.sem, a_known.at(0))
            with act.If(act.value_load(bounded_a[0:1, 0:1], min_val=0, max_val=1) == 1):
                first_half(False)
            with act.Else():
                first_half(True)

            act.wait_ge(qkv_st.sem, qkv_st.at(NB - 1))
            act.wait_ge(x2_st.sem, x2_st.at(NB - 1))

            def second_half(i, p):
                for s in range(HB):
                    if there(i):
                        g, h = s // 4, s % 4
                        for half in range(2):
                            if h == 0 and half == 0:
                                if exists(pv.at(i, 4 * (g - 1))):
                                    act.wait_ge(pv.sem, pv.at(i, 4 * (g - 1)))
                            act.wait_ge(s_mm.sem, s_mm.at(i, 2 * s + half + 1))
                            act.activation(probs[g % 2][:, h, 2 * half:2 * half + 2, :],
                                           PS[:, 2 * half:2 * half + 2, :], ACT.Exp).then_inc(s_exp.sem, 1)
                    if s == 12 and there(i - 1):
                        relu(ffn[1], i - 1, 6)
                        gates(ffn[1], i - 1, 7)

            over_batches(act, second_half, NB, 1)

        @block.vector
        def _(dve):
            raw_q, raw_k = wqkv_raw[:, 0:INNER], wqkv_raw[:, INNER:2 * INNER]
            dve.wait_ge(w_in.sem, 160)
            dve.tensor_scalar(raw_q, raw_q, SCALE_A, None, ALU.mult).then_inc(wsplit.sem, 1)
            dve.wait_ge(wsplit.sem, 1)
            dve.tensor_copy(wqk_hi, wqkv_raw[:, 0:2 * INNER]).then_inc(wsplit.sem, 1)
            dve.wait_ge(wsplit.sem, 2)
            dve.tensor_tensor(wqk_lo, wqkv_raw[:, 0:2 * INNER], wqk_hi.bitcast(F32), ALU.subtract).then_inc(wsplit.sem, 1)
            dve.wait_ge(const_ok.sem, 15)
            dve.tensor_copy(ones8[:, :], ones8f[:, :]).then_inc(b_ok.sem, 1)
            dve.wait_ge(wT.sem, 4)
            for n in range(2):
                dve.tensor_copy(WvT[:, 4 * n:4 * n + 4, :], PS[:, n, :].rearrange("p (a n) -> p a n", a=4))\
                   .then_inc(wT_sb.sem, 1)
            dve.tensor_copy(W7T[:, 0:4, :], PS[:, 2, :].rearrange("p (a n) -> p a n", a=4)).then_inc(wT_sb.sem, 1)
            dve.tensor_copy(W7T[:, 4:7, :], PS[:, 3, 0:3 * D].rearrange("p (a n) -> p a n", a=3)).then_inc(wT_sb.sem, 1)
            dve.wait_ge(wT.sem, 5)
            dve.tensor_copy(b_all[:, :], PS[:, 4, 0:D]).then_inc(b_ok.sem, 1)
            dve.wait_ge(wT_sb.sem, 4)
            w3 = W7T[:, 3:6, :].rearrange("p a n -> p (a n)")
            dve.tensor_copy(w3h[:, :], w3).then_inc(w3s.sem, 1)
            dve.wait_ge(w3s.sem, 1)
            dve.tensor_tensor(w3l[:, :], w3, w3h[:, :].bitcast(F32), ALU.subtract).then_inc(w3s.sem, 1)
            dve.wait_ge(c_in.sem, 64)
            dve.tensor_scalar(mu[:, 2:4], mu[:, 0:2], -1.0, 1.0, ALU.mult, ALU.add).then_inc(b_ok.sem, 1)
            dve.tensor_tensor(w_sq, wqkv_raw[:, 0:2 * INNER], wqkv_raw[:, 0:2 * INNER], ALU.mult).then_inc(w_sq_ok.sem, 1)
            dve.wait_ge(w_norm_ps.sem, 1)
            dve.reduce_max(w_norm[:, :], PS[0:1, 0:4, :].rearrange("p a n -> p (a n)"), AX_X).then_inc(a_known.sem, 1)
            dve.wait_ge(a_known.sem, 1)
            dve.tensor_scalar(bounded_a[:, :], w_norm[:, :], REACH ** 2 / D, None, ALU.is_lt).then_inc(a_known.sem, 1)

            def ln_stats(n, j, src):
                st, mom, ve, _ = stats[n]
                mean, d, both, m2, d2, m2e = (mom[:, t, :] for t in range(6))
                for c in range(NC):
                    dve.bn_stats(st[:, c, :], src[:, c, :]).then_inc(ln[n].sem, 1)
                dve.wait_ge(ln[n].sem, ln[n].at(j, NC))
                dve.tensor_tensor(both, st[:, :, 1], st[:, :, 4], ALU.add).then_inc(ln[n].sem, 1)
                dve.tensor_tensor(d, st[:, :, 1], st[:, :, 4], ALU.subtract).then_inc(ln[n].sem, 1)
                dve.tensor_tensor(m2, st[:, :, 2], st[:, :, 5], ALU.add).then_inc(ln[n].sem, 1)
                dve.wait_ge(ln[n].sem, ln[n].at(j, NC + 3))
                dve.tensor_scalar(mean, both, 0.5, None, ALU.mult).then_inc(ln[n].sem, 1)
                dve.scalar_tensor_tensor(d2, d, 0.25, d, ALU.mult, ALU.mult).then_inc(ln[n].sem, 1)
                dve.tensor_scalar(m2e, m2, 1.0 / D, EPS, ALU.mult, ALU.add).then_inc(ln[n].sem, 1)
                dve.wait_ge(ln[n].sem, ln[n].at(j, NC + 6))
                dve.tensor_tensor(ve[:, :], d2, m2e, ALU.add).then_inc(ln[n].sem, 1)

            def ln_norm(n, j, src, dst):
                _, mom, _, rs = stats[n]
                dve.wait_ge(ln[n].sem, ln[n].at(j, NC + 4))
                dve.wait_ge(rstd[n].sem, rstd[n].at(j))
                for c in range(NC):
                    dve.tensor_scalar(dst[:, c, :], src[:, c, :], mom[:, 0, c:c + 1], rs[:, c:c + 1],
                                      ALU.subtract, ALU.mult).then_inc(ln[n].sem, 1)

            def ln1(j):
                dve.wait_ge(xa_in.sem, xa_in.at(j))
                ln_stats(0, j, xa)
                if exists(h1_T.at(j - 1)):
                    dve.wait_ge(h1_T.sem, h1_T.at(j - 1))
                ln_norm(0, j, xa, h1)

            def k_maxima(j):
                for a in range(PAIRS):
                    dve.wait_ge(kx_mm.sem, kx_mm.at(j, a + 1))
                    dve.reduce_max(k_max[:, a:a + 1], PS[:, 5 + a % 2, :], AX_X).then_inc(kx_max.sem, 1)

            def k_shift(j):
                dve.wait_ge(kx_T.sem, kx_T.at(j))
                dve.tensor_tensor(k_neg[:, :, :], PS[0:8, 5, 0:P].unsqueeze(1).to_broadcast([8, PAIRS, P]),
                                  negmask[:, :, :], ALU.mult).then_inc(kx_ok.sem, 1)

            def q_shift(i, c):
                src = PS[:, 0:2, :].rearrange("p a (h d) -> p (a h) d", d=DA)
                dve.wait_ge(q_mm.sem, q_mm.at(i, c + 1))
                dve.reduce_max(q_max[:, :], src, AX_X).then_inc(q_mx.sem, 1)
                dve.wait_ge(q_mx.sem, q_mx.at(i, 2 * c + 1))
                if exists(q_exp.at(i, c)):
                    dve.wait_ge(q_exp.sem, q_exp.at(i, c))
                dve.tensor_tensor(q_sh.rearrange("p (h d) -> p h d", h=HA), src,
                                  q_max[:, :].unsqueeze(2).to_broadcast([P, HA, DA]), ALU.subtract)\
                   .then_inc(q_mx.sem, 1)

            def q_sums(i, c):
                if exists(q_rc.at(i, 2 * c)):
                    dve.wait_ge(q_rc.sem, q_rc.at(i, 2 * c))
                dve.wait_ge(q_exp.sem, q_exp.at(i, c + 1))
                dve.reduce_sum(q_sum[:, :], EQ[c].rearrange("p (h d) -> p h d", h=HA), AX_X).then_inc(q_rc.sem, 1)
                dve.wait_ge(q_rc.sem, q_rc.at(i, 2 * c + 1))
                if exists(q_hat.at(i, c)):
                    dve.wait_ge(q_hat.sem, q_hat.at(i, c))
                dve.reciprocal(q_rcp[:, :], q_sum[:, :]).then_inc(q_rc.sem, 1)

            def c_norm(i):
                src = PS[:, 5:7, :].rearrange("p a (b n) -> p (a b) n", n=P)
                dve.wait_ge(c_mm.sem, c_mm.at(i))
                for s in range(2):
                    lo, hi = DA * s, DA * s + DA
                    dve.reduce_sum(z_sum[lo:hi, :], src[lo:hi, :, lo:hi], AX_X).then_inc(c_ev.sem, 1)
                dve.wait_ge(c_ev.sem, c_ev.at(i, 2))
                dve.reciprocal(z_rcp[:, :], z_sum[:, :]).then_inc(c_ev.sem, 1)
                dve.wait_ge(c_ev.sem, c_ev.at(i, 3))
                for s in range(2):
                    lo, hi = DA * s, DA * s + DA
                    dve.tensor_tensor(ctx_bd[lo:hi, :, lo:hi], src[lo:hi, :, lo:hi],
                                      z_rcp[lo:hi, :].unsqueeze(2).to_broadcast([DA, PAIRS, DA]), ALU.mult)\
                       .then_inc(c_ev.sem, 1)

            def m_copy(j):
                dve.wait_ge(m_mm.sem, m_mm.at(j))
                dve.tensor_copy(M_sb[:, :], PS[:, 5, 0:D]).then_inc(m_ev.sem, 1)

            def add_x1(j):
                dve.wait_ge(xb_ok.sem, xb_ok.at(j))
                dve.wait_ge(y_mm.sem, y_mm.at(j))
                dve.tensor_tensor(x1[:, :, :], as_chunks(PS[:, 4, :]), xr, ALU.add).then_inc(x1_ok.sem, 1)
                dve.wait_ge(x1_ok.sem, x1_ok.at(j))
                ln_stats(1, j, x1)

            def mix(f, j, bank, scaled):
                if scaled:
                    dve.wait_ge(f["hT"].sem, f["hT"].at(j))
                    if exists(f["r"].at(j - 1)):
                        dve.wait_ge(f["r"].sem, f["r"].at(j - 1))
                    for n in range(2):
                        dve.tensor_scalar(mixed[n][:, :], PS[:, bank, :], mu[:, n:n + 1], None, ALU.mult)\
                           .then_inc(f["mix"].sem, 1)
                    dve.wait_ge(f["mix"].sem, f["mix"].at(j, 2))
                else:
                    dve.wait_ge(f["mu"].sem, f["mu"].at(j))
                for n in range(2):
                    dve.scalar_tensor_tensor(mixed[n][:, 1:N], PS[:, bank, 0:N - 1], mu[:, 2 + n:3 + n],
                                             mixed[n][:, 1:N], ALU.mult, ALU.add)\
                       .then_inc(f["mix"].sem, 1 if scaled else 2)

            def square(f, j, bank):
                dve.wait_ge(f["relu"].sem, f["relu"].at(j))
                if exists(f["v"].at(j - 1)):
                    dve.wait_ge(f["v"].sem, f["v"].at(j - 1))
                dve.tensor_tensor(k_act[:, :], PS[:, bank, :], k_relu[:, :], ALU.mult).then_inc(f["act"].sem, 1)

            def gate_v(f, j, bank, res, dst):
                dve.wait_ge(f["gate"].sem, f["gate"].at(j))
                dve.wait_ge(f["v"].sem, f["v"].at(j))
                dve.scalar_tensor_tensor(gated[:, :, :], gate[:, :, :], 1.0, as_chunks(PS[:, bank, :]),
                                         ALU.add, ALU.mult).then_inc(f["x"].sem, 1)
                dve.wait_ge(f["x"].sem, f["x"].at(j, 1))
                dve.scalar_tensor_tensor(dst[:, :, :], gated[:, :, :], 0.5, res[:, :, :], ALU.mult, ALU.add)\
                   .then_inc(f["x"].sem, 1)

            def split_h3(j):
                dve.wait_ge(h3_T.sem, h3_T.at(j))
                if exists(p_mm.at(j - 1)):
                    dve.wait_ge(p_mm.sem, p_mm.at(j - 1))
                dve.tensor_copy(h3h[:, :], PS[:, 7, :]).then_inc(h3_sp.sem, 1)
                dve.wait_ge(h3_sp.sem, h3_sp.at(j, 1))
                dve.tensor_tensor(h3l[:, :], PS[:, 7, :], h3h[:, :].bitcast(F32), ALU.subtract).then_inc(h3_sp.sem, 1)

            def end_ffn1(j):
                if exists(x2_st.at(j - 1)):
                    dve.wait_ge(x2_st.sem, x2_st.at(j - 1))
                gate_v(ffn[0], j, 4, x1, x2)
                dve.wait_ge(ffn[0]["x"].sem, ffn[0]["x"].at(j))
                ln_stats(2, j, x2)

            def norm_maxima(j):
                dve.wait_ge(n_sq.sem, n_sq.at(j))
                dve.reduce_sum(qk_norm[:, :, :], qk_sq[:, :, :].rearrange("p c (h d) -> p c h d", d=DB), AX_X)\
                   .then_inc(n_red.sem, 1)
                dve.wait_ge(n_red.sem, n_red.at(j))
                dve.tensor_tensor(norm_max[:, :, :], norm_max[:, :, :], qk_norm[:, :, :], ALU.max).then_inc(n_max.sem, 1)

            def first_half(guarded):
                def step(i, p):
                    j = i - 1
                    main = there(i)
                    if main and guarded:
                        q_shift(i, 0)
                    if there(i - 2):
                        ln_norm(2, i - 2, x2, h3)
                        split_h3(i - 2)
                    if main and guarded:
                        q_shift(i, 1)
                    if main:
                        q_sums(i, 0)
                    if there(j):
                        m_copy(j)
                    if main:
                        q_sums(i, 1)
                    if main and guarded:
                        q_shift(i, 2)
                    if there(j):
                        add_x1(j)
                    if main:
                        q_sums(i, 2)
                    if main and guarded:
                        q_shift(i, 3)
                    if there(j):
                        ln_norm(1, j, x1, hn)
                    if there(i + 1):
                        ln1(i + 1)
                    if main:
                        q_sums(i, 3)
                    if there(i - 2):
                        norm_maxima(i - 2)
                    if there(j):
                        mix(ffn[0], j, 7, False)
                        square(ffn[0], j, 4)
                    if main:
                        c_norm(i)
                    if there(j):
                        end_ffn1(j)
                    if guarded and there(i + 1):
                        k_maxima(i + 1)
                        k_shift(i + 1)
                if guarded:
                    k_maxima(0)
                    k_shift(0)
                over_batches(dve, step, NB, 2)

            ln1(0)
            dve.wait_ge(a_known.sem, a_known.at(0))
            with dve.If(dve.value_load(bounded_a[0:1, 0:1], min_val=0, max_val=1) == 1):
                first_half(False)
            with dve.Else():
                first_half(True)

            dve.wait_ge(n_max.sem, n_max.at(NB - 1))
            for t in range(2):
                dve.reduce_max(norm_col[:, t:t + 1], norm_max[:, :, HB * t:HB * t + HB], mybir.AxisListType.XY)\
                   .then_inc(b_known.sem, 1)
            dve.wait_ge(n_T.sem, n_T.at(0))
            dve.reduce_max(norm_two[:, 0:2], PS[0:1, 4, 0:2 * P].rearrange("p (t n) -> p t n", t=2), AX_X)\
               .then_inc(n_red.sem, 1)
            dve.wait_ge(n_red.sem, NB + 1)
            dve.tensor_tensor(norm_two[:, 2:3], norm_two[:, 0:1], norm_two[:, 1:2], ALU.mult).then_inc(b_known.sem, 1)
            dve.wait_ge(b_known.sem, b_known.at(0, 3))
            dve.tensor_scalar(bounded_b[:, :], norm_two[:, 2:3], REACH ** 2 * DB, None, ALU.is_lt).then_inc(b_known.sem, 1)

            dve.wait_ge(qkv_st.sem, qkv_st.at(NB - 1))
            dve.wait_ge(x2_st.sem, x2_st.at(NB - 1))

            def k_copy(i, g, guarded):
                dve.wait_ge(kT_ps.sem, kT_ps.at(i, g + 1))
                if exists(k_padded[g % 2].at(i, 64 * (g // 2))):
                    dve.wait_ge(k_padded[g % 2].sem, k_padded[g % 2].at(i, 64 * (g // 2)))
                if guarded:
                    if exists(mx_mm.at(i, 8 * (g - 1))):
                        dve.wait_ge(mx_mm.sem, mx_mm.at(i, 8 * (g - 1)))
                if exists(s_mm.at(i, 8 * (g - 1))):
                    dve.wait_ge(s_mm.sem, s_mm.at(i, 8 * (g - 1)))
                dve.tensor_copy(k_st[g % 2][:, :], PS[:, 7, :]).then_inc(kT_sb.sem, 1)

            def q_copy(i, g, bank):
                dve.wait_ge(qT_ps.sem, qT_ps.at(i, g + 1))
                if exists(s_mm.at(i, 8 * (g - 1))):
                    dve.wait_ge(s_mm.sem, s_mm.at(i, 8 * (g - 1)))
                dve.tensor_copy(q_st[g % 2][:, :], PS[:, bank, :]).then_inc(qT_sb.sem, 1)

            def maxima(i, g):
                for m in range(8):
                    h, half = m // 2, m % 2
                    dve.wait_ge(mx_mm.sem, mx_mm.at(i, 8 * g + m + 1))
                    dve.reduce_max(row_max[:, 2 * half:2 * half + 2, h], PS[:, 2 * half:2 * half + 2, :], AX_X)\
                       .then_inc(mx_ok.sem, 1)
                dve.wait_ge(mx_T.sem, mx_T.at(i, g + 1))
                dve.tensor_scalar(neg_c[:, :], PS[0:4, 0, :], -1.0, None, ALU.mult).then_inc(mx_neg.sem, 1)

            def pv_copy(i, g):
                dve.wait_ge(pv.sem, pv.at(i, 4 * g + 4))
                if exists(u_T.at(i, g - 1)):
                    dve.wait_ge(u_T.sem, u_T.at(i, g - 1))
                dve.tensor_copy(U[g % 2][:, :], PS[:, 4 + g % 2, :]).then_inc(pv_sb.sem, 1)

            def normalise(i, g, bank):
                src = PS[:, bank, :].rearrange("p (c j r) -> p c j r", c=NC, j=4)
                dve.wait_ge(u_T.sem, u_T.at(i, g + 1))
                dve.reciprocal(den_rcp[:, :, :], src[:, :, :, DB]).then_inc(u_norm.sem, 1)
                dve.wait_ge(u_norm.sem, u_norm.at(i, 2 * g + 1))
                dve.tensor_tensor(c_tok[:, :, 32 * g:32 * g + 32].rearrange("p c (j d) -> p c j d", j=4),
                                  src[:, :, :, 0:DB], den_rcp[:, :, :].unsqueeze(3).to_broadcast([P, NC, 4, DB]),
                                  ALU.mult).then_inc(u_norm.sem, 1)

            def add_x3(j):
                dve.wait_ge(x2_in.sem, x2_in.at(j))
                dve.wait_ge(o_mm.sem, o_mm.at(j))
                dve.tensor_tensor(x1[:, :, :], as_chunks(PS[:, 6, :]), x2[:, :, :], ALU.add).then_inc(x3_ok.sem, 1)
                dve.wait_ge(x3_ok.sem, x3_ok.at(j))
                ln_stats(3, j, x1)

            def second_half(guarded):
                def step(i, p):
                    j = i - 1
                    main, side = there(i), there(j)
                    if main:
                        if guarded:
                            maxima(i, 0)
                        k_copy(i, 1, guarded)
                    if side:
                        normalise(j, 2, 6)
                    if main:
                        q_copy(i, 1, 6)
                    if side:
                        pv_copy(j, 3)
                    if main:
                        if guarded:
                            maxima(i, 1)
                        k_copy(i, 2, guarded)
                    if side:
                        normalise(j, 3, 6)
                    if main:
                        q_copy(i, 2, 6)
                    if side:
                        dve.wait_ge(ct_ps.sem, ct_ps.at(j))
                        dve.tensor_copy(cT[:, :], PS[:, 7, :]).then_inc(ct_sb.sem, 1)
                    if main:
                        pv_copy(i, 0)
                    if side:
                        add_x3(j)
                    if main:
                        if guarded:
                            maxima(i, 2)
                        k_copy(i, 3, guarded)
                        normalise(i, 0, 6)
                    if side:
                        ln_norm(3, j, x1, hn)
                    if main:
                        q_copy(i, 3, 6)
                    if side:
                        mix(ffn[1], j, 7, True)
                    if main:
                        pv_copy(i, 1)
                        if guarded:
                            maxima(i, 3)
                    if side:
                        square(ffn[1], j, 6)
                    if there(i + 1):
                        k_copy(i + 1, 0, guarded)
                    if side:
                        if exists(out_st.at(j - 1)):
                            dve.wait_ge(out_st.sem, out_st.at(j - 1))
                        gate_v(ffn[1], j, 6, x1, gated)
                    if there(i + 1):
                        q_copy(i + 1, 0, 7)
                    if main:
                        normalise(i, 1, 6)
                        pv_copy(i, 2)
                over_batches(dve, step, NB, 1)

            k_copy(0, 0, False)
            q_copy(0, 0, 6)
            dve.wait_ge(b_known.sem, b_known.at(0))
            with dve.If(dve.value_load(bounded_b[0:1, 0:1], min_val=0, max_val=1) == 1):
                second_half(False)
            with dve.Else():
                second_half(True)

        @block.tensor
        def _(pe):
            pe.wait_ge(w_in.sem, 160)
            pe.wait_ge(id_ok.sem, 1)
            pe.wait_ge(const_ok.sem, 15)
            for n in range(2):
                for a in range(4):
                    last_mm = pe.transpose(PS[:, n, a * P:(a + 1) * P],
                                           wqkv_raw[:, 2 * INNER + (4 * n + a) * P:2 * INNER + (4 * n + a + 1) * P],
                                           ident[:, :])
                last_mm.then_inc(wT.sem, 1)
            for n, some in ((2, range(0, 4)), (3, range(4, 7))):
                for a, w in enumerate(some):
                    last_mm = pe.transpose(PS[:, n, a * P:(a + 1) * P], raw7[:, w, :], ident[:, :])
                last_mm.then_inc(wT.sem, 1)
            pe.matmul(PS[:, 4, 0:D], ones_row[:, :], b_row[:, :], start=True, stop=True).then_inc(wT.sem, 1)
            pe.wait_ge(wsplit.sem, 3)
            pe.wait_ge(wT_sb.sem, 4)
            pe.wait_ge(w3s.sem, 2)
            pe.wait_ge(b_ok.sem, 3)
            pe.wait_ge(w_sq_ok.sem, 1)
            for b in range(4):
                mm = pe.matmul(PS[0:1, b, :], ones_col[:, :], w_sq[:, b * 512:b * 512 + 512], start=True, stop=True)
            mm.then_inc(w_norm_ps.sem, 1)

            def four_transposes(src, bank):
                for c in range(NC):
                    mm = pe.transpose(PS[:, bank, c * P:(c + 1) * P], src(c), ident[:, :])
                return mm

            def halves(dst, w, h, stop=True):
                pe.matmul(dst, w[0], h[0], start=True, stop=False)
                pe.matmul(dst, w[0], h[1], start=False, stop=False)
                return pe.matmul(dst, w[1], h[0], start=False, stop=stop)

            def head_T(n):
                if exists(ffn[0]["x"].at(n - 3, 1)):
                    pe.wait_ge(ffn[0]["x"].sem, ffn[0]["x"].at(n - 3, 1))
                if exists(x1_ok.at(n - 2)):
                    pe.wait_ge(x1_ok.sem, x1_ok.at(n - 2))
                pe.wait_ge(ln[0].sem, ln[0].at(n))
                four_transposes(lambda c: h1[:, c, :], 4).then_inc(h1_T.sem, 1)

            def head_kmax(n):
                pe.wait_ge(h1_sp.sem, h1_sp.at(n))
                if exists(c_ev.at(n - 1)):
                    pe.wait_ge(c_ev.sem, c_ev.at(n - 1))
                for a in range(PAIRS):
                    if a >= 2:
                        pe.wait_ge(kx_max.sem, kx_max.at(n, a - 1))
                    pe.matmul(PS[:, 5 + a % 2, :], wqk_hi[:, INNER + a * P:INNER + (a + 1) * P], h1h[:, :],
                              start=True, stop=True).then_inc(kx_mm.sem, 1)
                pe.wait_ge(kx_max.sem, kx_max.at(n))
                pe.transpose(PS[0:8, 5, 0:P], k_max[:, :], ident[:, :]).then_inc(kx_T.sem, 1)

            def proj_q(i, c, guarded):
                if c == 0:
                    pe.wait_ge(h1_sp.sem, h1_sp.at(i))
                if guarded:
                    if exists(q_mx.at(i, 2 * c)):
                        pe.wait_ge(q_mx.sem, q_mx.at(i, 2 * c))
                else:
                    if exists(q_exp.at(i, c)):
                        pe.wait_ge(q_exp.sem, q_exp.at(i, c))
                for b in range(2):
                    cols = slice(b * 512, b * 512 + 512)
                    tok = slice(c * P, c * P + P)
                    mm = halves(PS[:, b, :], (h1h[:, tok], h1l[:, tok]), (wqk_hi[:, cols], wqk_lo[:, cols]))
                mm.then_inc(q_mm.sem, 1)

            def proj_k(i, c, guarded):
                if exists(k_exp.at(i, c)):
                    pe.wait_ge(k_exp.sem, k_exp.at(i, c))
                if guarded and c == 0:
                    pe.wait_ge(kx_ok.sem, kx_ok.at(i))
                for b in range(2):
                    cols = slice(INNER + b * 512, INNER + b * 512 + 512)
                    tok = slice(c * P, c * P + P)
                    mm = halves(PS[:, 2 + b, :], (h1h[:, tok], h1l[:, tok]), (wqk_hi[:, cols], wqk_lo[:, cols]),
                                stop=not guarded)
                    if guarded:
                        mm = pe.matmul(PS[:, 2 + b, :], ones8[:, :],
                                       k_neg[:, 4 * b:4 * b + 4, :].rearrange("p a n -> p (a n)"),
                                       start=False, stop=True)
                mm.then_inc(k_mm.sem, 1)

            def context(i, c):
                if c == 0:
                    if exists(t_ev.at(i - 1)):
                        pe.wait_ge(t_ev.sem, t_ev.at(i - 1))
                    if exists(m_ev.at(i - 1)):
                        pe.wait_ge(m_ev.sem, m_ev.at(i - 1))
                pe.wait_ge(q_hat.sem, q_hat.at(i, c + 1))
                pe.wait_ge(k_exp.sem, k_exp.at(i, c + 1))
                for a in range(PAIRS):
                    cols = slice(a * P, a * P + P)
                    mm = pe.matmul(PS[:, 5 + a // 4, (a % 4) * P:(a % 4) * P + P], EK[c][:, cols], EQ[c][:, cols],
                                   start=(c == 0 and a % 4 == 0), stop=(c == NC - 1), skip_group_check=True)
                mm.then_inc(c_mm.sem, 1)

            def ctx_wout(j):
                pe.wait_ge(c_ev.sem, c_ev.at(j))
                for a in range(PAIRS):
                    mm = pe.matmul(PS[:, 5 + a // 4, (a % 4) * P:(a % 4) * P + P], ctx_bd[:, a, :], wout_sb[:, a, :],
                                   start=True, stop=True)
                mm.then_inc(t_mm.sem, 1)

            def wv_ctx_wout(j):
                pe.wait_ge(t_ev.sem, t_ev.at(j))
                for a in range(PAIRS):
                    mm = pe.matmul(PS[:, 5, 0:D], WvT[:, a, :], T_sb[:, a, :], start=(a == 0), stop=(a == PAIRS - 1))
                mm.then_inc(m_mm.sem, 1)

            def attn_out(j, p):
                pe.wait_ge(m_ev.sem, m_ev.at(j))
                if exists(p_ev.at(j - 1, 3)):
                    pe.wait_ge(p_ev.sem, p_ev.at(j - 1, 3))
                for c in range(NC):
                    mm = pe.matmul(PS[:, 4, c * D:(c + 1) * D], h1T[p][:, c * P:(c + 1) * P], M_sb[:, :],
                                   start=True, stop=True)
                mm.then_inc(y_mm.sem, 1)

            def ffn_T(f, n, j, bank):
                pe.wait_ge(ln[n].sem, ln[n].at(j))
                four_transposes(lambda c: hn[:, c, :], bank).then_inc(f["hT"].sem, 1)

            def ffn_kr(f, j, bank_k, bank_r):
                pe.wait_ge(f["mix"].sem, f["mix"].at(j))
                pe.matmul(PS[:, bank_k, :], WkT, mixed[1][:, :], start=True, stop=True).then_inc(f["k"].sem, 1)
                for c in range(NC):
                    mm = pe.matmul(PS[:, bank_r, c * D:(c + 1) * D], mixed[0][:, c * P:(c + 1) * P], WrT,
                                   start=True, stop=True)
                mm.then_inc(f["r"].sem, 1)

            def ffn_v(f, j, bank):
                pe.wait_ge(f["act"].sem, f["act"].at(j))
                for c in range(NC):
                    mm = pe.matmul(PS[:, bank, c * D:(c + 1) * D], k_act[:, c * P:(c + 1) * P], WvfT,
                                   start=True, stop=True)
                mm.then_inc(f["v"].sem, 1)

            def h3_transposes(j):
                pe.wait_ge(ln[2].sem, ln[2].at(j))
                pe.wait_ge(ffn[0]["gate"].sem, ffn[0]["gate"].at(j))
                four_transposes(lambda c: h3[:, c, :], 7).then_inc(h3_T.sem, 1)

            def proj_b(j, chunks):
                for c in chunks:
                    if c == 0:
                        pe.wait_ge(h3_sp.sem, h3_sp.at(j))
                        pe.wait_ge(ffn[0]["x"].sem, ffn[0]["x"].at(j, 1))
                    if c >= 2:
                        pe.wait_ge(p_ev.sem, p_ev.at(j, c - 1))
                    tok = slice(c * P, c * P + P)
                    halves(PS[:, (4, 7)[c % 2], 0:W3], (h3h[:, tok], h3l[:, tok]), (w3h[:, :], w3l[:, :]))\
                        .then_inc(p_mm.sem, 1)

            def first_half(guarded):
                def step(i, p):
                    j = i - 1
                    main, side, late = there(i), there(j), there(i - 2)
                    if main:
                        proj_q(i, 0, guarded)
                        proj_k(i, 0, guarded)
                    if late:
                        h3_transposes(i - 2)
                    if main:
                        proj_q(i, 1, guarded)
                    if side:
                        ctx_wout(j)
                    if late:
                        proj_b(i - 2, (0, 1))
                    if main:
                        proj_k(i, 1, guarded)
                    if late:
                        proj_b(i - 2, (2, 3))
                    if side:
                        wv_ctx_wout(j)
                    if main:
                        proj_q(i, 2, guarded)
                    if side:
                        attn_out(j, 1 - p)
                    if main:
                        proj_k(i, 2, guarded)
                        context(i, 0)
                        proj_q(i, 3, guarded)
                        proj_k(i, 3, guarded)
                    if side:
                        if exists(p_ev.at(j - 1)):
                            pe.wait_ge(p_ev.sem, p_ev.at(j - 1))
                        ffn_T(ffn[0], 1, j, 7)
                    if main:
                        context(i, 1)
                    if there(i + 1):
                        head_T(i + 1)
                    if main:
                        context(i, 2)
                    if side:
                        if there(i + 1):
                            pe.wait_ge(h1_sb.sem, h1_sb.at(i + 1))
                        pe.wait_ge(x1_ok.sem, x1_ok.at(j))
                        ffn_kr(ffn[0], j, 4, 7)
                    if main:
                        context(i, 3)
                    if side:
                        ffn_v(ffn[0], j, 4)
                    if guarded and there(i + 1):
                        head_kmax(i + 1)
                if guarded:
                    head_kmax(0)
                over_batches(pe, step, NB, 2)

            pe.wait_ge(a_known.sem, a_known.at(0))
            head_T(0)
            with pe.If(pe.value_load(bounded_a[0:1, 0:1], min_val=0, max_val=1) == 1):
                first_half(False)
            with pe.Else():
                first_half(True)

            pe.wait_ge(qkv_st.sem, qkv_st.at(NB - 1))
            pe.wait_ge(x2_st.sem, x2_st.at(NB - 1))
            pe.wait_ge(zeroed.sem, zeroed.at(0))
            pe.wait_ge(b_known.sem, b_known.at(0, 2))
            for t in range(2):
                mm = pe.transpose(PS[0:1, 4, t * P:t * P + P], norm_col[:, t:t + 1], ident[:, :])
            mm.then_inc(n_T.sem, 1)

            def parts_T(i, g, t, bank):
                pe.wait_ge(part.sem, part.at(i, 8 * g + 8))
                mm = four_transposes(lambda c: parts[g % 2][:, t, c, :].bitcast(F32), bank)
                mm.then_inc((qT_ps, kT_ps)[t].sem, 1)

            def maxima(i, g):
                if exists(s_exp.at(i, 8 * g)):
                    pe.wait_ge(s_exp.sem, s_exp.at(i, 8 * g))
                pe.wait_ge(qT_sb.sem, qT_sb.at(i, g + 1))
                pe.wait_ge(kT_sb.sem, kT_sb.at(i, g + 1))
                for m in range(8):
                    h, half = m // 2, m % 2
                    if m >= 2:
                        pe.wait_ge(mx_ok.sem, mx_ok.at(i, 8 * g + m - 1))
                    rows = slice(32 * h, 32 * h + 32)
                    for t in range(2):
                        c = 2 * half + t
                        mm = pe.matmul(PS[:, c, :], q_st[g % 2][rows, c * P:(c + 1) * P], k_st[g % 2][rows, :],
                                       start=True, stop=True)
                    mm.then_inc(mx_mm.sem, 1)
                pe.wait_ge(mx_ok.sem, mx_ok.at(i, 8 * g + 8))
                for c in range(NC):
                    mm = pe.transpose(PS[0:4, 0, c * P:(c + 1) * P], row_max[:, c, :], ident[:, :])
                mm.then_inc(mx_T.sem, 1)

            def scores(i, s, guarded):
                g, h = s // 4, s % 4
                if h == 0:
                    pe.wait_ge(k_padded[g % 2].sem, k_padded[g % 2].at(i, 64 * (g // 2) + 64))
                    pe.wait_ge(qT_sb.sem, qT_sb.at(i, g + 1))
                    if guarded:
                        pe.wait_ge(mx_neg.sem, mx_neg.at(i, g + 1))
                for half in range(2):
                    if exists(s_exp.at(i, 2 * s + half - 1)):
                        pe.wait_ge(s_exp.sem, s_exp.at(i, 2 * s + half - 1))
                    for t in range(2):
                        kc = 2 * half + t
                        mm = pe.matmul(PS[:, kc, :], k_pad[g % 2][:, h, kc * P:(kc + 1) * P], q_st[g % 2][:, :],
                                       start=True, stop=not guarded)
                        if guarded:
                            mm = pe.matmul(PS[:, kc, :], sel4[:, h, :], neg_c[:, :], start=False, stop=True)
                    mm.then_inc(s_mm.sem, 1)

            def weigh_values(i, g, kc, p):
                if kc == 0:
                    if exists(pv_sb.at(i, g - 1)):
                        pe.wait_ge(pv_sb.sem, pv_sb.at(i, g - 1))
                    pe.wait_ge(v_ok.sem, v_ok.at(i))
                pe.wait_ge(s_exp.sem, s_exp.at(i, 8 * g + 7 + kc // 2))
                for h in range(4):
                    mm = pe.matmul(PS[32 * h:32 * h + 32, 4 + g % 2, :], v32[p][:, kc, 4 * g + h, :],
                                   probs[g % 2][:, h, kc, :], start=(kc == 0), stop=(kc == NC - 1),
                                   tile_position=(0, 32 * h), skip_group_check=True)
                mm.then_inc(pv.sem, 1)

            def u_transposes(i, g, bank):
                pe.wait_ge(pv_sb.sem, pv_sb.at(i, g + 1))
                four_transposes(lambda c: U[g % 2][:, c * P:(c + 1) * P], bank).then_inc(u_T.sem, 1)

            parts_T(0, 0, 1, 7)
            parts_T(0, 0, 0, 6)

            def second_step(i, p, guarded):
                j = i - 1
                f = ffn[1]
                main, side = there(i), there(j)
                for s in range(HB):
                    g = s // 4
                    if main:
                        if guarded and s % 4 == 0:
                            maxima(i, g)
                        scores(i, s, guarded)
                    if main and g >= 1:
                        weigh_values(i, g - 1, s % 4, p)
                    if side and g == 0:
                        weigh_values(j, NG - 1, s % 4, 1 - p)
                    if s == 0:
                        if main:
                            pe.wait_ge(qT_sb.sem, qT_sb.at(i, 1))
                            parts_T(i, 1, 1, 7)
                        if side:
                            pe.wait_ge(u_norm.sem, u_norm.at(j, 4))
                            u_transposes(j, 2, 6)
                    if s == 1 and main:
                        if exists(u_norm.at(j, 6)):
                            pe.wait_ge(u_norm.sem, u_norm.at(j, 6))
                        pe.wait_ge(qT_sb.sem, qT_sb.at(i, 1))
                        parts_T(i, 1, 0, 6)
                    if s == 4:
                        if main:
                            pe.wait_ge(kT_sb.sem, kT_sb.at(i, 2))
                            parts_T(i, 2, 1, 7)
                            pe.wait_ge(qT_sb.sem, qT_sb.at(i, 2))
                        if side:
                            u_transposes(j, 3, 6)
                    if s == 5 and main:
                        if exists(u_norm.at(j)):
                            pe.wait_ge(u_norm.sem, u_norm.at(j))
                        pe.wait_ge(qT_sb.sem, qT_sb.at(i, 2))
                        parts_T(i, 2, 0, 6)
                    if s == 6 and side:
                        if main:
                            pe.wait_ge(kT_sb.sem, kT_sb.at(i, 3))
                        pe.wait_ge(u_norm.sem, u_norm.at(j))
                        four_transposes(lambda c: c_tok[:, c, :], 7).then_inc(ct_ps.sem, 1)
                    if s == 7 and side:
                        if main:
                            pe.wait_ge(qT_sb.sem, qT_sb.at(i, 3))
                        pe.wait_ge(ct_sb.sem, ct_sb.at(j))
                        for c in range(NC):
                            mm = pe.matmul(PS[:, 6, c * D:(c + 1) * D], cT[:, c * P:(c + 1) * P], WOT,
                                           start=True, stop=True)
                        mm.then_inc(o_mm.sem, 1)
                    if s == 8 and main:
                        if exists(ct_sb.at(j)):
                            pe.wait_ge(ct_sb.sem, ct_sb.at(j))
                        pe.wait_ge(kT_sb.sem, kT_sb.at(i, 3))
                        parts_T(i, 3, 1, 7)
                        if exists(x3_ok.at(j)):
                            pe.wait_ge(x3_ok.sem, x3_ok.at(j))
                        pe.wait_ge(qT_sb.sem, qT_sb.at(i, 3))
                        u_transposes(i, 0, 6)
                    if s == 9 and main:
                        pe.wait_ge(u_norm.sem, u_norm.at(i, 2))
                        parts_T(i, 3, 0, 6)
                    if s == 10 and side:
                        if main:
                            pe.wait_ge(kT_sb.sem, kT_sb.at(i, 4))
                        ffn_T(f, 3, j, 7)
                    if s == 11 and side:
                        if main:
                            pe.wait_ge(qT_sb.sem, qT_sb.at(i, 4))
                        ffn_kr(f, j, 6, 7)
                    if s == 13:
                        if there(i + 1):
                            if exists(f["gate"].at(j)):
                                pe.wait_ge(f["gate"].sem, f["gate"].at(j))
                            pe.wait_ge(kT_sb.sem, kT_sb.at(i, 4))
                            parts_T(i + 1, 0, 1, 7)
                        if side:
                            ffn_v(f, j, 6)
                    if s == 14 and there(i + 1):
                        pe.wait_ge(kT_sb.sem, kT_sb.at(i + 1, 1))
                        parts_T(i + 1, 0, 0, 7)
                    if s == 15 and main:
                        if exists(f["x"].at(j)):
                            pe.wait_ge(f["x"].sem, f["x"].at(j))
                        pe.wait_ge(qT_sb.sem, qT_sb.at(i, 4))
                        u_transposes(i, 1, 6)

            pe.wait_ge(b_known.sem, b_known.at(0))
            with pe.If(pe.value_load(bounded_b[0:1, 0:1], min_val=0, max_val=1) == 1):
                over_batches(pe, lambda i, p: second_step(i, p, False), NB, 1)
            with pe.Else():
                over_batches(pe, lambda i, p: second_step(i, p, True), NB, 1)


_PRE = "L0_"
_INS = ["attn_a_x", "attn_a_w_qkv", "attn_a_w_out", "attn_a_b_out", "attn_b_W_Q", "attn_b_W_K", "attn_b_W_V",
        "attn_b_W_O", "ffn_W_r", "ffn_W_k", "ffn_W_v", "ffn_mu_r", "ffn_mu_k"]


def rope_tables(n, d, heads, theta=10000.0):
    inv = 1.0 / theta ** (np.arange(0, d, 2, dtype=np.float32) / np.float32(d))
    angle = np.outer(np.arange(n, dtype=np.float32), inv.astype(np.float32)).astype(np.float32)
    cos, sin = np.repeat(np.cos(angle), 2, axis=-1), np.repeat(np.sin(angle), 2, axis=-1)
    sin[:, 0::2] *= -1.0

    def lay(t):
        both = np.concatenate([np.tile(t / np.sqrt(d), (1, heads)), np.tile(t, (1, heads))], axis=1)
        return np.ascontiguousarray(both.reshape(n // P, P, -1).transpose(1, 0, 2)).astype(np.float32)

    return lay(cos), lay(sin)


def kernel(**inputs):
    import numpy as _np
    import concourse.bacc as _bacc
    from concourse.bass_utils import run_bass_kernel_spmd as _run

    nc = _bacc.Bacc("TRN2", target_bir_lowering=False, num_devices=1)
    arrays, args = {}, []
    for name in _INS:
        a = _np.ascontiguousarray(inputs[_PRE + name])
        arrays[f"in_{name}"] = a
        args.append(nc.dram_tensor(f"in_{name}", a.shape, mybir.dt.from_np(a.dtype), kind="ExternalInput").ap())
    shape = tuple(inputs["L0_attn_a_x"].shape)
    for name, a in zip(("cos", "sin"), rope_tables(shape[1], 8, 16)):
        arrays[f"rope_{name}"] = a
        args.append(nc.dram_tensor(f"rope_{name}", a.shape, F32, kind="ExternalInput").ap())
    out = nc.dram_tensor("out_0", shape, F32, kind="ExternalOutput").ap()
    hybrid_block(nc, *args, out)
    r = _run(nc, [arrays], core_ids=[0])
    return r.results[0]["out_0"]
```

```python
from contextlib import ExitStack

import numpy as np

import concourse.bass as bass
from concourse import mybir

F32 = mybir.dt.float32
F32R = mybir.dt.float32r
I32 = mybir.dt.int32
ALU = mybir.AluOpType
ACT = mybir.ActivationFunctionType
AX_X = mybir.AxisListType.X

P = 128
EPS = 1e-5


class Signal:

    def __init__(self, ctx, nc, name, per):
        self.sem = ctx.enter_context(nc.semaphore(name))
        self.per = per

    def at(self, batch, count=None):
        return batch * self.per + (self.per if count is None else count)


def exists(value):
    return not isinstance(value, int) or value > 0


def over_batches(eng, step, n, tail, last=1):
    for b in range(3):
        step(b, b % 2)
    with eng.Fori(3, n - last - 1, 2) as i:
        step(i, 1)
        step(i + 1, 0)
    for b in range(n - last, n + tail):
        step(b, b % 2)


def hybrid_block(nc, x, w_qkv, w_out, b_out, W_Q, W_K, W_V, W_O, W_r, W_k, W_v, mu_r, mu_k,
                 rope_cos, rope_sin, out):
    NB, N, D = x.shape
    NC = N // P
    INNER = w_out.shape[0]
    DA = 64
    HA = INNER // DA
    PAIRS = INNER // P
    HB = 16
    DB = D // HB
    NG = HB // 4
    W3 = 3 * D
    assert D == P and NC == 4 and PAIRS == 8 and DB == 8 and NB % 2 == 0 and NB >= 8
    SCALE_A = DA ** -0.5
    REACH = 40.0

    x2_dram = nc.dram_tensor("x2_scratch", [NB, P, NC * D], F32, kind="Internal").ap()
    qkv_dram = nc.dram_tensor("qkv_scratch", [NB, P, NC * W3], F32, kind="Internal").ap()

    x_view = x.rearrange("b (c p) d -> b p c d", p=P)
    out_view = out.rearrange("b (c p) d -> b p c d", p=P)

    with ExitStack() as ctx:
        def sb(name, shape, dt=F32):
            return ctx.enter_context(nc.sbuf_tensor(name, shape, dt))

        def sig(name, per=1):
            return Signal(ctx, nc, name, per)

        work = sb("work", [P, 16384])
        work_r = sb("work_r", [P, 4096], F32R)
        taken = [0]

        def carve(cols):
            at = taken[0]
            taken[0] += cols
            assert taken[0] <= 16384
            return work[:, at:at + cols]

        E_all = carve(NC * 2 * INNER)
        E_v = E_all.rearrange("p (c n) -> p c n", c=NC)
        EQ = [E_v[:, c, 0:INNER] for c in range(NC)]
        EK = [E_v[:, c, INNER:2 * INNER] for c in range(NC)]
        wqkv_raw = E_all[:, 0:3 * INNER]
        ctx_bd = carve(INNER).rearrange("p (a n) -> p a n", a=PAIRS)
        T_sb = carve(INNER).rearrange("p (a n) -> p a n", a=PAIRS)
        q_sh = carve(INNER)
        WvT = carve(INNER).rearrange("p (a n) -> p a n", a=PAIRS)
        wout_sb = carve(INNER).rearrange("p (a n) -> p a n", a=PAIRS)
        h1T = [carve(N) for _ in range(2)]
        xa = carve(N).rearrange("p (c d) -> p c d", c=NC)
        h1 = carve(N).rearrange("p (c d) -> p c d", c=NC)
        xr = carve(N).rearrange("p (c d) -> p c d", c=NC)
        h3 = carve(N).rearrange("p (c d) -> p c d", c=NC)
        wqk_hi, wqk_lo = work_r[:, 0:2 * INNER], work_r[:, 2 * INNER:4 * INNER]
        probs = [work[:, g * 8192:(g + 1) * 8192].rearrange("p (j k n) -> p j k n", j=4, k=NC)
                 for g in range(2)]
        k_pad = [work_r[:, g * 2048:(g + 1) * 2048].rearrange("p (j n) -> p j n", j=4)
                 for g in range(2)]

        ident = sb("ident", [P, P])
        qkv_back = sb("qkv_back", [P, NC * W3])
        raw7 = qkv_back[:, 0:7 * D].rearrange("p (n d) -> p n d", n=7)
        W7T = sb("W7T", [P, 7, D])
        WrT, WkT, WvfT, WOT = (W7T[:, n, :] for n in (0, 1, 2, 6))
        mu = sb("mu", [P, 4])
        b_row = sb("b_row", [1, D])
        ones_row = sb("ones_row", [1, P])
        b_all = sb("b_all", [P, D])
        one = sb("one", [P, 1])
        half_neg = sb("half_neg", [P, NC])
        cos_t = sb("cos_t", [P, NC, 2 * D])
        sin_t = sb("sin_t", [P, NC, 2 * D])

        h1h, h1l = sb("h1h", [P, N], F32R), sb("h1l", [P, N], F32R)
        h3h, h3l = sb("h3h", [P, N], F32R), sb("h3l", [P, N], F32R)
        w3h, w3l = sb("w3h", [P, W3], F32R), sb("w3l", [P, W3], F32R)
        ones8f = sb("ones8f", [8, P])
        ones8 = sb("ones8", [8, P], F32R)
        mask_cos = sb("mask_cos", [P, PAIRS * P])
        negmask = mask_cos[0:8, :].rearrange("p (a n) -> p a n", a=PAIRS)
        qk_cos = mask_cos[:, :].rearrange("p (c d) -> p c d", c=NC)
        k_neg = sb("k_neg", [8, PAIRS, P], F32R)
        k_max = sb("k_max", [P, PAIRS])
        M_sb = sb("M_sb", [P, D])
        q_max = sb("q_max", [P, HA])
        q_sum, q_rcp = sb("q_sum", [P, HA]), sb("q_rcp", [P, HA])
        z_sum, z_rcp = sb("z_sum", [P, PAIRS]), sb("z_rcp", [P, PAIRS])
        stats = [(sb(f"st{n}", [P, NC, 6]), sb(f"mom{n}", [P, 6, NC]), sb(f"ve{n}", [P, NC]),
                  sb(f"rs{n}", [P, NC])) for n in range(4)]
        x1 = sb("x1", [P, NC, D])
        x2 = sb("x2", [P, NC, D])
        hn = sb("hn", [P, NC, D])
        mixed = [sb("mixed_r", [P, N]), sb("mixed_k", [P, N])]
        k_relu, k_act = sb("k_relu", [P, N]), sb("k_act", [P, N])
        gate = sb("gate", [P, NC, D])
        gated = sb("gated", [P, NC, D])
        qkv_sb = sb("qkv_sb", [P, NC, W3])

        qk_rot = sb("qk_rot", [P, NC, 2 * D])
        rot = sb("rot", [P, NC, 2 * D])
        v32 = [sb(f"v32_{p}", [P, NC, HB, 32]) for p in range(2)]
        halves_first = [sb(s, [P, N], F32R) for s in ("k_hi", "k_lo", "q_hi", "q_lo")]
        kq_halves = [halves_first, [h1h, h1l, h3h, h3l]]
        head_rows = sb("head_rows", [P, 4])
        q_st = [sb(f"q_st{g}", [P, N], F32R) for g in range(2)]
        k_st = [sb(f"k_st{g}", [P, N], F32R) for g in range(2)]
        row_max = sb("row_max", [P, NC, 4])
        neg_c = sb("neg_c", [4, N], F32R)
        sel4f = sb("sel4f", [4, 4, P])
        sel4 = sb("sel4", [4, 4, P], F32R)
        U = [sb(f"U{g}", [P, N]) for g in range(2)]
        den_rcp = sb("den_rcp", [P, NC, 4])
        c_tok = sb("c_tok", [P, NC, D])
        cT = sb("cT", [P, N])
        w_sq = [[h[:, :] for h in halves_first[2 * t:2 * t + 2]] for t in range(2)]
        ones_col = sb("ones_col", [P, 1], F32R)
        w_norm = sb("w_norm", [1, 1])
        qk_sq = sb("qk_sq", [P, NC, 2 * D])
        qk_norm = sb("qk_norm", [P, NC, 2 * HB])
        norm_max = sb("norm_max", [P, NC, 2 * HB])
        norm_col = sb("norm_col", [P, 2])
        norm_two = sb("norm_two", [1, 3])
        bounded_a, bounded_b = sb("bounded_a", [1, 1], I32), sb("bounded_b", [1, 1], I32)
        PS = ctx.enter_context(nc.psum_tensor("PS", [P, 8, 512], F32))

        def there(batch):
            return not isinstance(batch, int) or 0 <= batch < NB

        def after_last(batch):
            return isinstance(batch, int) and batch == NB

        def as_chunks(ap):
            return ap.rearrange("p (c d) -> p c d", c=NC)

        wq_in, wk_in, wout_in, w_in, c_in = (sig(s, n) for s, n in (
            ("wq_in", 16), ("wk_in", 16), ("wout_in", 16), ("w_in", 16 * 9), ("c_in", 16 * 4)))
        id0, id_ok, const_ok = sig("id0"), sig("id_ok"), sig("const_ok")
        w_sq_ok, w_norm_ps, a_known, b_known = sig("w_sq_ok"), sig("w_norm_ps"), sig("a_known", 2), sig("b_known", 4)
        n_sq, n_red, n_max, n_T = sig("n_sq", NC), sig("n_red"), sig("n_max"), sig("n_T")
        w_hi, w_lo, wT, wT_sb, w3s, b_ps, b_ok = (sig(s, n) for s, n in (
            ("w_hi", 2), ("w_lo", 2), ("wT", 5), ("wT_sb", 5), ("w3s", 2), ("b_ps", 1), ("b_ok", 6)))

        xa_in, xr_in, x2_st, qkv_st = (sig(s, 16) for s in ("xa_in", "xr_in", "x2_st", "qkv_st"))
        ln = [sig(f"ln{n}", 2 * NC + 7) for n in range(4)]
        rstd = [sig(f"rstd{n}") for n in range(4)]
        h1_T, h1_sb, h1_sp = sig("h1_T"), sig("h1_sb"), sig("h1_sp", 2)
        kx_mm, kx_max, kx_T, kx_ok = (sig("kx_mm", PAIRS), sig("kx_max", PAIRS), sig("kx_T"),
                                      sig("kx_ok"))
        q_mm, k_mm, q_mx, q_exp, k_exp = (sig("q_mm", NC), sig("k_mm", NC), sig("q_mx", 2 * NC),
                                          sig("q_exp", NC), sig("k_exp", NC))
        q_rc, q_hat, c_mm, c_ev = sig("q_rc", 2 * NC), sig("q_hat", NC), sig("c_mm", NC), sig("c_ev", 5)
        t_mm, t_ev, m_mm, m_ev, y_mm, xb_ok, x1_ok = (sig(s) for s in (
            "t_mm", "t_ev", "m_mm", "m_ev", "y_mm", "xb_ok", "x1_ok"))
        ffn = []
        for n in range(2):
            ffn.append({s: sig(f"f{n}_{s}", c) for s, c in (
                ("hT", 1), ("mu", 2), ("mix", 4), ("k", 1), ("r", 1), ("relu", 1), ("act", 1),
                ("gate", 1), ("v", 1), ("x", 2))})
        h3_T, h3_sp, p_mm, p_ev = sig("h3_T"), sig("h3_sp", 2), sig("p_mm", NC), sig("p_ev", NC)
        qkv_in, x2_in, out_st = sig("qkv_in", 16), sig("x2_in", 16), sig("out_st", 16)
        k_in, q_in = ([sig(f"{s}_in{g}", 16 * 4 * NG // 2) for g in range(2)] for s in "kq")
        roped, v_ok = sig("roped", 4), sig("v_ok")
        kT_ps, qT_ps, split, masked = sig("kT_ps"), sig("qT_ps"), sig("split", 4), sig("masked", 4 * NG)
        mx_mm, mx_ok, mx_T, mx_neg = (sig("mx_mm", 8 * NG), sig("mx_ok", 8 * NG), sig("mx_T", NG),
                                      sig("mx_neg", NG))
        s_mm, s_exp, pv, pv_sb = sig("s_mm", 32), sig("s_exp", 32), sig("pv", 16), sig("pv_sb", NG)
        u_T, u_norm = sig("u_T", NG), sig("u_norm", 2 * NG)
        ct_ps, ct_sb, o_mm, x3_ok = sig("ct_ps"), sig("ct_sb"), sig("o_mm"), sig("x3_ok")

        block = ctx.enter_context(nc.Block())

        @block.sync
        def _(sp):
            sp.dma_start(xa, x_view[0]).then_inc(xa_in.sem, 16)
            for n, arrived in enumerate((wq_in, wk_in, w_in)):
                cols = slice(n * INNER, (n + 1) * INNER)
                sp.dma_start(wqkv_raw[:, cols], w_qkv[:, cols]).then_inc(arrived.sem, 16)
            for n, w in enumerate((W_r, W_k, W_v, W_Q, W_K, W_V, W_O)):
                sp.dma_start(raw7[:, n, :], w).then_inc(w_in.sem, 16)
            sp.dma_start(b_row[:, :], b_out.rearrange("(a d) -> a d", a=1)).then_inc(w_in.sem, 16)
            sp.dma_start(wout_sb, w_out.rearrange("(a p) d -> p a d", p=P)).then_inc(wout_in.sem, 16)
            sp.dma_start(mu[:, 0:1], mu_r.rearrange("(d a) -> d a", a=1)).then_inc(c_in.sem, 16)
            sp.dma_start(mu[:, 1:2], mu_k.rearrange("(d a) -> d a", a=1)).then_inc(c_in.sem, 16)
            sp.dma_start(cos_t[:, :, :], rope_cos).then_inc(c_in.sem, 16)
            sp.dma_start(sin_t[:, :, :], rope_sin).then_inc(c_in.sem, 16)

            def side(j):
                if exists(x1_ok.at(j - 1)):
                    sp.wait_ge(x1_ok.sem, x1_ok.at(j - 1))
                sp.dma_start(xr, x_view[j]).then_inc(xr_in.sem, 16)

            def store_x2(j):
                sp.wait_ge(ffn[0]["x"].sem, ffn[0]["x"].at(j))
                sp.dma_start(x2_dram[j], x2[:, :, :].rearrange("p c d -> p (c d)")).then_inc(x2_st.sem, 16)

            def store_qkv(j):
                sp.wait_ge(p_ev.sem, p_ev.at(j))
                sp.dma_start(qkv_dram[j], qkv_sb[:, :, :].rearrange("p c d -> p (c d)")).then_inc(qkv_st.sem, 16)

            def load_back(b):
                sp.wait_ge(v_ok.sem, v_ok.at(b - 1))
                sp.dma_start(qkv_back[:, :], qkv_dram[b]).then_inc(qkv_in.sem, 16)

            def stack_k(i, p, g):
                k_hi, k_lo = kq_halves[p][0:2]
                if isinstance(i, int) and i == 0 and g == 0:
                    sp.wait_ge(split.sem, split.at(0, 2))
                else:
                    if exists(masked.at(i, 4 * (g - 1))):
                        sp.wait_ge(masked.sem, masked.at(i, 4 * (g - 1)))
                for r, src in enumerate((k_hi, k_lo, k_hi, k_lo)):
                    sp.dma_start(k_st[g % 2][32 * r:32 * r + 32, :].bitcast(F32),
                                 src[32 * g:32 * g + 32, :].bitcast(F32)).then_inc(k_in[g % 2].sem, 16)

            def stack_q(i, p, g):
                q_hi, q_lo = kq_halves[p][2:4]
                if isinstance(i, int) and i == 0 and g == 0:
                    sp.wait_ge(split.sem, split.at(0))
                if exists(s_mm.at(i, 8 * (g - 1))):
                    sp.wait_ge(s_mm.sem, s_mm.at(i, 8 * (g - 1)))
                for r, src in enumerate((q_hi, q_hi, q_lo, q_lo)):
                    sp.dma_start(q_st[g % 2][32 * r:32 * r + 32, :].bitcast(F32),
                                 src[32 * g:32 * g + 32, :].bitcast(F32)).then_inc(q_in[g % 2].sem, 16)

            def first_half(i, p):
                if there(i - 1):
                    side(i - 1)
                if after_last(i - 1):
                    load_back(1)
                    stack_k(0, 0, 0)
                    stack_q(0, 0, 0)
                    stack_k(0, 0, 1)
                if after_last(i):
                    sp.wait_ge(qkv_st.sem, qkv_st.at(0))
                    sp.dma_start(qkv_back[:, :], qkv_dram[0]).then_inc(qkv_in.sem, 16)
                if there(i + 1):
                    sp.wait_ge(ln[0].sem, ln[0].at(i))
                    sp.dma_start(xa, x_view[i + 1]).then_inc(xa_in.sem, 16)
                if there(i - 2):
                    store_qkv(i - 2)
                if there(i - 1):
                    store_x2(i - 1)

            over_batches(sp, first_half, NB, 2)


            sp.wait_ge(x2_st.sem, x2_st.at(NB - 1))
            sp.wait_ge(qkv_st.sem, qkv_st.at(NB - 1))

            def second_half(i, p):
                if there(i - 1):
                    if exists(x3_ok.at(i - 2)):
                        sp.wait_ge(x3_ok.sem, x3_ok.at(i - 2))
                    sp.dma_start(x2[:, :, :].rearrange("p c d -> p (c d)"), x2_dram[i - 1]).then_inc(x2_in.sem, 16)
                for g in range(1, NG):
                    if there(i):
                        if g > 1:
                            stack_k(i, p, g)
                        stack_q(i, p, g)
                    if g == 1 and there(i + 2):
                        load_back(i + 2)
                if there(i + 1):
                    stack_k(i + 1, 1 - p, 0)
                    stack_q(i + 1, 1 - p, 0)
                    stack_k(i + 1, 1 - p, 1)
                if there(i - 1):
                    sp.wait_ge(ffn[1]["x"].sem, ffn[1]["x"].at(i - 1))
                    sp.dma_start(out_view[i - 1], gated[:, :, :]).then_inc(out_st.sem, 16)

            over_batches(sp, second_half, NB, 1, last=3)
            sp.wait_ge(out_st.sem, out_st.at(NB - 1))

        @block.gpsimd
        def _(pool):
            def rsqrt_var(n, j):
                _, _, ve, rs = stats[n]
                pool.wait_ge(ln[n].sem, ln[n].at(j, NC + 7))
                pool.tensor_tensor(rs[:, :], ve[:, :], half_neg[:, :], ALU.pow).then_inc(rstd[n].sem, 1)

            def split_h1(j, p):
                pool.wait_ge(h1_sb.sem, h1_sb.at(j))
                pool.tensor_tensor(h1h[:, :], h1T[p], one[:, 0:1].to_broadcast([P, N]), ALU.mult).then_inc(h1_sp.sem, 1)
                pool.wait_ge(h1_sp.sem, h1_sp.at(j, 1))
                pool.tensor_tensor(h1l[:, :], h1T[p], h1h[:, :].bitcast(F32), ALU.subtract).then_inc(h1_sp.sem, 1)

            def q_hats(i, c):
                pool.wait_ge(q_rc.sem, q_rc.at(i, 2 * c + 2))
                q3 = EQ[c].rearrange("p (h d) -> p h d", h=HA)
                pool.tensor_tensor(q3, q3, q_rcp[:, :].unsqueeze(2).to_broadcast([P, HA, DA]), ALU.mult)\
                    .then_inc(q_hat.sem, 1)

            def add_bias(j):
                pool.wait_ge(xr_in.sem, xr_in.at(j))
                pool.tensor_tensor(xr, xr, b_all[:, :].unsqueeze(1).to_broadcast([P, NC, D]), ALU.add)\
                    .then_inc(xb_ok.sem, 1)

            pool.memset(ident[:, :], 0.0).then_inc(id0.sem, 1)
            pool.memset(half_neg[:, :], -0.5).then_inc(const_ok.sem, 1)
            pool.memset(one[:, :], 1.0).then_inc(const_ok.sem, 1)
            pool.memset(ones_row[:, :], 1.0).then_inc(const_ok.sem, 1)
            pool.memset(ones8f[:, :], 1.0).then_inc(const_ok.sem, 1)
            pool.wait_ge(id0.sem, 1)
            pool.affine_select(out=ident[:, :], in_=ident[:, :], compare_op=ALU.not_equal, fill=1.0, base=0,
                               pattern=[[-1, P]], channel_multiplier=1).then_inc(id_ok.sem, 1)
            pool.wait_ge(const_ok.sem, 4)
            rsqrt_var(0, 0)
            pool.memset(negmask, 0.0).then_inc(const_ok.sem, 1)
            pool.memset(sel4f[:, :, :], 0.0).then_inc(const_ok.sem, 1)
            pool.memset(ctx_bd, 0.0).then_inc(const_ok.sem, 1)
            pool.memset(norm_max[:, :, :], 0.0).then_inc(const_ok.sem, 1)
            pool.wait_ge(const_ok.sem, 8)
            pool.affine_select(out=negmask, in_=negmask, compare_op=ALU.not_equal, fill=-1.0,
                               base=0, pattern=[[-1, PAIRS], [0, P]], channel_multiplier=1).then_inc(const_ok.sem, 1)
            pool.affine_select(out=sel4f[:, :, :], in_=sel4f[:, :, :], compare_op=ALU.not_equal, fill=1.0,
                               base=0, pattern=[[-1, 4], [0, P]], channel_multiplier=1).then_inc(const_ok.sem, 1)
            split_h1(0, 0)
            for t in range(2):
                pool.memset(v32[t][:, :, :, :], 0.0).then_inc(const_ok.sem, 1)
            pool.wait_ge(const_ok.sem, 12)
            for t in range(2):
                pool.memset(v32[t][:, :, :, DB:DB + 1], 1.0).then_inc(const_ok.sem, 1)
            pool.wait_ge(b_ok.sem, 6)

            def norms(j):
                if exists(n_red.at(j - 1)):
                    pool.wait_ge(n_red.sem, n_red.at(j - 1))
                for c in range(NC):
                    pool.wait_ge(p_ev.sem, p_ev.at(j, c + 1))
                    qk = qkv_sb[:, c, 0:2 * D]
                    pool.tensor_tensor(qk_sq[:, c, :], qk, qk, ALU.mult).then_inc(n_sq.sem, 1)

            back = qkv_back[:, :].rearrange("p (c d) -> p c d", c=NC)

            def rope(i):
                qk = back[:, :, 0:2 * D]
                pool.wait_ge(qkv_in.sem, qkv_in.at(i))
                pool.tensor_tensor(qk_cos[:, :, :], qk, cos_t[:, :, :], ALU.mult).then_inc(roped.sem, 1)
                pool.tensor_tensor(rot[:, :, 0::2], qk[:, :, 1::2], sin_t[:, :, 0::2], ALU.mult).then_inc(roped.sem, 1)
                pool.tensor_tensor(rot[:, :, 1::2], qk[:, :, 0::2], sin_t[:, :, 1::2], ALU.mult).then_inc(roped.sem, 1)

            def rope_sum(i):
                if exists(kT_ps.at(i - 1)):
                    pool.wait_ge(kT_ps.sem, kT_ps.at(i - 1))
                if exists(qT_ps.at(i - 1)):
                    pool.wait_ge(qT_ps.sem, qT_ps.at(i - 1))
                pool.wait_ge(roped.sem, roped.at(i, 3))
                pool.tensor_tensor(qk_rot[:, :, :], qk_cos[:, :, :], rot[:, :, :], ALU.add).then_inc(roped.sem, 1)

            def v_copy(i, p):
                if exists(pv.at(i - 2)):
                    pool.wait_ge(pv.sem, pv.at(i - 2))
                pool.tensor_tensor(v32[p][:, :, :, 0:DB], back[:, :, 2 * D:W3].rearrange("p c (h d) -> p c h d", h=HB),
                                   one[:, 0:1].unsqueeze(2).unsqueeze(3).to_broadcast([P, NC, HB, DB]),
                                   ALU.mult).then_inc(v_ok.sem, 1)

            def first_half(i, p):
                j = i - 1
                if there(i - 2):
                    rsqrt_var(2, i - 2)
                if there(i):
                    q_hats(i, 0)
                if there(j):
                    add_bias(j)
                if there(i + 1):
                    rsqrt_var(0, i + 1)
                if there(i):
                    q_hats(i, 1)
                if there(j):
                    rsqrt_var(1, j)
                if there(i):
                    q_hats(i, 2)
                if there(i - 2):
                    norms(i - 2)
                if there(i):
                    q_hats(i, 3)
                if there(i + 1):
                    split_h1(i + 1, 1 - p)
                if after_last(i):
                    rope(0)
                    rope_sum(0)
                    v_copy(0, 0)

            over_batches(pool, first_half, NB, 2)
            rope(1)
            rope_sum(1)

            def second_half(i, p):
                if there(i + 1):
                    v_copy(i + 1, 1 - p)
                if there(i + 2):
                    rope(i + 2)
                if there(i - 1):
                    rsqrt_var(3, i - 1)
                if there(i + 2):
                    rope_sum(i + 2)

            over_batches(pool, second_half, NB, 1, last=3)

        @block.scalar
        def _(act):
            def h1_copy(j, p):
                act.wait_ge(h1_T.sem, h1_T.at(j))
                act.activation(h1T[p], PS[:, 4, :], ACT.Copy).then_inc(h1_sb.sem, 1)

            def exp_q(i, c, guarded):
                if exists(c_mm.at(i - 1, c + 1)):
                    act.wait_ge(c_mm.sem, c_mm.at(i - 1, c + 1))
                if guarded:
                    act.wait_ge(q_mx.sem, q_mx.at(i, 2 * c + 2))
                    act.activation(EQ[c], q_sh, ACT.Exp).then_inc(q_exp.sem, 1)
                else:
                    act.wait_ge(q_mm.sem, q_mm.at(i, c + 1))
                    act.activation(EQ[c], PS[:, 0:2, :].rearrange("p a n -> p (a n)"), ACT.Exp).then_inc(q_exp.sem, 1)

            def exp_k(i, c):
                act.wait_ge(k_mm.sem, k_mm.at(i, c + 1))
                act.activation(EK[c], PS[:, 2:4, :].rearrange("p a n -> p (a n)"), ACT.Exp).then_inc(k_exp.sem, 1)

            def relu(f, j, bank):
                act.wait_ge(f["k"].sem, f["k"].at(j))
                act.activation(k_relu[:, :], PS[:, bank, :], ACT.Relu).then_inc(f["relu"].sem, 1)

            def gates(f, j, bank):
                act.wait_ge(f["r"].sem, f["r"].at(j))
                act.activation(gate[:, :, :].rearrange("p c d -> p (c d)"), PS[:, bank, :], ACT.Tanh, scale=0.5)\
                   .then_inc(f["gate"].sem, 1)

            def scale_mu(f, j, bank):
                act.wait_ge(f["hT"].sem, f["hT"].at(j))
                if exists(f["r"].at(j - 1)):
                    act.wait_ge(f["r"].sem, f["r"].at(j - 1))
                for n in range(2):
                    act.activation(mixed[n][:, :], PS[:, bank, :], ACT.Copy, scale=mu[:, n:n + 1])\
                       .then_inc(f["mu"].sem, 1)

            def t_copy(j):
                act.wait_ge(t_mm.sem, t_mm.at(j))
                act.activation(T_sb.rearrange("p a n -> p (a n)"), PS[:, 5:7, :].rearrange("p a n -> p (a n)"),
                               ACT.Copy).then_inc(t_ev.sem, 1)

            def m_copy(j):
                act.wait_ge(m_mm.sem, m_mm.at(j))
                act.activation(M_sb[:, :], PS[:, 5, 0:D], ACT.Copy).then_inc(m_ev.sem, 1)

            def p_copy(j, chunks):
                for c in chunks:
                    if c == 0:
                        if exists(qkv_st.at(j - 1)):
                            act.wait_ge(qkv_st.sem, qkv_st.at(j - 1))
                        if exists(n_sq.at(j - 1)):
                            act.wait_ge(n_sq.sem, n_sq.at(j - 1))
                    act.wait_ge(p_mm.sem, p_mm.at(j, c + 1))
                    act.activation(qkv_sb[:, c, :], PS[:, (4, 7)[c % 2], 0:W3], ACT.Copy).then_inc(p_ev.sem, 1)

            halves_of = [slice(n * INNER, (n + 1) * INNER) for n in range(2)]
            for n, scale, arrived in ((0, SCALE_A, wq_in), (1, 1.0, wk_in)):
                act.wait_ge(arrived.sem, 16)
                act.activation(wqk_hi[:, halves_of[n]], wqkv_raw[:, halves_of[n]], ACT.Copy, scale=scale)\
                   .then_inc(w_hi.sem, 1)
            for n, scale in ((0, SCALE_A), (1, 1.0)):
                for b in range(2):
                    at = n * INNER + b * N
                    act.activation(w_sq[n][b], wqkv_raw[:, at:at + N], ACT.Square, scale=scale)\
                       .then_inc(w_sq_ok.sem, 1)
            h1_copy(0, 0)
            act.wait_ge(wT.sem, 2)
            for n in range(2):
                act.activation(WvT[:, 4 * n:4 * n + 4, :], PS[:, n, :].rearrange("p (a n) -> p a n", a=4), ACT.Copy)\
                   .then_inc(wT_sb.sem, 1)
            act.wait_ge(b_ok.sem, 6)

            def first_half(guarded):
                def step(i, p):
                    j = i - 1
                    main = there(i)
                    if main:
                        exp_q(i, 0, guarded)
                        exp_k(i, 0)
                    if there(j):
                        t_copy(j)
                    if main:
                        exp_q(i, 1, guarded)
                    if there(j):
                        m_copy(j)
                    if main:
                        exp_k(i, 1)
                        exp_q(i, 2, guarded)
                    if there(i - 2):
                        p_copy(i - 2, (0, 1))
                    if main:
                        exp_k(i, 2)
                        exp_q(i, 3, guarded)
                    if there(i - 2):
                        p_copy(i - 2, (2, 3))
                    if there(j):
                        scale_mu(ffn[0], j, 7)
                    if main:
                        exp_k(i, 3)
                    if there(i + 1):
                        h1_copy(i + 1, 1 - p)
                    if there(j):
                        relu(ffn[0], j, 4)
                        gates(ffn[0], j, 7)
                over_batches(act, step, NB, 2)

            act.wait_ge(a_known.sem, a_known.at(0))
            with act.If(act.value_load(bounded_a[0:1, 0:1], min_val=0, max_val=1) == 1):
                first_half(False)
            with act.Else():
                first_half(True)

            act.wait_ge(x1_ok.sem, x1_ok.at(NB - 1))

            def second_half(i, p):
                for s in range(HB):
                    if there(i):
                        g, h = s // 4, s % 4
                        for half in range(2):
                            if h == 0:
                                if exists(pv.at(i, 4 * (g - 2) + 2 * half + 2)):
                                    act.wait_ge(pv.sem, pv.at(i, 4 * (g - 2) + 2 * half + 2))
                            act.wait_ge(s_mm.sem, s_mm.at(i, 2 * s + half + 1))
                            act.activation(probs[g % 2][:, h, 2 * half:2 * half + 2, :],
                                           PS[:, 2 * half:2 * half + 2, :], ACT.Exp).then_inc(s_exp.sem, 1)
                    if s == 12 and there(i - 1):
                        relu(ffn[1], i - 1, 6)
                        gates(ffn[1], i - 1, 7)

            over_batches(act, second_half, NB, 1, last=3)

        @block.vector
        def _(dve):
            def ln_stats(n, j, src):
                st, mom, ve, _ = stats[n]
                mean, d, both, m2, d2, m2e = (mom[:, t, :] for t in range(6))
                for c in range(NC):
                    dve.bn_stats(st[:, c, :], src[:, c, :]).then_inc(ln[n].sem, 1)
                dve.wait_ge(ln[n].sem, ln[n].at(j, NC))
                dve.tensor_tensor(both, st[:, :, 1], st[:, :, 4], ALU.add).then_inc(ln[n].sem, 1)
                dve.tensor_tensor(d, st[:, :, 1], st[:, :, 4], ALU.subtract).then_inc(ln[n].sem, 1)
                dve.tensor_tensor(m2, st[:, :, 2], st[:, :, 5], ALU.add).then_inc(ln[n].sem, 1)
                dve.wait_ge(ln[n].sem, ln[n].at(j, NC + 3))
                dve.tensor_scalar(mean, both, 0.5, None, ALU.mult).then_inc(ln[n].sem, 1)
                dve.scalar_tensor_tensor(d2, d, 0.25, d, ALU.mult, ALU.mult).then_inc(ln[n].sem, 1)
                dve.tensor_scalar(m2e, m2, 1.0 / D, EPS, ALU.mult, ALU.add).then_inc(ln[n].sem, 1)
                dve.wait_ge(ln[n].sem, ln[n].at(j, NC + 6))
                dve.tensor_tensor(ve[:, :], d2, m2e, ALU.add).then_inc(ln[n].sem, 1)

            def ln_norm(n, j, src, dst):
                _, mom, _, rs = stats[n]
                dve.wait_ge(ln[n].sem, ln[n].at(j, NC + 4))
                dve.wait_ge(rstd[n].sem, rstd[n].at(j))
                for c in range(NC):
                    dve.tensor_scalar(dst[:, c, :], src[:, c, :], mom[:, 0, c:c + 1], rs[:, c:c + 1],
                                      ALU.subtract, ALU.mult).then_inc(ln[n].sem, 1)

            def ln1_stats(j):
                dve.wait_ge(xa_in.sem, xa_in.at(j))
                ln_stats(0, j, xa)

            def ln1_norm(j):
                if exists(h1_T.at(j - 1)):
                    dve.wait_ge(h1_T.sem, h1_T.at(j - 1))
                ln_norm(0, j, xa, h1)

            def k_maxima(j):
                for a in range(PAIRS):
                    dve.wait_ge(kx_mm.sem, kx_mm.at(j, a + 1))
                    dve.reduce_max(k_max[:, a:a + 1], PS[:, 5 + a % 2, :], AX_X).then_inc(kx_max.sem, 1)

            def k_shift(j):
                dve.wait_ge(kx_T.sem, kx_T.at(j))
                dve.tensor_tensor(k_neg[:, :, :], PS[0:8, 5, 0:P].unsqueeze(1).to_broadcast([8, PAIRS, P]),
                                  negmask, ALU.mult).then_inc(kx_ok.sem, 1)

            def q_shift(i, c):
                src = PS[:, 0:2, :].rearrange("p a (h d) -> p (a h) d", d=DA)
                dve.wait_ge(q_mm.sem, q_mm.at(i, c + 1))
                dve.reduce_max(q_max[:, :], src, AX_X).then_inc(q_mx.sem, 1)
                dve.wait_ge(q_mx.sem, q_mx.at(i, 2 * c + 1))
                if exists(q_exp.at(i, c)):
                    dve.wait_ge(q_exp.sem, q_exp.at(i, c))
                dve.tensor_tensor(q_sh.rearrange("p (h d) -> p h d", h=HA), src,
                                  q_max[:, :].unsqueeze(2).to_broadcast([P, HA, DA]), ALU.subtract)\
                   .then_inc(q_mx.sem, 1)

            def q_sums(i, c, guarded):
                if guarded:
                    q_shift(i, c)
                if exists(q_rc.at(i, 2 * c)):
                    dve.wait_ge(q_rc.sem, q_rc.at(i, 2 * c))
                dve.wait_ge(q_exp.sem, q_exp.at(i, c + 1))
                dve.reduce_sum(q_sum[:, :], EQ[c].rearrange("p (h d) -> p h d", h=HA), AX_X).then_inc(q_rc.sem, 1)
                dve.wait_ge(q_rc.sem, q_rc.at(i, 2 * c + 1))
                if exists(q_hat.at(i, c)):
                    dve.wait_ge(q_hat.sem, q_hat.at(i, c))
                dve.reciprocal(q_rcp[:, :], q_sum[:, :]).then_inc(q_rc.sem, 1)

            def c_norm(i):
                src = PS[:, 5:7, :].rearrange("p a (b n) -> p (a b) n", n=P)
                dve.wait_ge(c_mm.sem, c_mm.at(i))
                for s in range(2):
                    lo, hi = DA * s, DA * s + DA
                    dve.reduce_sum(z_sum[lo:hi, :], src[lo:hi, :, lo:hi], AX_X).then_inc(c_ev.sem, 1)
                dve.wait_ge(c_ev.sem, c_ev.at(i, 2))
                dve.reciprocal(z_rcp[:, :], z_sum[:, :]).then_inc(c_ev.sem, 1)
                dve.wait_ge(c_ev.sem, c_ev.at(i, 3))
                for s in range(2):
                    lo, hi = DA * s, DA * s + DA
                    dve.tensor_tensor(ctx_bd[lo:hi, :, lo:hi], src[lo:hi, :, lo:hi],
                                      z_rcp[lo:hi, :].unsqueeze(2).to_broadcast([DA, PAIRS, DA]), ALU.mult)\
                       .then_inc(c_ev.sem, 1)

            def add_x1(j):
                dve.wait_ge(xb_ok.sem, xb_ok.at(j))
                dve.wait_ge(y_mm.sem, y_mm.at(j))
                dve.tensor_tensor(x1[:, :, :], as_chunks(PS[:, 4, :]), xr, ALU.add).then_inc(x1_ok.sem, 1)
                dve.wait_ge(x1_ok.sem, x1_ok.at(j))
                ln_stats(1, j, x1)

            def mix(f, j, bank, scaled):
                if scaled:
                    dve.wait_ge(f["hT"].sem, f["hT"].at(j))
                    if exists(f["r"].at(j - 1)):
                        dve.wait_ge(f["r"].sem, f["r"].at(j - 1))
                    for n in range(2):
                        dve.tensor_scalar(mixed[n][:, :], PS[:, bank, :], mu[:, n:n + 1], None, ALU.mult)\
                           .then_inc(f["mix"].sem, 1)
                    dve.wait_ge(f["mix"].sem, f["mix"].at(j, 2))
                else:
                    dve.wait_ge(f["mu"].sem, f["mu"].at(j))
                for n in range(2):
                    dve.scalar_tensor_tensor(mixed[n][:, 1:N], PS[:, bank, 0:N - 1], mu[:, 2 + n:3 + n],
                                             mixed[n][:, 1:N], ALU.mult, ALU.add)\
                       .then_inc(f["mix"].sem, 1 if scaled else 2)

            def square(f, j, bank):
                dve.wait_ge(f["relu"].sem, f["relu"].at(j))
                if exists(f["v"].at(j - 1)):
                    dve.wait_ge(f["v"].sem, f["v"].at(j - 1))
                dve.tensor_tensor(k_act[:, :], PS[:, bank, :], k_relu[:, :], ALU.mult).then_inc(f["act"].sem, 1)

            def gate_v(f, j, bank, res, dst):
                dve.wait_ge(f["gate"].sem, f["gate"].at(j))
                dve.wait_ge(f["v"].sem, f["v"].at(j))
                dve.scalar_tensor_tensor(gated[:, :, :], gate[:, :, :], 1.0, as_chunks(PS[:, bank, :]),
                                         ALU.add, ALU.mult).then_inc(f["x"].sem, 1)
                dve.wait_ge(f["x"].sem, f["x"].at(j, 1))
                dve.scalar_tensor_tensor(dst[:, :, :], gated[:, :, :], 0.5, res[:, :, :], ALU.mult, ALU.add)\
                   .then_inc(f["x"].sem, 1)

            def split_h3(j):
                dve.wait_ge(h3_T.sem, h3_T.at(j))
                if exists(p_mm.at(j - 1)):
                    dve.wait_ge(p_mm.sem, p_mm.at(j - 1))
                dve.tensor_copy(h3h[:, :], PS[:, 7, :]).then_inc(h3_sp.sem, 1)
                dve.wait_ge(h3_sp.sem, h3_sp.at(j, 1))
                dve.tensor_tensor(h3l[:, :], PS[:, 7, :], h3h[:, :].bitcast(F32), ALU.subtract).then_inc(h3_sp.sem, 1)

            def end_ffn1(j):
                if exists(x2_st.at(j - 1)):
                    dve.wait_ge(x2_st.sem, x2_st.at(j - 1))
                gate_v(ffn[0], j, 4, x1, x2)
                dve.wait_ge(ffn[0]["x"].sem, ffn[0]["x"].at(j))
                ln_stats(2, j, x2)

            def norm_maxima(j):
                dve.wait_ge(n_sq.sem, n_sq.at(j))
                dve.reduce_sum(qk_norm[:, :, :], qk_sq[:, :, :].rearrange("p c (h d) -> p c h d", d=DB), AX_X)\
                   .then_inc(n_red.sem, 1)
                dve.wait_ge(n_red.sem, n_red.at(j))
                dve.tensor_tensor(norm_max[:, :, :], norm_max[:, :, :], qk_norm[:, :, :], ALU.max).then_inc(n_max.sem, 1)

            def split_kq(i, p, t, bank):
                hi, lo = kq_halves[p][2 * t:2 * t + 2]
                dve.wait_ge((kT_ps, qT_ps)[t].sem, (kT_ps, qT_ps)[t].at(i))
                if exists(q_in[1].at(i - 2)):
                    dve.wait_ge(q_in[1].sem, q_in[1].at(i - 2))
                dve.tensor_copy(hi[:, :], PS[:, bank, :]).then_inc(split.sem, 1)
                dve.wait_ge(split.sem, split.at(i, 2 * t + 1))
                dve.tensor_tensor(lo[:, :], PS[:, bank, :], hi[:, :].bitcast(F32), ALU.subtract).then_inc(split.sem, 1)

            def mask_k(i, g):
                dve.wait_ge(k_in[g % 2].sem, k_in[g % 2].at(i, 64 * (g // 2) + 64))
                if exists(s_mm.at(i, 8 * (g - 1))):
                    dve.wait_ge(s_mm.sem, s_mm.at(i, 8 * (g - 1)))
                for j in range(4):
                    dve.tensor_scalar(k_pad[g % 2][:, j, :], k_st[g % 2][:, :].bitcast(F32), head_rows[:, j:j + 1],
                                      None, ALU.mult).then_inc(masked.sem, 1)

            def first_half(guarded):
                def step(i, p):
                    j = i - 1
                    main = there(i)
                    if main:
                        q_sums(i, 0, guarded)
                    if there(i - 2):
                        ln_norm(2, i - 2, x2, h3)
                    if there(i + 1):
                        ln1_stats(i + 1)
                    if after_last(j):
                        split_kq(0, 0, 0, 2)
                    if there(i - 2):
                        split_h3(i - 2)
                    if main:
                        q_sums(i, 1, guarded)
                    if there(j):
                        add_x1(j)
                    if there(i + 1):
                        ln1_norm(i + 1)
                    if there(j):
                        ln_norm(1, j, x1, hn)
                    if main:
                        q_sums(i, 2, guarded)
                    if main:
                        q_sums(i, 3, guarded)
                    if there(j):
                        mix(ffn[0], j, 7, False)
                    if there(j):
                        square(ffn[0], j, 4)
                    if after_last(j):
                        split_kq(0, 0, 1, 3)
                        mask_k(0, 0)
                    if there(i - 2):
                        norm_maxima(i - 2)
                    if main:
                        c_norm(i)
                    if there(j):
                        end_ffn1(j)
                    if guarded and there(i + 1):
                        k_maxima(i + 1)
                        k_shift(i + 1)
                if guarded:
                    k_maxima(0)
                    k_shift(0)
                over_batches(dve, step, NB, 2)

            ln1_stats(0)
            dve.wait_ge(const_ok.sem, 4)
            dve.tensor_copy(ones_col[:, :], one[:, :]).then_inc(b_ok.sem, 1)
            dve.tensor_copy(ones8[:, :], ones8f[:, :]).then_inc(b_ok.sem, 1)
            ln1_norm(0)
            for n, scale in ((0, SCALE_A), (1, 1.0)):
                cols = slice(n * INNER, (n + 1) * INNER)
                dve.wait_ge(w_hi.sem, n + 1)
                dve.scalar_tensor_tensor(wqk_lo[:, cols], wqkv_raw[:, cols], scale, wqk_hi[:, cols].bitcast(F32),
                                         ALU.mult, ALU.subtract).then_inc(w_lo.sem, 1)
            dve.wait_ge(w_norm_ps.sem, 1)
            dve.reduce_max(w_norm[:, :], PS[0:1, 5:7, :].rearrange("p a n -> p (a n)"), AX_X).then_inc(a_known.sem, 1)
            dve.wait_ge(a_known.sem, 1)
            dve.tensor_scalar(bounded_a[:, :], w_norm[:, :], REACH ** 2 / D, None, ALU.is_lt).then_inc(a_known.sem, 1)
            dve.wait_ge(wT.sem, 5)
            dve.tensor_copy(W7T[:, 0:4, :], PS[:, 2, :].rearrange("p (a n) -> p a n", a=4)).then_inc(wT_sb.sem, 1)
            dve.tensor_copy(W7T[:, 4:7, :], PS[:, 3, 0:3 * D].rearrange("p (a n) -> p a n", a=3)).then_inc(wT_sb.sem, 1)
            dve.tensor_copy(b_all[:, :], PS[:, 3, 3 * D:4 * D]).then_inc(b_ok.sem, 1)
            dve.wait_ge(wT_sb.sem, 4)
            w3 = W7T[:, 3:6, :].rearrange("p a n -> p (a n)")
            dve.tensor_copy(w3h[:, :], w3).then_inc(w3s.sem, 1)
            dve.wait_ge(w3s.sem, 1)
            dve.tensor_tensor(w3l[:, :], w3, w3h[:, :].bitcast(F32), ALU.subtract).then_inc(w3s.sem, 1)
            dve.wait_ge(c_in.sem, 64)
            dve.tensor_scalar(mu[:, 2:4], mu[:, 0:2], -1.0, 1.0, ALU.mult, ALU.add).then_inc(b_ok.sem, 1)
            dve.wait_ge(const_ok.sem, 10)
            dve.tensor_copy(sel4[:, :, :], sel4f[:, :, :]).then_inc(b_ok.sem, 1)
            dve.wait_ge(id_ok.sem, 1)
            dve.reduce_sum(head_rows[:, :], ident[:, :].rearrange("p (r j d) -> p j r d", r=4, j=4), mybir.AxisListType.XY)\
               .then_inc(b_ok.sem, 1)
            dve.wait_ge(a_known.sem, a_known.at(0))
            with dve.If(dve.value_load(bounded_a[0:1, 0:1], min_val=0, max_val=1) == 1):
                first_half(False)
            with dve.Else():
                first_half(True)

            dve.wait_ge(n_max.sem, n_max.at(NB - 1))
            for t in range(2):
                dve.reduce_max(norm_col[:, t:t + 1], norm_max[:, :, HB * t:HB * t + HB], mybir.AxisListType.XY)\
                   .then_inc(b_known.sem, 1)
            dve.wait_ge(n_T.sem, n_T.at(0))
            dve.reduce_max(norm_two[:, 0:2], PS[0:1, 4, 0:2 * P].rearrange("p (t n) -> p t n", t=2), AX_X)\
               .then_inc(n_red.sem, 1)
            dve.wait_ge(n_red.sem, NB + 1)
            dve.tensor_tensor(norm_two[:, 2:3], norm_two[:, 0:1], norm_two[:, 1:2], ALU.mult).then_inc(b_known.sem, 1)
            dve.wait_ge(b_known.sem, b_known.at(0, 3))
            dve.tensor_scalar(bounded_b[:, :], norm_two[:, 2:3], REACH ** 2 * DB, None, ALU.is_lt).then_inc(b_known.sem, 1)

            def maxima(i, g):
                for m in range(8):
                    h, half = m // 2, m % 2
                    dve.wait_ge(mx_mm.sem, mx_mm.at(i, 8 * g + m + 1))
                    dve.reduce_max(row_max[:, 2 * half:2 * half + 2, h], PS[:, 2 * half:2 * half + 2, :], AX_X)\
                       .then_inc(mx_ok.sem, 1)
                dve.wait_ge(mx_T.sem, mx_T.at(i, g + 1))
                dve.tensor_scalar(neg_c[:, :], PS[0:4, 0, :], -1.0, None, ALU.mult).then_inc(mx_neg.sem, 1)

            def pv_copy(i, g):
                dve.wait_ge(pv.sem, pv.at(i, 4 * g + 4))
                if exists(u_T.at(i, g - 1)):
                    dve.wait_ge(u_T.sem, u_T.at(i, g - 1))
                dve.tensor_copy(U[g % 2][:, :], PS[:, 4 + g % 2, :]).then_inc(pv_sb.sem, 1)

            def normalise(i, g, bank):
                src = PS[:, bank, :].rearrange("p (c j r) -> p c j r", c=NC, j=4)
                dve.wait_ge(u_T.sem, u_T.at(i, g + 1))
                dve.reciprocal(den_rcp[:, :, :], src[:, :, :, DB]).then_inc(u_norm.sem, 1)
                dve.wait_ge(u_norm.sem, u_norm.at(i, 2 * g + 1))
                dve.tensor_tensor(c_tok[:, :, 32 * g:32 * g + 32].rearrange("p c (j d) -> p c j d", j=4),
                                  src[:, :, :, 0:DB], den_rcp[:, :, :].unsqueeze(3).to_broadcast([P, NC, 4, DB]),
                                  ALU.mult).then_inc(u_norm.sem, 1)

            def add_x3(j):
                dve.wait_ge(x2_in.sem, x2_in.at(j))
                dve.wait_ge(o_mm.sem, o_mm.at(j))
                dve.tensor_tensor(x1[:, :, :], as_chunks(PS[:, 6, :]), x2[:, :, :], ALU.add).then_inc(x3_ok.sem, 1)
                dve.wait_ge(x3_ok.sem, x3_ok.at(j))
                ln_stats(3, j, x1)

            def second_half(guarded):
                def step(i, p):
                    j = i - 1
                    main, side = there(i), there(j)
                    nxt = there(i + 1)
                    if main and guarded:
                        maxima(i, 0)
                    if main:
                        mask_k(i, 1)
                    if side:
                        normalise(j, 2, 6)
                    if nxt:
                        split_kq(i + 1, 1 - p, 0, 7)
                        split_kq(i + 1, 1 - p, 1, 7)
                    if side:
                        pv_copy(j, 3)
                    if main and guarded:
                        maxima(i, 1)
                    if side:
                        normalise(j, 3, 6)
                    if main:
                        mask_k(i, 2)
                    if side:
                        dve.wait_ge(ct_ps.sem, ct_ps.at(j))
                        dve.tensor_copy(cT[:, :], PS[:, 7, :]).then_inc(ct_sb.sem, 1)
                    if main:
                        pv_copy(i, 0)
                    if side:
                        add_x3(j)
                    if main and guarded:
                        maxima(i, 2)
                    if main:
                        normalise(i, 0, 6)
                    if main:
                        mask_k(i, 3)
                    if side:
                        ln_norm(3, j, x1, hn)
                    if side:
                        mix(ffn[1], j, 7, True)
                    if main:
                        pv_copy(i, 1)
                    if main and guarded:
                        maxima(i, 3)
                    if side:
                        square(ffn[1], j, 6)
                    if nxt:
                        mask_k(i + 1, 0)
                    if side:
                        if exists(out_st.at(j - 1)):
                            dve.wait_ge(out_st.sem, out_st.at(j - 1))
                        gate_v(ffn[1], j, 6, x1, gated)
                    if main:
                        normalise(i, 1, 6)
                        pv_copy(i, 2)
                over_batches(dve, step, NB, 1, last=3)

            dve.wait_ge(b_known.sem, b_known.at(0))
            with dve.If(dve.value_load(bounded_b[0:1, 0:1], min_val=0, max_val=1) == 1):
                second_half(False)
            with dve.Else():
                second_half(True)

        @block.tensor
        def _(pe):
            def weight_transposes():
                pe.wait_ge(w_in.sem, 16 * 9)
                for n in range(2):
                    for a in range(4):
                        mm = pe.transpose(PS[:, n, a * P:(a + 1) * P],
                                          wqkv_raw[:, 2 * INNER + (4 * n + a) * P:2 * INNER + (4 * n + a + 1) * P],
                                          ident[:, :])
                    mm.then_inc(wT.sem, 1)
                for n, some in ((2, range(0, 4)), (3, range(4, 7))):
                    for a, w in enumerate(some):
                        mm = pe.transpose(PS[:, n, a * P:(a + 1) * P], raw7[:, w, :], ident[:, :])
                    mm.then_inc(wT.sem, 1)
                pe.matmul(PS[:, 3, 3 * D:4 * D], ones_row[:, :], b_row[:, :], start=True, stop=True).then_inc(wT.sem, 1)

            def weight_norms():
                pe.wait_ge(w_sq_ok.sem, 4)
                for b in range(2):
                    for n in range(2):
                        mm = pe.matmul(PS[0:1, 5 + b, :], ones_col[:, :], w_sq[n][b],
                                       start=(n == 0), stop=(n == 1))
                mm.then_inc(w_norm_ps.sem, 1)

            def four_transposes(src, bank):
                for c in range(NC):
                    mm = pe.transpose(PS[:, bank, c * P:(c + 1) * P], src(c), ident[:, :])
                return mm

            def halves(dst, w, h, stop=True):
                pe.matmul(dst, w[0], h[0], start=True, stop=False)
                pe.matmul(dst, w[0], h[1], start=False, stop=False)
                return pe.matmul(dst, w[1], h[0], start=False, stop=stop)

            def head_T(n):
                if exists(p_ev.at(n - 3, 3)):
                    pe.wait_ge(p_ev.sem, p_ev.at(n - 3, 3))
                if exists(x1_ok.at(n - 2)):
                    pe.wait_ge(x1_ok.sem, x1_ok.at(n - 2))
                pe.wait_ge(ln[0].sem, ln[0].at(n))
                four_transposes(lambda c: h1[:, c, :], 4).then_inc(h1_T.sem, 1)

            def head_kmax(n):
                pe.wait_ge(h1_sp.sem, h1_sp.at(n))
                if exists(c_ev.at(n - 1)):
                    pe.wait_ge(c_ev.sem, c_ev.at(n - 1))
                for a in range(PAIRS):
                    if a >= 2:
                        pe.wait_ge(kx_max.sem, kx_max.at(n, a - 1))
                    pe.matmul(PS[:, 5 + a % 2, :], wqk_hi[:, INNER + a * P:INNER + (a + 1) * P], h1h[:, :],
                              start=True, stop=True).then_inc(kx_mm.sem, 1)
                pe.wait_ge(kx_max.sem, kx_max.at(n))
                pe.transpose(PS[0:8, 5, 0:P], k_max[:, :], ident[:, :]).then_inc(kx_T.sem, 1)

            def proj_q(i, c, guarded):
                if c == 0:
                    pe.wait_ge(h1_sp.sem, h1_sp.at(i))
                if guarded:
                    if exists(q_mx.at(i, 2 * c)):
                        pe.wait_ge(q_mx.sem, q_mx.at(i, 2 * c))
                else:
                    if exists(q_exp.at(i, c)):
                        pe.wait_ge(q_exp.sem, q_exp.at(i, c))
                for b in range(2):
                    cols = slice(b * 512, b * 512 + 512)
                    tok = slice(c * P, c * P + P)
                    mm = halves(PS[:, b, :], (h1h[:, tok], h1l[:, tok]), (wqk_hi[:, cols], wqk_lo[:, cols]))
                mm.then_inc(q_mm.sem, 1)

            def proj_k(i, c, guarded):
                if exists(k_exp.at(i, c)):
                    pe.wait_ge(k_exp.sem, k_exp.at(i, c))
                if guarded and c == 0:
                    pe.wait_ge(kx_ok.sem, kx_ok.at(i))
                for b in range(2):
                    cols = slice(INNER + b * 512, INNER + b * 512 + 512)
                    tok = slice(c * P, c * P + P)
                    mm = halves(PS[:, 2 + b, :], (h1h[:, tok], h1l[:, tok]), (wqk_hi[:, cols], wqk_lo[:, cols]),
                                stop=not guarded)
                    if guarded:
                        mm = pe.matmul(PS[:, 2 + b, :], ones8[:, :],
                                       k_neg[:, 4 * b:4 * b + 4, :].rearrange("p a n -> p (a n)"),
                                       start=False, stop=True)
                mm.then_inc(k_mm.sem, 1)

            def context(i, c):
                if c == 0:
                    if exists(t_ev.at(i - 1)):
                        pe.wait_ge(t_ev.sem, t_ev.at(i - 1))
                    if exists(m_ev.at(i - 1)):
                        pe.wait_ge(m_ev.sem, m_ev.at(i - 1))
                pe.wait_ge(q_hat.sem, q_hat.at(i, c + 1))
                pe.wait_ge(k_exp.sem, k_exp.at(i, c + 1))
                for a in range(PAIRS):
                    cols = slice(a * P, a * P + P)
                    mm = pe.matmul(PS[:, 5 + a // 4, (a % 4) * P:(a % 4) * P + P], EK[c][:, cols], EQ[c][:, cols],
                                   start=(c == 0 and a % 4 == 0), stop=(c == NC - 1), skip_group_check=True)
                mm.then_inc(c_mm.sem, 1)

            def ctx_wout(j):
                pe.wait_ge(wout_in.sem, 16)
                pe.wait_ge(c_ev.sem, c_ev.at(j))
                for a in range(PAIRS):
                    mm = pe.matmul(PS[:, 5 + a // 4, (a % 4) * P:(a % 4) * P + P], ctx_bd[:, a, :], wout_sb[:, a, :],
                                   start=True, stop=True)
                mm.then_inc(t_mm.sem, 1)

            def wv_ctx_wout(j):
                pe.wait_ge(t_ev.sem, t_ev.at(j))
                for a in range(PAIRS):
                    mm = pe.matmul(PS[:, 5, 0:D], WvT[:, a, :], T_sb[:, a, :], start=(a == 0), stop=(a == PAIRS - 1))
                mm.then_inc(m_mm.sem, 1)

            def attn_out(j, p):
                pe.wait_ge(m_ev.sem, m_ev.at(j))
                if exists(ffn[0]["x"].at(j - 1, 1)):
                    pe.wait_ge(ffn[0]["x"].sem, ffn[0]["x"].at(j - 1, 1))
                for c in range(NC):
                    mm = pe.matmul(PS[:, 4, c * D:(c + 1) * D], h1T[p][:, c * P:(c + 1) * P], M_sb[:, :],
                                   start=True, stop=True)
                mm.then_inc(y_mm.sem, 1)

            def ffn_T(f, n, j, bank):
                pe.wait_ge(ln[n].sem, ln[n].at(j))
                four_transposes(lambda c: hn[:, c, :], bank).then_inc(f["hT"].sem, 1)

            def ffn_kr(f, j, bank_k, bank_r):
                pe.wait_ge(f["mix"].sem, f["mix"].at(j))
                pe.matmul(PS[:, bank_k, :], WkT, mixed[1][:, :], start=True, stop=True).then_inc(f["k"].sem, 1)
                for c in range(NC):
                    mm = pe.matmul(PS[:, bank_r, c * D:(c + 1) * D], mixed[0][:, c * P:(c + 1) * P], WrT,
                                   start=True, stop=True)
                mm.then_inc(f["r"].sem, 1)

            def ffn_v(f, j, bank):
                pe.wait_ge(f["act"].sem, f["act"].at(j))
                for c in range(NC):
                    mm = pe.matmul(PS[:, bank, c * D:(c + 1) * D], k_act[:, c * P:(c + 1) * P], WvfT,
                                   start=True, stop=True)
                mm.then_inc(f["v"].sem, 1)

            def h3_transposes(j):
                pe.wait_ge(ln[2].sem, ln[2].at(j))
                pe.wait_ge(ffn[0]["gate"].sem, ffn[0]["gate"].at(j))
                four_transposes(lambda c: h3[:, c, :], 7).then_inc(h3_T.sem, 1)

            def proj_b(j, chunks):
                for c in chunks:
                    if c == 0:
                        pe.wait_ge(w3s.sem, 2)
                        pe.wait_ge(h3_sp.sem, h3_sp.at(j))
                        if there(j + 1):
                            pe.wait_ge(x1_ok.sem, x1_ok.at(j + 1))
                    if c >= 2:
                        pe.wait_ge(p_ev.sem, p_ev.at(j, c - 1))
                    tok = slice(c * P, c * P + P)
                    halves(PS[:, (4, 7)[c % 2], 0:W3], (h3h[:, tok], h3l[:, tok]), (w3h[:, :], w3l[:, :]))\
                        .then_inc(p_mm.sem, 1)

            def kq_T(i, t, bank):
                pe.wait_ge(roped.sem, roped.at(i))
                mm = four_transposes(lambda c: qk_rot[:, c, (1 - t) * D:(2 - t) * D], bank)
                mm.then_inc((kT_ps, qT_ps)[t].sem, 1)

            def first_half(guarded):
                def step(i, p):
                    j = i - 1
                    main, side, late = there(i), there(j), there(i - 2)
                    if main:
                        proj_q(i, 0, guarded)
                        proj_k(i, 0, guarded)
                    if side:
                        ctx_wout(j)
                    if main:
                        proj_q(i, 1, guarded)
                    if side:
                        wv_ctx_wout(j)
                    if main:
                        proj_k(i, 1, guarded)
                    if after_last(j):
                        kq_T(0, 0, 2)
                        kq_T(0, 1, 3)
                    if late:
                        h3_transposes(i - 2)
                    if side:
                        attn_out(j, 1 - p)
                    if main:
                        context(i, 0)
                        proj_q(i, 2, guarded)
                    if late:
                        proj_b(i - 2, (0, 1))
                    if main:
                        proj_k(i, 2, guarded)
                        proj_q(i, 3, guarded)
                    if late:
                        proj_b(i - 2, (2, 3))
                    if main:
                        context(i, 1)
                    if side:
                        if exists(p_ev.at(j - 1)):
                            pe.wait_ge(p_ev.sem, p_ev.at(j - 1))
                        ffn_T(ffn[0], 1, j, 7)
                    if main:
                        proj_k(i, 3, guarded)
                    if there(i + 1):
                        head_T(i + 1)
                    if main:
                        context(i, 2)
                    if side:
                        if there(i + 1):
                            pe.wait_ge(h1_sb.sem, h1_sb.at(i + 1))
                        pe.wait_ge(x1_ok.sem, x1_ok.at(j))
                        ffn_kr(ffn[0], j, 4, 7)
                    if main:
                        context(i, 3)
                    if side:
                        ffn_v(ffn[0], j, 4)
                    if guarded and there(i + 1):
                        head_kmax(i + 1)
                if guarded:
                    head_kmax(0)
                over_batches(pe, step, NB, 2)

            pe.wait_ge(id_ok.sem, 1)
            pe.wait_ge(const_ok.sem, 4)
            head_T(0)
            pe.wait_ge(b_ok.sem, 2)
            weight_norms()
            weight_transposes()
            pe.wait_ge(a_known.sem, a_known.at(0))
            fast = pe.value_load(bounded_a[0:1, 0:1], min_val=0, max_val=1)
            pe.wait_ge(w_hi.sem, 2)
            pe.wait_ge(w_lo.sem, 2)
            pe.wait_ge(wT_sb.sem, 4)
            pe.wait_ge(b_ok.sem, 3)
            with pe.If(fast == 1):
                first_half(False)
            with pe.Else():
                first_half(True)

            pe.wait_ge(b_known.sem, b_known.at(0, 2))
            for t in range(2):
                mm = pe.transpose(PS[0:1, 4, t * P:t * P + P], norm_col[:, t:t + 1], ident[:, :])
            mm.then_inc(n_T.sem, 1)

            def maxima(i, g):
                if exists(s_exp.at(i, 8 * g)):
                    pe.wait_ge(s_exp.sem, s_exp.at(i, 8 * g))
                pe.wait_ge(masked.sem, masked.at(i, 4 * g + 4))
                pe.wait_ge(q_in[g % 2].sem, q_in[g % 2].at(i, 64 * (g // 2) + 64))
                for m in range(8):
                    h, half = m // 2, m % 2
                    if m >= 2:
                        pe.wait_ge(mx_ok.sem, mx_ok.at(i, 8 * g + m - 1))
                    for t in range(2):
                        c = 2 * half + t
                        mm = pe.matmul(PS[:, c, :], q_st[g % 2][:, c * P:(c + 1) * P], k_pad[g % 2][:, h, :],
                                       start=True, stop=True)
                    mm.then_inc(mx_mm.sem, 1)
                pe.wait_ge(mx_ok.sem, mx_ok.at(i, 8 * g + 8))
                for c in range(NC):
                    mm = pe.transpose(PS[0:4, 0, c * P:(c + 1) * P], row_max[:, c, :], ident[:, :])
                mm.then_inc(mx_T.sem, 1)

            def scores(i, s, half, guarded):
                g, h = s // 4, s % 4
                if h == 0 and half == 0:
                    pe.wait_ge(masked.sem, masked.at(i, 4 * g + 4))
                    pe.wait_ge(q_in[g % 2].sem, q_in[g % 2].at(i, 64 * (g // 2) + 64))
                    if guarded:
                        pe.wait_ge(mx_neg.sem, mx_neg.at(i, g + 1))
                if exists(s_exp.at(i, 2 * s + half - 1)):
                    pe.wait_ge(s_exp.sem, s_exp.at(i, 2 * s + half - 1))
                for kc in (2 * half, 2 * half + 1):
                    mm = pe.matmul(PS[:, kc, :], k_pad[g % 2][:, h, kc * P:(kc + 1) * P], q_st[g % 2][:, :],
                                   start=True, stop=not guarded)
                    if guarded:
                        mm = pe.matmul(PS[:, kc, :], sel4[:, h, :], neg_c[:, :], start=False, stop=True)
                mm.then_inc(s_mm.sem, 1)

            def weigh_values(i, g, kc, p):
                if kc == 0:
                    if exists(pv_sb.at(i, g - 1)):
                        pe.wait_ge(pv_sb.sem, pv_sb.at(i, g - 1))
                    pe.wait_ge(v_ok.sem, v_ok.at(i))
                pe.wait_ge(s_exp.sem, s_exp.at(i, 8 * g + 7 + kc // 2))
                for h in range(4):
                    mm = pe.matmul(PS[32 * h:32 * h + 32, 4 + g % 2, :], v32[p][:, kc, 4 * g + h, :],
                                   probs[g % 2][:, h, kc, :], start=(kc == 0), stop=(kc == NC - 1),
                                   tile_position=(0, 32 * h), skip_group_check=True)
                mm.then_inc(pv.sem, 1)

            def u_transposes(i, g, bank):
                pe.wait_ge(pv_sb.sem, pv_sb.at(i, g + 1))
                four_transposes(lambda c: U[g % 2][:, c * P:(c + 1) * P], bank).then_inc(u_T.sem, 1)

            def second_step(i, p, guarded):
                j = i - 1
                f = ffn[1]
                main, side = there(i), there(j)
                for s in range(HB):
                    g = s // 4
                    if main:
                        if guarded and s % 4 == 0:
                            maxima(i, g)
                        scores(i, s, 0, guarded)
                    if main and g >= 1:
                        weigh_values(i, g - 1, s % 4, p)
                    if side and g == 0:
                        weigh_values(j, NG - 1, s % 4, 1 - p)
                    if main:
                        scores(i, s, 1, guarded)
                    if s == 0 and side:
                        pe.wait_ge(u_norm.sem, u_norm.at(j, 4))
                        u_transposes(j, 2, 6)
                    if s == 1 and there(i + 1):
                        if exists(f["gate"].at(j - 1)):
                            pe.wait_ge(f["gate"].sem, f["gate"].at(j - 1))
                        kq_T(i + 1, 0, 7)
                    if s == 2 and there(i + 1):
                        pe.wait_ge(split.sem, split.at(i + 1, 2))
                        kq_T(i + 1, 1, 7)
                    if s == 4 and side:
                        pe.wait_ge(u_norm.sem, u_norm.at(j, 6))
                        u_transposes(j, 3, 6)
                    if s == 6 and side:
                        if exists(f["gate"].at(j - 1)):
                            pe.wait_ge(f["gate"].sem, f["gate"].at(j - 1))
                        if there(i + 1):
                            pe.wait_ge(split.sem, split.at(i + 1))
                        pe.wait_ge(u_norm.sem, u_norm.at(j))
                        four_transposes(lambda c: c_tok[:, c, :], 7).then_inc(ct_ps.sem, 1)
                    if s == 7 and side:
                        pe.wait_ge(ct_sb.sem, ct_sb.at(j))
                        for c in range(NC):
                            mm = pe.matmul(PS[:, 6, c * D:(c + 1) * D], cT[:, c * P:(c + 1) * P], WOT,
                                           start=True, stop=True)
                        mm.then_inc(o_mm.sem, 1)
                    if s == 8 and main:
                        if exists(x3_ok.at(j)):
                            pe.wait_ge(x3_ok.sem, x3_ok.at(j))
                        u_transposes(i, 0, 6)
                    if s == 10 and side:
                        ffn_T(f, 3, j, 7)
                    if s == 12 and side:
                        if main:
                            pe.wait_ge(u_norm.sem, u_norm.at(i, 2))
                        ffn_kr(f, j, 6, 7)
                    if s == 14 and side:
                        ffn_v(f, j, 6)
                    if s == 15 and main:
                        if exists(f["x"].at(j, 1)):
                            pe.wait_ge(f["x"].sem, f["x"].at(j, 1))
                        u_transposes(i, 1, 6)

            pe.wait_ge(b_known.sem, b_known.at(0))
            with pe.If(pe.value_load(bounded_b[0:1, 0:1], min_val=0, max_val=1) == 1):
                over_batches(pe, lambda i, p: second_step(i, p, False), NB, 1, last=3)
            with pe.Else():
                over_batches(pe, lambda i, p: second_step(i, p, True), NB, 1, last=3)


_PRE = "L0_"
_INS = ["attn_a_x", "attn_a_w_qkv", "attn_a_w_out", "attn_a_b_out", "attn_b_W_Q", "attn_b_W_K", "attn_b_W_V",
        "attn_b_W_O", "ffn_W_r", "ffn_W_k", "ffn_W_v", "ffn_mu_r", "ffn_mu_k"]


def rope_tables(n, d, heads, theta=10000.0):
    inv = 1.0 / theta ** (np.arange(0, d, 2, dtype=np.float32) / np.float32(d))
    angle = np.outer(np.arange(n, dtype=np.float32), inv.astype(np.float32)).astype(np.float32)
    cos, sin = np.repeat(np.cos(angle), 2, axis=-1), np.repeat(np.sin(angle), 2, axis=-1)
    sin[:, 0::2] *= -1.0

    def lay(t):
        both = np.concatenate([np.tile(t / np.sqrt(d), (1, heads)), np.tile(t, (1, heads))], axis=1)
        return np.ascontiguousarray(both.reshape(n // P, P, -1).transpose(1, 0, 2)).astype(np.float32)

    return lay(cos), lay(sin)


def kernel(**inputs):
    import numpy as _np
    import concourse.bacc as _bacc
    from concourse.bass_utils import run_bass_kernel_spmd as _run

    nc = _bacc.Bacc("TRN2", target_bir_lowering=False, num_devices=1)
    arrays, args = {}, []
    for name in _INS:
        a = _np.ascontiguousarray(inputs[_PRE + name])
        arrays[f"in_{name}"] = a
        args.append(nc.dram_tensor(f"in_{name}", a.shape, mybir.dt.from_np(a.dtype), kind="ExternalInput").ap())
    shape = tuple(inputs["L0_attn_a_x"].shape)
    for name, a in zip(("cos", "sin"), rope_tables(shape[1], 8, 16)):
        arrays[f"rope_{name}"] = a
        args.append(nc.dram_tensor(f"rope_{name}", a.shape, F32, kind="ExternalInput").ap())
    out = nc.dram_tensor("out_0", shape, F32, kind="ExternalOutput").ap()
    hybrid_block(nc, *args, out)
    r = _run(nc, [arrays], core_ids=[0])
    return r.results[0]["out_0"]
```
